# Optimizing a Trainium2 kernel written in Bass

```python
import numpy as np
import jax
import jax.numpy as jnp

def _softmax(x, axis=-1):
    return jax.nn.softmax(x, axis=axis)

def _gelu(x):
    return jax.nn.gelu(x, approximate=True)

def _silu(x):
    return jax.nn.silu(x)

def _sigmoid(x):
    return jax.nn.sigmoid(x)

def _layernorm(x, axis=-1, eps=1e-05):
    m = jnp.mean(x, axis=axis, keepdims=True)
    v = jnp.var(x, axis=axis, keepdims=True)
    return (x - m) / jnp.sqrt(v + eps)

def _scatter_add(tgt, idx, src, axis=0):
    return tgt.at[idx].add(src)

def _segment_sum(src, seg, n):
    return jax.ops.segment_sum(src, seg, n)
kernel_name = 'mk_gnn_preln_d2_gnn_r64_fff323'

def setup_inputs(seed: int=0):
    np.random.seed(seed)
    _w = jnp.asarray

    def _rec_inputs():
        import jax
        import jax.numpy as jnp
        _gk = jax.random.key(seed)
        x = -0.000202 + 1 * jax.random.normal(jax.random.fold_in(_gk, 1), (100000, 64), jnp.float32)
        src = jax.random.randint(jax.random.fold_in(_gk, 2), (25000,), 0, 100000, jnp.int32)
        dst = jnp.minimum((100000 * jax.random.uniform(jax.random.fold_in(_gk, 3), (25000,)) ** 2.0).astype(jnp.int32), 99999)
        _o = jnp.argsort(dst, stable=True)
        src = src[_o]
        dst = dst[_o]
        edge_type_8 = jax.random.randint(jax.random.fold_in(_gk, 12), (25000,), 0, 8, jnp.int32)
        edge_weight = jax.random.uniform(jax.random.fold_in(_gk, 13), (25000,), jnp.float32, 0.0, 0.999999)
        return (x, src, dst, edge_type_8, edge_weight)
    x, src, dst, edge_type_8, edge_weight = _rec_inputs()

    def _L0_gnn_setup():
        import jax, jax.numpy as jnp
        import numpy as np
        N = 100000
        E = 25000
        F_IN = 64
        F_OUT = 64
        K = 2
        T = 2
        BN_EPS = 1e-05
        key = jax.random.key(seed)
        ks = jax.random.split(key, 9)
        x = jax.random.normal(ks[0], (N, F_IN), jnp.float32)
        edge_index = jax.random.randint(ks[1], (2, E), 0, N)
        edge_weight = jax.random.uniform(ks[2], (E,), jnp.float32)
        s = 1.0 / np.sqrt(F_IN)
        init_weight = jax.random.uniform(ks[3], (K, F_IN, F_OUT), jnp.float32, -s, s)
        weight = jax.random.uniform(ks[4], (T - 1, K, F_OUT, F_OUT), jnp.float32, -s, s)
        root_weight = jax.random.uniform(ks[5], (T, K, F_IN, F_OUT), jnp.float32, -s, s)
        bias = jax.random.uniform(ks[6], (T, K, 1, F_OUT), jnp.float32, -s, s)
        bn_gamma = jnp.ones((F_OUT,), jnp.float32)
        bn_beta = jnp.zeros((F_OUT,), jnp.float32)
        bn_mean = jax.random.normal(ks[7], (F_OUT,), jnp.float32) * 0.1
        bn_var = jax.random.uniform(ks[8], (F_OUT,), jnp.float32, 0.5, 1.5)
        return {'x': x, 'edge_weight': edge_weight, 'init_weight': init_weight, 'weight': weight, 'root_weight': root_weight, 'bias': bias, 'bn_gamma': bn_gamma, 'bn_beta': bn_beta, 'bn_mean': bn_mean, 'bn_var': bn_var, 'edge_index': edge_index}
    _L0_gnn_all = _L0_gnn_setup()
    _L0_gnn_in = {k: v for k, v in _L0_gnn_all.items() if k in ('init_weight', 'weight', 'root_weight', 'bias', 'bn_gamma', 'bn_beta', 'bn_mean', 'bn_var')}
    del _L0_gnn_all

    def _L1_gnn_setup():
        import jax, jax.numpy as jnp
        import numpy as np
        N_NODES = 100000
        N_EDGES = 18750
        D_IN = 64
        D_OUT = 64
        N_REL = 8
        key = jax.random.key(seed)
        k1, k2, k3, k4, k5 = jax.random.split(key, 5)
        x = jax.random.normal(k1, (N_NODES, D_IN), dtype=jnp.float32)
        edge_index = jax.random.randint(k2, (2, N_EDGES), 0, N_NODES, dtype=jnp.int32)
        edge_type = jax.random.randint(k3, (N_EDGES,), 0, N_REL, dtype=jnp.int32)
        wb = float(np.sqrt(6.0 / (D_IN + D_OUT)))
        weight = jax.random.uniform(k4, (N_REL, D_IN, D_OUT), dtype=jnp.float32, minval=-wb, maxval=wb)
        self_loop_w = jax.random.uniform(k5, (D_OUT, D_IN), dtype=jnp.float32, minval=-wb, maxval=wb)
        return {'x': x, 'edge_index': edge_index, 'edge_type': edge_type, 'weight': weight, 'self_loop_w': self_loop_w}
    _L1_gnn_all = _L1_gnn_setup()
    _L1_gnn_in = {k: v for k, v in _L1_gnn_all.items() if k in ('weight', 'self_loop_w')}
    del _L1_gnn_all
    return {'x': x, 'src': src, 'dst': dst, 'edge_type_8': edge_type_8, 'edge_weight': edge_weight, 'L0_gnn_init_weight': _L0_gnn_in['init_weight'], 'L0_gnn_weight': _L0_gnn_in['weight'], 'L0_gnn_root_weight': _L0_gnn_in['root_weight'], 'L0_gnn_bias': _L0_gnn_in['bias'], 'L0_gnn_bn_gamma': _L0_gnn_in['bn_gamma'], 'L0_gnn_bn_beta': _L0_gnn_in['bn_beta'], 'L0_gnn_bn_mean': _L0_gnn_in['bn_mean'], 'L0_gnn_bn_var': _L0_gnn_in['bn_var'], 'L1_gnn_weight': _L1_gnn_in['weight'], 'L1_gnn_self_loop_w': _L1_gnn_in['self_loop_w']}

def reference(x, src, dst, edge_type_8, edge_weight, L0_gnn_init_weight, L0_gnn_weight, L0_gnn_root_weight, L0_gnn_bias, L0_gnn_bn_gamma, L0_gnn_bn_beta, L0_gnn_bn_mean, L0_gnn_bn_var, L1_gnn_weight, L1_gnn_self_loop_w):
    import jax
    import jax.numpy as jnp

    def _L0_gnn_ref(x, edge_weight, init_weight, weight, root_weight, bias, bn_gamma, bn_beta, bn_mean, bn_var, edge_index):
        import jax, jax.numpy as jnp
        import numpy as np
        N = 100000
        E = 25000
        F_IN = 64
        F_OUT = 64
        K = 2
        T = 2
        BN_EPS = 1e-05
        row, col = (edge_index[0], edge_index[1])
        deg = jax.ops.segment_sum(edge_weight, col, num_segments=N)
        dinv = jnp.where(deg > 0, jax.lax.rsqrt(jnp.maximum(deg, 1e-12)), 0.0)
        norm = dinv[row] * edge_weight * dinv[col]

        def propagate(h):
            msg = jnp.moveaxis(jnp.take(h, row, axis=1), 0, 1)
            msg = msg * norm[:, None, None]
            agg = jax.ops.segment_sum(msg, col, num_segments=N)
            return jnp.moveaxis(agg, 0, 1)
        x0 = jnp.broadcast_to(x[None], (K, N, F_IN))
        out = jnp.einsum('knf,kfo->kno', x0, init_weight)
        out = propagate(out)
        out = out + jnp.einsum('knf,kfo->kno', x0, root_weight[0]) + bias[0]
        for t in range(1, T):
            out = jax.nn.relu(out)
            out = jnp.einsum('knf,kfo->kno', out, weight[t - 1])
            out = propagate(out)
            out = out + jnp.einsum('knf,kfo->kno', x0, root_weight[t]) + bias[t]
        out = out.mean(axis=0)
        out = (out - bn_mean) * jax.lax.rsqrt(bn_var + BN_EPS) * bn_gamma + bn_beta
        return jax.nn.relu(out)

    def _L1_gnn_ref(x, edge_index, edge_type, weight, self_loop_w):
        import jax, jax.numpy as jnp
        import numpy as np
        N_NODES = 100000
        N_EDGES = 18750
        D_IN = 64
        D_OUT = 64
        N_REL = 8
        num_nodes = x.shape[0]
        num_relations = weight.shape[0]
        src, dst = (edge_index[0], edge_index[1])
        x_src = x[src]
        out = jnp.zeros((num_nodes, weight.shape[2]), dtype=x.dtype)
        for r in range(num_relations):
            mask = (edge_type == r)[:, None]
            msg = jnp.where(mask, x_src @ weight[r], 0.0)
            out = out + jax.ops.segment_sum(msg, dst, num_segments=num_nodes)
        out = out + x @ self_loop_w.T
        return jax.nn.relu(out)
    edge_index = jnp.stack([src, dst])
    h = jnp.maximum(_layernorm(x, axis=-1), 0.0)
    x = x + _L0_gnn_ref(h, edge_weight, L0_gnn_init_weight, L0_gnn_weight, L0_gnn_root_weight, L0_gnn_bias, L0_gnn_bn_gamma, L0_gnn_bn_beta, L0_gnn_bn_mean, L0_gnn_bn_var, edge_index)
    h = jnp.maximum(_layernorm(x, axis=-1), 0.0)
    x = x + _L1_gnn_ref(h, edge_index, edge_type_8, L1_gnn_weight, L1_gnn_self_loop_w)
    return x

_drawn_inputs = setup_inputs


def setup_inputs(seed=0):
    import zlib

    import numpy as np

    out = dict(_drawn_inputs(seed))
    spreads = {'L0_gnn_bn_gamma': (1.0, 0.2), 'L0_gnn_bn_beta': (0.0, 0.1)}
    factors = {'L0_gnn_init_weight': 5.671}
    for name, (base, spread) in spreads.items():
        noise = np.random.default_rng([zlib.crc32(name.encode()), seed]).standard_normal(out[name].shape)
        drawn = base * np.exp(spread * noise) if base else spread * noise
        out[name] = jnp.asarray(drawn.astype(out[name].dtype))
    for name, factor in factors.items():
        out[name] = (out[name] * factor).astype(out[name].dtype)
    return out
```

```python
import concourse.bass as bass
from concourse import mybir
from contextlib import ExitStack


class Stats:

    def __init__(self, sem, name):
        self.total = sem(name + "_total")
        self.centred = sem(name + "_centred")
        self.squared = sem(name + "_squared")
        self.spread = sem(name + "_spread")
        self.root = sem(name + "_root")
        self.scale = sem(name + "_scale")
        self.hidden = sem(name + "_hidden")


class Lane:

    def __init__(self, sb, sem, name, fp32, rows, tiles, banks):
        self.rows, self.tiles = rows, tiles
        self.xc = sb(name + "_xc", [128, 2, tiles, 64], fp32)
        self.sq = sb(name + "_sq", [128, 2, tiles, 64], fp32)
        self.sum = sb(name + "_sum", [128, 2, tiles], fp32)
        self.var = sb(name + "_var", [128, 2, tiles], fp32)
        self.std = sb(name + "_std", [128, 2, tiles], fp32)
        self.inv = sb(name + "_inv", [128, 2, tiles], fp32)
        self.h = sb(name + "_h", [128, 2, tiles, 64], fp32)
        self.hT = sb(name + "_hT", [128, 2, tiles // 2, 128], fp32)
        self.x1 = sb(name + "_x1", [128, 2, tiles, 64], fp32)
        self.transposed_bank, self.product_bank = banks
        self.norm1 = Stats(sem, name + "_n1")
        self.norm2 = Stats(sem, name + "_n2")
        self.turned1 = sem(name + "_turned1")
        self.turned2 = sem(name + "_turned2")
        self.taken1 = sem(name + "_taken1")
        self.taken2 = sem(name + "_taken2")
        self.product1 = sem(name + "_product1")
        self.product2 = sem(name + "_product2")
        self.added1 = sem(name + "_added1")
        self.added2 = sem(name + "_added2")
        self.mid = sem(name + "_mid")
        self.out = sem(name + "_out")


def gnn_kernel(nc, x, src, dst, edge_type, edge_weight, init_weight, weight, root_weight, bias,
               bn_gamma, bn_beta, bn_mean, bn_var, rel_weight, self_loop, out):
    fp32, i32 = mybir.dt.float32, mybir.dt.int32
    ALU = mybir.AluOpType
    ACT = mybir.ActivationFunctionType
    AX = mybir.AxisListType

    N, F = x.shape
    E = src.shape[0]
    R = rel_weight.shape[0]
    EPS = 1e-5
    COLS = 200
    EP = E // COLS
    GROUP = 4
    GROUPS = COLS // GROUP
    ITERS = GROUPS // 2
    PAIRS = ITERS // 2
    ROWS = 128 * COLS
    DT = 8
    DP = N // (DT * 2 * GROUPS)
    CHUNK = DT * DP
    NOWHERE = 131071
    assert EP * COLS == E and DP * DT * 2 * GROUPS == N and F == 64 and ITERS % 2 == 1

    ctx = ExitStack()
    with ctx:
        def sb(name, shape, dt):
            return ctx.enter_context(nc.sbuf_tensor(name, shape, dt))

        def sem(name):
            return ctx.enter_context(nc.semaphore(name))

        def dram(name, shape, dt=fp32):
            return nc.dram_tensor(name, shape, dt).ap()

        table = [dram(f"sum_table{k}", [ROWS + 1, F]) for k in range(3)]
        xs_dram = dram("x_of_src", [ROWS, F])
        xd_dram = dram("x_of_dst", [ROWS, F])
        hs_dram = dram("h_of_src", [ROWS, F])
        us_dram = dram("root_term_of_src", [ROWS, F])
        src_by_column = dram("src_by_column", [COLS, 128])

        def by_col(t):
            return t[0:ROWS, :].rearrange("(p j) f -> p j f", j=COLS)

        src_i = sb("src_i", [128, COLS], i32)
        dst_i = sb("dst_i", [128, COLS], i32)
        typ_i = sb("typ_i", [128, COLS], i32)
        ew = sb("ew", [128, COLS], fp32)
        next_i = sb("next_i", [128, 1], i32)
        src1 = sb("src1", [128, COLS], fp32)
        srcf = sb("srcf", [128, COLS], fp32)
        dstf = sb("dstf", [128, COLS], fp32)
        typf = sb("typf", [128, COLS], fp32)
        nextf = sb("nextf", [128, 1], fp32)
        same = sb("same", [128, COLS], fp32)
        final = sb("final", [128, COLS], fp32)
        deg = sb("deg", [128, COLS], fp32)
        eq = sb("eq", [128, COLS], fp32)
        tmp = sb("tmp", [128, COLS], fp32)
        root = sb("root", [128, COLS], fp32)
        dinv = sb("dinv", [128, COLS], fp32)
        norm = sb("norm", [128, COLS], fp32)
        dinv_src = sb("dinv_src", [128, COLS], fp32)
        place = sb("place", [128, COLS], fp32)
        block_base = sb("block_base", [128, COLS], fp32)
        look = sb("look", [128, 2 * COLS + 1], fp32)
        slot_i = sb("slot_i", [128, COLS], i32)
        dstx_i = sb("dstx_i", [128, COLS], i32)
        dsto_i = sb("dsto_i", [128, COLS], i32)
        patch_i = sb("patch_i", [128, 1], i32)
        patchf = sb("patchf", [128, 1], fp32)
        mask = sb("mask", [128, COLS, R], fp32)
        carry_in = sb("carry_in", [128, 128], fp32)
        carry_back = sb("carry_back", [128, 128], fp32)
        diag = sb("diag", [128, 2, 128], fp32)
        srcT = sb("srcT", [COLS // 2, 2, 128], fp32)

        ident = sb("ident", [128, 128], fp32)
        ones = sb("ones", [128, 128], fp32)
        before = sb("before", [128, 128], fp32)
        after = sb("after", [128, 128], fp32)
        count_i = sb("count_i", [128, COLS], i32)
        count1 = sb("count1", [128, COLS], fp32)
        base_i = sb("base_i", [128, 1], i32)
        basef = sb("basef", [128, 1], fp32)
        rel_i = sb("rel_i", [128, R], i32)
        relf = sb("relf", [128, R], fp32)
        eps = sb("eps", [128, 1], fp32)
        zrow = sb("zrow", [1, F], fp32)
        w_arma = sb("w_arma", [128, 128], fp32)
        b_arma = sb("b_arma", [128, 1], fp32)
        w_next = sb("w_next", [128, F], fp32)
        w_root = sb("w_root", [128, 128], fp32)
        w_rootk = sb("w_rootk", [128, 2, F], fp32)
        w_loop = sb("w_loop", [128, 128], fp32)
        w_loopT = sb("w_loopT", [128, 128], fp32)
        w_rel = sb("w_rel", [128, R // 2, F], fp32)
        bnv = sb("bnv", [128, 4, F], fp32)
        bvec = sb("bvec", [128, 2, F], fp32)
        bns = sb("bns", [128, F], fp32)
        bn_t = sb("bn_t", [128, F], fp32)
        bias_row = sb("bias_row", [1, DT, F], fp32)

        xr = sb("xr", [128, 4 * GROUP, F], fp32)
        hr = sb("hr", [128, 4 * GROUP, F], fp32)
        cat = sb("cat", [128, 4 * GROUP, 2 * F], fp32)
        ar = sb("ar", [128, 4 * GROUP, F], fp32)
        ur = sb("ur", [128, 4 * GROUP, F], fp32)
        tr = sb("tr", [128, 4 * GROUP, F], fp32)
        state = sb("state", [128, 4 * GROUP, F], fp32)
        idx = sb("idx", [128, 4, GROUP], i32)
        msg = sb("msg", [128, 2, GROUP, F], fp32)
        sbc = sb("sbc", [128, 4, GROUP * 128], fp32)
        past_first = sb("past_first", [128, 2, GROUP * 128], fp32)
        pick = sb("pick", [128, 2, GROUP * 128], fp32)
        found = sb("found", [128, 2, GROUP, COLS], fp32)
        dropped = sb("dropped", [128, 2, GROUP, COLS], fp32)
        catT = sb("catT", [128, 2, GROUP * 128], fp32)
        reluT = sb("reluT", [128, 2, GROUP * 128], fp32)
        spread = sb("spread", [128, 2, GROUP, R, F], fp32)
        spreadT = sb("spreadT", [128, GROUP, R * F], fp32)
        patch_row = sb("patch_row", [128, F], fp32)
        patched = sb("patched", [128, F], fp32)
        dx = sb("dx", [128, 4, DT * F], fp32)
        dout = sb("dout", [128, 4, DT * F], fp32)
        eout = sb("eout", [128, 4 * GROUP, F], fp32)

        bank = ctx.enter_context(nc.psum_tensor("bank", [128, 8, 512], fp32))
        edge = Lane(sb, sem, "edge", fp32, 128, GROUP, ((0, 1), (2, 3)))
        dense = Lane(sb, sem, "dense", fp32, DP, DT, ((4, 5), (6, 7)))

        edges_in = sem("edges_in")
        weights_in = sem("weights_in")
        filled = sem("filled")
        const = sem("const")
        pool_chain = sem("pool_chain")
        pool_passed = sem("pool_passed")
        prep = sem("prep")
        shown = sem("shown")
        rooted = sem("rooted")
        src_out = sem("src_out")
        zero_out = sem("zero_out")
        ready0 = sem("ready0")
        ready1 = sem("ready1")
        weights_ok = sem("weights_ok")
        idx_set = sem("idx_set")
        gathered = [sem(f"gathered{s}") for s in range(4)]
        bc_in = [sem(f"bc_in{p}") for p in range(2)]
        below = sem("below")
        picked = sem("picked")
        looked = sem("looked")
        placed = sem("placed")
        matched = sem("matched")
        x_spilled = [sem(f"x_spilled{p}") for p in range(2)]
        h_spilled = [sem(f"h_spilled{p}") for p in range(2)]
        u_spilled = [sem(f"u_spilled{p}") for p in range(2)]
        t_spilled = [sem(f"t_spilled{p}") for p in range(2)]
        h_in = [sem(f"h_in{p}") for p in range(2)]
        xu_in = [sem(f"xu_in{p}") for p in range(2)]
        dense_in = [sem(f"dense_in{p}") for p in range(2)]
        dense_out = [sem(f"dense_out{p}") for p in range(2)]
        weighed = sem("weighed")
        scanned = sem("scanned")
        cat_turned = sem("cat_turned")
        cat_taken = sem("cat_taken")
        arma_done = sem("arma_done")
        arma_relu = sem("arma_relu")
        arma_out = sem("arma_out")
        root_taken = sem("root_taken")
        summed = sem("summed")
        spread_done = sem("spread_done")
        spread_turned = sem("spread_turned")
        spread_taken = sem("spread_taken")
        rel_out = sem("rel_out")
        carried = sem("carried")
        patch_in = sem("patch_in")
        patch_made = sem("patch_made")
        patch_out = sem("patch_out")
        scattered = [sem(f"scattered{s}") for s in range(4)]

        block = ctx.enter_context(nc.Block())

        def turns(par):
            return PAIRS + 1 if par == 0 else PAIRS

        def each_iteration(eng, body):
            body(0, 0, 0)
            body(1, 1, 0)
            with eng.Fori(1, PAIRS) as k:
                body(2 * k, 0, k)
                body(2 * k + 1, 1, k)
            body(2 * PAIRS, 0, PAIRS)

        def wait_past(eng, s, value):
            if not (isinstance(value, int) and value <= 0):
                eng.wait_ge(s, value)

        def cols(it, q):
            return bass.ds(2 * GROUP * it + GROUP * q, GROUP)

        def slots(par):
            return slice(2 * GROUP * par, 2 * GROUP * par + 2 * GROUP)

        def slot(par, q):
            s = 2 * par + q
            return slice(GROUP * s, GROUP * s + GROUP)

        def wide(ap, n):
            return ap.unsqueeze(2).to_broadcast([ap.shape[0], ap.shape[1], n])

        def dense_rows(t, it):
            return t[bass.ds(2 * CHUNK * it, 2 * CHUNK), :].rearrange(
                "(c p t) f -> p c (t f)", c=2, t=DT)

        @block.sync
        def _(eng):
            eng.wait_ge(filled, 1)
            for a, b in ((src_i, src), (dst_i, dst), (typ_i, edge_type), (ew, edge_weight)):
                eng.dma_start(a[0:EP, :], b.rearrange("(p j) -> p j", j=COLS)).then_inc(edges_in, 16)
            with nc.allow_non_contiguous_dma(reason="one element per partition"):
                eng.dma_start(next_i[0:EP - 1, :], dst.rearrange("(p j) -> p j", j=COLS)[1:EP, 0:1]
                              ).then_inc(edges_in, 16)
            for k in range(2):
                h = slice(k * F, (k + 1) * F)
                eng.dma_start(w_arma[0:F, h], init_weight[k]).then_inc(weights_in, 16)
                eng.dma_start(w_arma[F:128, h], root_weight[0, k]).then_inc(weights_in, 16)
                eng.dma_start(w_rootk[0:F, k, :], root_weight[1, k]).then_inc(weights_in, 16)
                eng.dma_start(w_rootk[F:128, k, :], root_weight[1, k]).then_inc(weights_in, 16)
                eng.dma_start(w_loop[h, h], self_loop).then_inc(weights_in, 16)
                eng.dma_start(bvec[:, k, :], bias[1, k].to_broadcast([128, F])).then_inc(weights_in, 16)
            eng.dma_start(w_next[:, :], weight[0].rearrange("k f o -> (k f) o")).then_inc(weights_in, 16)
            eng.dma_start(b_arma[:, :], bias[0].rearrange("k a o -> (k o) a")).then_inc(weights_in, 16)
            eng.dma_start(w_rel[:, :, :], rel_weight.rearrange("(c r) f o -> (r f) c o", r=2)
                          ).then_inc(weights_in, 16)
            for k, v in enumerate((bn_gamma, bn_beta, bn_mean, bn_var)):
                eng.dma_start(bnv[:, k, :], v.unsqueeze(0).to_broadcast([128, F])).then_inc(weights_in, 16)
            eng.wait_ge(const, 1)
            for k in range(3):
                eng.dma_start(table[k][ROWS:ROWS + 1, :], zrow[:, :]).then_inc(zero_out, 16)
            eng.wait_ge(ready0, 2)
            eng.dma_start(src_by_column.rearrange("(c j) p -> j c p", c=2), srcT[:, :, :]
                          ).then_inc(src_out, 16)
            eng.wait_ge(src_out, 16)

            def store(stage_base, it, par, k, ring, where, done):
                eng.dma_start(by_col(where)[:, bass.ds(2 * GROUP * it, 2 * GROUP), :],
                              ring[:, slots(par), :]).then_inc(done[par], 16)

            def load(it, par, ring, where, s):
                eng.dma_start(ring[:, slots(par), :],
                              by_col(where)[:, bass.ds(2 * GROUP * it, 2 * GROUP), :]).then_inc(s[par], 16)

            def before_this(it, par, k):
                return it - 1, 1 - par, (k if par == 1 else k - 1)

            def spilling(stage, load_part, store_part):
                def body(it, par, k):
                    load_part(it, par, k)
                    if not (isinstance(it, int) and it == 0):
                        store_part(*before_this(it, par, k))
                each_iteration(eng, body)
                store_part(2 * PAIRS, 0, PAIRS)

            def gather_done(stage, par, k):
                for q in range(2):
                    eng.wait_ge(gathered[2 * par + q], 16 * GROUP * (stage * turns(par) + k + 1))

            def load0(it, par, k):
                wait_past(eng, picked, 2 * it - 2)
                eng.dma_start(sbc[:, 2 * par:2 * par + 2, :],
                              src_by_column[bass.ds(2 * GROUP * it, 2 * GROUP), :]
                              .rearrange("(g t) p -> g (t p)", g=2).unsqueeze(0)
                              .to_broadcast([128, 2, GROUP * 128])).then_inc(bc_in[par], 16)

            def store0(it, par, k):
                gather_done(0, par, k)
                store(0, it, par, k, xr, xd_dram, x_spilled)

            spilling(0, load0, store0)

            def load_dense(base, it, par, k):
                wait_past(eng, dense.mid, base * 2 * ITERS + 2 * it - 2)
                eng.dma_start(dx[0:DP, 2 * par:2 * par + 2, :], dense_rows(x, base * ITERS + it)
                              ).then_inc(dense_in[par], 16)

            def store_dense(base, it, par, k):
                eng.wait_ge(dense.out, base * 2 * ITERS + 2 * it + 2)
                eng.dma_start(dense_rows(out, base * ITERS + it), dout[0:DP, 2 * par:2 * par + 2, :]
                              ).then_inc(dense_out[par], 16)

            def store1(it, par, k):
                gather_done(1, par, k)
                store(1, it, par, k, xr, xs_dram, x_spilled)
                eng.wait_ge(edge.norm1.hidden, 2 * it + 2)
                store(1, it, par, k, hr, hs_dram, h_spilled)
                eng.wait_ge(scanned, 2 * GROUP * it + 2 * GROUP + 1)
                store(1, it, par, k, state, table[0], t_spilled)
                store_dense(0, it, par, k)

            spilling(1, lambda it, par, k: load_dense(0, it, par, k), store1)

            for p in range(2):
                eng.wait_ge(h_spilled[p], 16 * turns(p))

            def load2(it, par, k):
                wait_past(eng, cat_turned, 2 * it - 2)
                eng.dma_start(cat[:, slots(par), F:2 * F],
                              by_col(hs_dram)[:, bass.ds(2 * GROUP * it, 2 * GROUP), :]).then_inc(h_in[par], 16)
                load_dense(1, it, par, k)

            def store2(it, par, k):
                eng.wait_ge(root_taken, 2 * it + 2)
                store(2, it, par, k, ur, us_dram, u_spilled)
                eng.wait_ge(scanned, COLS + 2 * GROUP * it + 2 * GROUP + 1)
                store(2, it, par, k, state, table[1], t_spilled)
                store_dense(1, it, par, k)

            spilling(2, load2, store2)

            for p in range(2):
                eng.wait_ge(u_spilled[p], 16 * turns(p))
                eng.wait_ge(x_spilled[p], 16 * 2 * turns(p))

            def load3(it, par, k):
                wait_past(eng, edge.mid, 2 * it - 2)
                load(it, par, xr, xs_dram, xu_in)
                load(it, par, ur, us_dram, xu_in)

            def store3(it, par, k):
                eng.wait_ge(scanned, 2 * COLS + 2 * GROUP * it + 2 * GROUP + 1)
                store(3, it, par, k, state, table[2], t_spilled)

            spilling(3, load3, store3)

            eng.wait_ge(edge.mid, GROUPS)
            eng.wait_ge(patch_out, 16 * 3)

            def load4(it, par, k):
                wait_past(eng, edge.out, 2 * it - 2)
                load(it, par, xr, xd_dram, xu_in)
                load(it, par, ur, table[1], xu_in)
                load(it, par, tr, table[2], xu_in)

            each_iteration(eng, load4)
            for p in range(2):
                eng.wait_ge(dense_out[p], 16 * 2 * turns(p))
                eng.wait_ge(t_spilled[p], 16 * 3 * turns(p))
            eng.wait_ge(zero_out, 16 * 3)

        @block.gpsimd
        def _(eng):
            eng.memset(zrow[:, :], 0.0).then_inc(const, 1)
            eng.memset(ones[:, :], 1.0).then_inc(pool_chain, 1)
            eng.memset(eps[:, :], EPS).then_inc(pool_chain, 1)
            eng.iota(count_i[:, :], pattern=[[1, COLS]], base=1, channel_multiplier=0).then_inc(pool_chain, 1)
            eng.iota(base_i[:, :], pattern=[[0, 1]], base=0, channel_multiplier=COLS).then_inc(pool_chain, 1)
            eng.iota(rel_i[:, :], pattern=[[1, R]], base=0, channel_multiplier=0).then_inc(pool_chain, 1)
            eng.wait_ge(pool_chain, 5)
            eng.affine_select(out=ident[:, :], in_=ones[:, :], compare_op=ALU.is_equal, fill=0.0, base=0,
                              pattern=[[-1, 128]], channel_multiplier=1).then_inc(const, 1)
            eng.affine_select(out=before[:, :], in_=ones[:, :], compare_op=ALU.is_gt, fill=0.0, base=0,
                              pattern=[[1, 128]], channel_multiplier=-1).then_inc(const, 1)
            eng.affine_select(out=after[:, :], in_=ones[:, :], compare_op=ALU.is_gt, fill=0.0, base=0,
                              pattern=[[-1, 128]], channel_multiplier=1).then_inc(const, 1)

            def await_count(s, value):
                wait_past(eng, s, value)
                eng.sem_inc(pool_passed, 1)

            def place_idx(stage, it, par, q, indices):
                eng.tensor_copy(idx[:, 2 * par + q, :], indices[:, cols(it, q)]).then_inc(idx_set, 1)
                await_count(idx_set, stage * GROUPS + 2 * it + q + 1)

            def gather(stage, it, par, q, indices, rows, ring):
                place_idx(stage, it, par, q, indices)
                for t in range(GROUP):
                    s = 2 * par + q
                    eng.indirect_dma_start(
                        out=ring[:, GROUP * s + t, 0:F], out_offset=None, in_=rows,
                        in_offset=bass.IndirectOffsetOnAxis(ap=idx[:, s, t:t + 1], axis=0),
                    ).then_inc(gathered[s], 16)

            eng.wait_ge(ready0, 1)

            def gather0(it, par, k):
                await_count(x_spilled[par], 16 * k)
                for q in range(2):
                    gather(0, it, par, q, dstx_i, x, xr)

            each_iteration(eng, gather0)

            def gather1(it, par, k):
                await_count(x_spilled[par], 16 * (turns(par) + k))
                for q in range(2):
                    await_count(edge.norm1.centred, 2 * it + q - 3)
                    gather(1, it, par, q, src_i, x, xr)

            each_iteration(eng, gather1)

            def patch(stage):
                for p in range(2):
                    eng.wait_ge(t_spilled[p], 16 * (stage + 1) * turns(p))
                eng.indirect_dma_start(
                    out=patch_row[:, :], out_offset=None, in_=table[stage][:, :],
                    in_offset=bass.IndirectOffsetOnAxis(ap=patch_i[:, 0:1], axis=0)).then_inc(patch_in, 16)
                eng.wait_ge(patch_made, stage + 1)
                eng.indirect_dma_start(
                    out=table[stage][:, :], out_offset=bass.IndirectOffsetOnAxis(ap=patch_i[:, 0:1], axis=0),
                    in_=patched[:, :], in_offset=None).then_inc(patch_out, 16)
                eng.wait_ge(patch_out, 16 * (stage + 1))

            patch(0)
            eng.wait_ge(zero_out, 16 * 3)

            def gather2(it, par, k):
                for q in range(2):
                    await_count(cat_turned, 2 * it + q - 3)
                    gather(2, it, par, q, slot_i, table[0][:, :], cat)

            each_iteration(eng, gather2)
            patch(1)

            def gather3(it, par, k):
                for q in range(2):
                    await_count(summed, 2 * it + q - 3)
                    gather(3, it, par, q, slot_i, table[1][:, :], ar)

            each_iteration(eng, gather3)
            patch(2)

            for p in range(2):
                eng.wait_ge(dense_out[p], 16 * 2 * turns(p))

            def scatter(it, par, k):
                for q in range(2):
                    s = 2 * par + q
                    await_count(scattered[s], 16 * GROUP * k)
                    place_idx(4, it, par, q, dsto_i)
                    await_count(edge.out, 2 * it + q + 1)
                    for t in range(GROUP):
                        eng.indirect_dma_start(
                            out=out, out_offset=bass.IndirectOffsetOnAxis(ap=idx[:, s, t:t + 1], axis=0),
                            in_=eout[:, GROUP * s + t, :], in_offset=None,
                            bounds_check=N - 1, oob_is_err=False).then_inc(scattered[s], 16)

            each_iteration(eng, scatter)
            for s in range(4):
                eng.wait_ge(scattered[s], 16 * GROUP * turns(s // 2))

        def act_square(eng, lane, s, q, n):
            eng.wait_ge(s.centred, n + 1)
            eng.activation(lane.sq[0:lane.rows, q], lane.xc[0:lane.rows, q], ACT.Square).then_inc(s.squared, 1)

        def act_root(eng, lane, s, q, n):
            eng.wait_ge(s.spread, n + 1)
            eng.activation(lane.std[0:lane.rows, q], lane.var[0:lane.rows, q], ACT.Sqrt,
                           bias=eps[0:lane.rows, :], scale=1.0 / F).then_inc(s.root, 1)

        def act_take(eng, lane, turned, taken, q, n):
            eng.wait_ge(turned, n + 1)
            pairs = lane.tiles // 2
            eng.activation(lane.hT[:, q, :, 0:lane.rows],
                           bank[:, lane.transposed_bank[q], 0:128 * pairs]
                           .rearrange("p (a b) -> p a b", a=pairs)[:, :, 0:lane.rows],
                           ACT.Copy).then_inc(taken, 1)

        @block.scalar
        def _(eng):
            eng.wait_ge(prep, PREP_DEG)
            eng.activation(root[:, :], tmp[:, :], ACT.Sqrt).then_inc(rooted, 1)
            eng.wait_ge(weights_in, 16 * 19)
            eng.wait_ge(pool_chain, 2)
            eng.activation(bn_t[:, :], bnv[:, 3, :], ACT.Sqrt, bias=eps[:, :]).then_inc(rooted, 1)

            def norms(lanes):
                for a in lanes:
                    act_square(eng, *a)
                for a in lanes:
                    act_root(eng, *a)

            def node_network(lanes1, lanes2):
                norms([(l, l.norm1, q, n1) for l, q, n1, n in lanes1])
                for l, q, n1, n in lanes2:
                    act_take(eng, l, l.turned1, l.taken1, q, n)
                norms([(l, l.norm2, q, n) for l, q, n1, n in lanes2])
                for l, q, n1, n in lanes2:
                    act_take(eng, l, l.turned2, l.taken2, q, n)

            def body1(it, par, k):
                d = [(dense, q, 2 * it + q, 2 * it + q) for q in range(2)]
                node_network([(edge, q, 2 * it + q, 0) for q in range(2)] + d, d)

            each_iteration(eng, body1)

            def body2(it, par, k):
                for q in range(2):
                    eng.wait_ge(cat_turned, 2 * it + q + 1)
                    eng.activation(catT[:, q, :], bank[:, edge.transposed_bank[q], :], ACT.Copy
                                   ).then_inc(cat_taken, 1)
                for q in range(2):
                    eng.wait_ge(arma_done, 2 * it + q + 1)
                    eng.activation(reluT[:, q, :], bank[:, edge.transposed_bank[q], :], ACT.Relu,
                                   bias=b_arma[:, :]).then_inc(arma_relu, 1)
                if not (isinstance(k, int) and k == 0):
                    eng.wait_ge(u_spilled[par], 16 * k)
                for q in range(2):
                    eng.wait_ge(arma_out, 2 * it + q + 1)
                    eng.activation(ur[:, slot(par, q), :],
                                   bank[:, edge.product_bank[q], 0:GROUP * F].rearrange("p (t f) -> p t f", f=F),
                                   ACT.Copy).then_inc(root_taken, 1)
                n = 2 * ITERS + 2 * it
                d = [(dense, q, n + q, n + q) for q in range(2)]
                node_network(d, d)

            each_iteration(eng, body2)

            def body3(it, par, k):
                norms([(edge, edge.norm1, q, GROUPS + 2 * it + q) for q in range(2)])
                for q in range(2):
                    for t in range(GROUP):
                        eng.wait_ge(spread_turned, GROUP * (2 * it + q) + t + 1)
                        eng.activation(spreadT[:, t, :], bank[:, 4 + t, :], ACT.Copy).then_inc(spread_taken, 1)

            each_iteration(eng, body3)

            def body4(it, par, k):
                e = [(edge, q, 2 * GROUPS + 2 * it + q, 2 * it + q) for q in range(2)]
                node_network(e, e)

            each_iteration(eng, body4)

        def pe_turn(eng, lane, hidden, turned, h, q, n, nh):
            eng.wait_ge(hidden, nh + 1)
            P = lane.rows
            for a in range(lane.tiles // 2):
                last = nc.tensor.transpose(bank[:, lane.transposed_bank[q], 128 * a:128 * a + P],
                                           h[0:P, 2 * a:2 * a + 2, :].rearrange("p t f -> p (t f)"),
                                           ident[0:P, 0:P])
            last.then_inc(turned, 1)

        def pe_product(eng, lane, taken, product, w, q, n, with_bias):
            eng.wait_ge(taken, n + 1)
            P = lane.rows
            b = lane.product_bank[q]
            if with_bias:
                nc.tensor.matmul(bank[0:P, b, 0:lane.tiles * F], ones[0:1, 0:P],
                                 bias_row[:, 0:lane.tiles, :].rearrange("p t f -> p (t f)"),
                                 start=True, stop=False)
            pairs = lane.tiles // 2
            for a in range(pairs):
                last = nc.tensor.matmul(bank[0:P, b, 128 * a:128 * a + 128], lane.hT[:, q, a, 0:P], w[:, :],
                                        start=not with_bias, stop=(a == pairs - 1 or not with_bias))
            last.then_inc(product, 1)

        def pe_network(eng, items):
            for lane, q, n1, n in items:
                pe_turn(eng, lane, lane.norm1.hidden, lane.turned1, lane.h[:, q], q, n, n1)
            for lane, q, n1, n in items:
                pe_product(eng, lane, lane.taken1, lane.product1, w_root, q, n, True)
            for lane, q, n1, n in items:
                pe_turn(eng, lane, lane.norm2.hidden, lane.turned2, lane.h[:, q], q, n, n)
            for lane, q, n1, n in items:
                pe_product(eng, lane, lane.taken2, lane.product2, w_loopT, q, n, False)

        @block.tensor
        def _(eng):
            eng.wait_ge(const, 4)
            eng.wait_ge(prep, PREP_DIAG)
            nc.tensor.matmul(bank[:, 0, 0:256], ones[:, :], diag[:, :, :].rearrange("p a b -> p (a b)"),
                             start=True, stop=True).then_inc(shown, 1)
            for c in range(2):
                nc.tensor.transpose(bank[0:COLS // 2, 4 + c, 0:128],
                                    srcf[:, c * (COLS // 2):(c + 1) * (COLS // 2)], ident[:, :]
                                    ).then_inc(shown, 1)
            eng.wait_ge(prep, PREP_TAIL)
            nc.tensor.matmul(bank[:, 1, 0:1], carry_in[:, :], deg[:, COLS - 1:COLS],
                             start=True, stop=True).then_inc(shown, 1)
            eng.wait_ge(prep, PREP_BACK)
            nc.tensor.matmul(bank[:, 2, 0:1], carry_back[:, :], dinv[:, 0:1],
                             start=True, stop=True).then_inc(shown, 1)
            eng.wait_ge(weights_in, 16 * 19)
            nc.tensor.transpose(bank[:, 3, 0:128], w_loop[:, :], ident[:, :]).then_inc(shown, 1)

            eng.wait_ge(ready0, 3)

            def body0(it, par, k):
                for q in range(2):
                    eng.wait_ge(picked, 2 * it + q + 1)
                    wait_past(eng, matched, 2 * it + q - 1)
                    for t in range(GROUP):
                        last = nc.tensor.matmul(bank[:, 4 * q + t, 0:2 * COLS + 1],
                                                pick[:, q, 128 * t:128 * t + 128], look[:, :],
                                                start=True, stop=True)
                    last.then_inc(looked, 1)

            each_iteration(eng, body0)
            eng.wait_ge(matched, GROUPS)
            eng.wait_ge(weights_ok, 2)

            def body1(it, par, k):
                pe_network(eng, [(dense, q, 2 * it + q, 2 * it + q) for q in range(2)])

            each_iteration(eng, body1)

            def carry(stage):
                eng.wait_ge(scanned, (stage + 1) * COLS + 1)
                last_slot = GROUP * 2 - 1
                nc.tensor.matmul(bank[:, 3, 0:F], carry_in[:, :], state[:, last_slot, :],
                                 start=True, stop=True).then_inc(carried, 1)

            carry(0)
            eng.wait_ge(patch_made, 1)

            def body2(it, par, k):
                for q in range(2):
                    s = 2 * par + q
                    eng.wait_ge(h_in[par], 16 * (k + 1))
                    eng.wait_ge(gathered[s], 16 * GROUP * (2 * turns(par) + k + 1))
                    wait_past(eng, arma_relu, 2 * it + q - 1)
                    for t in range(GROUP):
                        last = nc.tensor.transpose(bank[:, edge.transposed_bank[q], 128 * t:128 * t + 128],
                                                   cat[:, GROUP * s + t, :], ident[:, :])
                    last.then_inc(cat_turned, 1)
                for q in range(2):
                    eng.wait_ge(cat_taken, 2 * it + q + 1)
                    nc.tensor.matmul(bank[:, edge.transposed_bank[q], :], w_arma[:, :], catT[:, q, :],
                                     start=True, stop=True).then_inc(arma_done, 1)
                for q in range(2):
                    b = edge.product_bank[q]
                    wait_past(eng, weighed, GROUPS + 2 * it + q - 1)
                    nc.tensor.matmul(bank[:, b, 0:GROUP * F], ones[0:1, :],
                                     bias_row[:, 0:GROUP, :].rearrange("p t f -> p (t f)"),
                                     start=True, stop=False)
                    for t in range(GROUP):
                        nc.tensor.matmul(bank[:, b, F * t:F * t + F], catT[:, q, 128 * t:128 * t + 128],
                                         w_root[:, F:128], start=False, stop=(t == GROUP - 1))
                    eng.wait_ge(arma_relu, 2 * it + q + 1)
                    for t in range(GROUP):
                        last = nc.tensor.matmul(bank[:, b, GROUP * F + F * t:GROUP * F + F * t + F],
                                                reluT[:, q, 128 * t:128 * t + 128], w_next[:, :],
                                                start=True, stop=True)
                    last.then_inc(arma_out, 1)
                n = 2 * ITERS + 2 * it
                pe_network(eng, [(dense, q, n + q, n + q) for q in range(2)])

            each_iteration(eng, body2)
            carry(1)
            eng.wait_ge(patch_made, 2)

            def body3(it, par, k):
                for q in range(2):
                    def turn(t):
                        eng.wait_ge(spread_done, GROUP * (2 * it + q) + t + 1)
                        for c in range(R // 2):
                            last = nc.tensor.transpose(
                                bank[:, 4 + t, 128 * c:128 * c + 128],
                                spread[:, q, t, 2 * c:2 * c + 2, :].rearrange("p r f -> p (r f)"), ident[:, :])
                        last.then_inc(spread_turned, 1)

                    def multiply(t):
                        eng.wait_ge(spread_taken, GROUP * (2 * it + q) + t + 1)
                        for c in range(R // 2):
                            last = nc.tensor.matmul(bank[:, edge.product_bank[q], F * t:F * t + F],
                                                    spreadT[:, t, 128 * c:128 * c + 128], w_rel[:, c, :],
                                                    start=(c == 0), stop=(c == R // 2 - 1))
                        last.then_inc(rel_out, 1)

                    turn(0)
                    for t in range(1, GROUP):
                        turn(t)
                        multiply(t - 1)
                    multiply(GROUP - 1)

            each_iteration(eng, body3)
            carry(2)
            eng.wait_ge(patch_made, 3)

            def body4(it, par, k):
                pe_network(eng, [(edge, q, 2 * GROUPS + 2 * it + q, 2 * it + q) for q in range(2)])

            each_iteration(eng, body4)

        def ln_total(eng, lane, s, q, n, xin):
            nc.vector.tensor_reduce(lane.sum[0:lane.rows, q], xin, AX.X, ALU.add).then_inc(s.total, 1)

        def ln_centre(eng, lane, s, q, n, xin):
            eng.wait_ge(s.total, n + 1)
            nc.vector.scalar_tensor_tensor(out=lane.xc[0:lane.rows, q], in0=wide(lane.sum[0:lane.rows, q], F),
                                           scalar=-1.0 / F, in1=xin, op0=ALU.mult, op1=ALU.add
                                           ).then_inc(s.centred, 1)

        def ln_spread(eng, lane, s, q, n):
            eng.wait_ge(s.squared, n + 1)
            nc.vector.tensor_reduce(lane.var[0:lane.rows, q], lane.sq[0:lane.rows, q], AX.X, ALU.add
                                    ).then_inc(s.spread, 1)

        def ln_scale(eng, lane, s, q, n):
            eng.wait_ge(s.root, n + 1)
            nc.vector.reciprocal(lane.inv[0:lane.rows, q], lane.std[0:lane.rows, q]).then_inc(s.scale, 1)

        def ln_hidden(eng, lane, s, q, n, h):
            eng.wait_ge(s.scale, n + 1)
            nc.vector.scalar_tensor_tensor(out=h, in0=lane.xc[0:lane.rows, q], scalar=0.0,
                                           in1=wide(lane.inv[0:lane.rows, q], F), op0=ALU.max, op1=ALU.mult
                                           ).then_inc(s.hidden, 1)

        def norms_v(eng, items):
            for lane, s, q, n, xin, h in items:
                ln_total(eng, lane, s, q, n, xin)
            for lane, s, q, n, xin, h in items:
                ln_centre(eng, lane, s, q, n, xin)
            for lane, s, q, n, xin, h in items:
                ln_spread(eng, lane, s, q, n)
            for lane, s, q, n, xin, h in items:
                ln_scale(eng, lane, s, q, n)
            for lane, s, q, n, xin, h in items:
                ln_hidden(eng, lane, s, q, n, h)

        def tiles_of(ap, lane):
            return ap.rearrange("p (t f) -> p t f", f=F)

        def product_of(lane, q):
            return tiles_of(bank[0:lane.rows, lane.product_bank[q], 0:lane.tiles * F], lane)

        @block.vector
        def _(eng):
            v = nc.vector
            steps = [0]

            def link(ins):
                steps[0] += 1
                ins.then_inc(prep, 1)
                eng.wait_ge(prep, steps[0])

            link(v.memset(src_i[:, :], 0))
            link(v.memset(typ_i[:, :], 0))
            link(v.memset(ew[:, :], 0.0))
            link(v.memset(next_i[:, :], NOWHERE))
            link(v.memset(w_loop[:, :], 0.0))
            v.memset(dst_i[:, :], NOWHERE).then_inc(filled, 1)
            link(v.memset(w_root[:, :], 0.0))
            eng.wait_ge(edges_in, 16 * 5)
            eng.wait_ge(const, 4)
            for a, b in ((srcf, src_i), (dstf, dst_i), (typf, typ_i), (nextf, next_i), (count1, count_i),
                         (basef, base_i), (relf, rel_i)):
                link(v.tensor_copy(a[:, :], b[:, :]))
            first, last = dstf[:, 0:1], dstf[:, COLS - 1:COLS]
            link(v.tensor_scalar(diag[:, 0, :], ident[:, :], first, None, ALU.mult))
            link(v.tensor_scalar(diag[:, 1, :], ident[:, :], last, None, ALU.mult))
            assert steps[0] == PREP_DIAG
            link(v.tensor_scalar(tmp[:, :], dstf[:, :], float(N - 1), None, ALU.min))
            link(v.tensor_copy(dstx_i[:, :], tmp[:, :]))
            v.tensor_scalar(src1[:, :], srcf[:, :], 1.0, None, ALU.add).then_inc(ready0, 1)
            eng.wait_ge(shown, 3)
            for c in range(2):
                link(v.tensor_copy(srcT[:, c, :], bank[0:COLS // 2, 4 + c, 0:128]))
            v.tensor_scalar(tmp[:, :], dstf[:, :], first, None, ALU.is_equal).then_inc(ready0, 1)
            eng.wait_ge(ready0, 2)
            link(v.tensor_reduce(patchf[:, :], tmp[:, :], AX.X, ALU.add))
            link(v.scalar_tensor_tensor(out=patchf[:, :], in0=patchf[:, :], scalar=-1.0, in1=basef[:, :],
                                        op0=ALU.add, op1=ALU.add))
            link(v.tensor_copy(patch_i[:, :], patchf[:, :]))
            link(v.scalar_tensor_tensor(out=carry_in[:, :], in0=bank[:, 0, 0:128], scalar=last,
                                        in1=before[:, :], op0=ALU.is_equal, op1=ALU.mult))
            link(v.scalar_tensor_tensor(out=carry_back[:, :], in0=bank[:, 0, 128:256], scalar=first,
                                        in1=after[:, :], op0=ALU.is_equal, op1=ALU.mult))
            link(v.memset(same[:, 0:1], 0.0))
            link(v.tensor_tensor(same[:, 1:COLS], dstf[:, 1:COLS], dstf[:, 0:COLS - 1], ALU.is_equal))
            link(v.tensor_tensor(final[:, 0:COLS - 1], dstf[:, 0:COLS - 1], dstf[:, 1:COLS], ALU.not_equal))
            link(v.tensor_tensor(final[:, COLS - 1:COLS], last, nextf[:, :], ALU.not_equal))
            link(v.tensor_copy(deg[:, :], ew[:, :]))
            k = 1
            while k < COLS:
                link(v.tensor_tensor(eq[:, k:COLS], dstf[:, k:COLS], dstf[:, 0:COLS - k], ALU.is_equal))
                link(v.tensor_tensor(tmp[:, k:COLS], eq[:, k:COLS], deg[:, 0:COLS - k], ALU.mult))
                link(v.tensor_tensor(deg[:, k:COLS], deg[:, k:COLS], tmp[:, k:COLS], ALU.add))
                k *= 2
            assert steps[0] == PREP_TAIL, steps
            link(v.tensor_scalar(eq[:, :], dstf[:, :], first, None, ALU.is_equal))
            eng.wait_ge(shown, 4)
            link(v.tensor_copy(patchf[:, :], bank[:, 1, 0:1]))
            link(v.scalar_tensor_tensor(out=deg[:, :], in0=eq[:, :], scalar=patchf[:, :], in1=deg[:, :],
                                        op0=ALU.mult, op1=ALU.add))
            link(v.tensor_scalar(tmp[:, :], deg[:, :], 1e-12, None, ALU.max))
            assert steps[0] == PREP_DEG, steps
            link(v.tensor_scalar(eq[:, :], deg[:, :], 0.0, None, ALU.is_gt))
            eng.wait_ge(rooted, 1)
            link(v.reciprocal(dinv[:, :], root[:, :]))
            link(v.tensor_tensor(dinv[:, :], dinv[:, :], eq[:, :], ALU.mult))
            link(v.tensor_tensor(dinv[:, :], dinv[:, :], final[:, :], ALU.mult))
            link(v.scalar_tensor_tensor(out=look[:, 0:COLS], in0=dstf[:, :], scalar=1.0, in1=final[:, :],
                                        op0=ALU.add, op1=ALU.mult))
            link(v.tensor_copy(look[:, COLS:2 * COLS], dinv[:, :]))
            v.tensor_copy(look[:, 2 * COLS:2 * COLS + 1], basef[:, :]).then_inc(ready0, 1)
            k = 1
            while k < COLS:
                link(v.tensor_tensor(eq[:, 0:COLS - k], dstf[:, k:COLS], dstf[:, 0:COLS - k], ALU.is_equal))
                link(v.tensor_tensor(tmp[:, 0:COLS - k], eq[:, 0:COLS - k], dinv[:, k:COLS], ALU.mult))
                link(v.tensor_tensor(dinv[:, 0:COLS - k], dinv[:, 0:COLS - k], tmp[:, 0:COLS - k], ALU.add))
                k *= 2
            assert steps[0] == PREP_BACK, steps
            link(v.tensor_scalar(eq[:, :], dstf[:, :], last, None, ALU.is_equal))
            eng.wait_ge(shown, 5)
            link(v.tensor_copy(patchf[:, :], bank[:, 2, 0:1]))
            link(v.scalar_tensor_tensor(out=dinv[:, :], in0=eq[:, :], scalar=patchf[:, :], in1=dinv[:, :],
                                        op0=ALU.mult, op1=ALU.add))
            link(v.tensor_tensor(norm[:, :], dinv[:, :], ew[:, :], ALU.mult))
            link(v.scalar_tensor_tensor(out=tmp[:, :], in0=dstf[:, :], scalar=float(-NOWHERE), in1=final[:, :],
                                        op0=ALU.add, op1=ALU.mult))
            link(v.tensor_scalar(dsto_i[:, :], tmp[:, :], float(NOWHERE), None, ALU.add))
            link(v.tensor_tensor(mask[:, :, :], wide(typf[:, :], R),
                                 relf[:, None, :].to_broadcast([128, COLS, R]), ALU.is_equal))
            link(v.memset(state[:, :, :], 0.0))

            eng.wait_ge(weights_in, 16 * 19)
            eng.wait_ge(rooted, 2)
            link(v.reciprocal(bns[:, :], bn_t[:, :]))
            link(v.tensor_tensor(bns[:, :], bns[:, :], bnv[:, 0, :], ALU.mult))
            link(v.scalar_tensor_tensor(out=w_next[:, :], in0=w_next[:, :], scalar=0.5, in1=bns[:, :],
                                        op0=ALU.mult, op1=ALU.mult))
            link(v.tensor_tensor(w_rootk[:, 0, :], w_rootk[:, 0, :], w_rootk[:, 1, :], ALU.add))
            for c in range(2):
                h = slice(c * F, (c + 1) * F)
                link(v.scalar_tensor_tensor(out=w_root[h, h], in0=w_rootk[h, 0, :], scalar=0.5, in1=bns[h, :],
                                            op0=ALU.mult, op1=ALU.mult))
            link(v.tensor_tensor(bn_t[:, :], bvec[:, 0, :], bvec[:, 1, :], ALU.add))
            link(v.scalar_tensor_tensor(out=bn_t[:, :], in0=bn_t[:, :], scalar=0.5, in1=bnv[:, 2, :],
                                        op0=ALU.mult, op1=ALU.subtract))
            link(v.tensor_tensor(bn_t[:, :], bn_t[:, :], bns[:, :], ALU.mult))
            link(v.tensor_tensor(bias_row[:, :, :], bn_t[0:1, None, :].to_broadcast([1, DT, F]),
                                 bnv[0:1, 1:2, :].to_broadcast([1, DT, F]), ALU.add))
            eng.wait_ge(shown, 6)
            v.tensor_copy(w_loopT[:, :], bank[:, 3, 0:128]).then_inc(weights_ok, 1)

            def body0(it, par, k):
                for q in range(2):
                    if q == 0:
                        eng.wait_ge(bc_in[par], 16 * (k + 1))
                    wait_past(eng, looked, 2 * it + q - 1)
                    v.tensor_scalar(past_first[:, q, :], sbc[:, 2 * par + q, :], first, None, ALU.is_ge
                                    ).then_inc(below, 1)
                for q in range(2):
                    eng.wait_ge(below, 2 * it + q + 1)
                    v.scalar_tensor_tensor(out=pick[:, q, :], in0=sbc[:, 2 * par + q, :], scalar=nextf[:, :],
                                           in1=past_first[:, q, :], op0=ALU.is_lt, op1=ALU.mult
                                           ).then_inc(picked, 1)
                for q in range(2):
                    eng.wait_ge(looked, 2 * it + q + 1)
                    wait_past(eng, matched, 2 * it + q - 1)
                    for t in range(GROUP):
                        j = bass.ds(2 * GROUP * it + GROUP * q + t, 1)
                        v.scalar_tensor_tensor(out=found[:, q, t, :], in0=bank[:, 4 * q + t, 0:COLS],
                                               scalar=src1[:, j], in1=count1[:, :], op0=ALU.is_equal,
                                               op1=ALU.mult, accum_out=place[:, j]).then_inc(placed, 1)
                    for t in range(GROUP):
                        j = bass.ds(2 * GROUP * it + GROUP * q + t, 1)
                        eng.wait_ge(placed, 2 * GROUP * it + GROUP * q + t + 1)
                        v.scalar_tensor_tensor(out=dropped[:, q, t, :], in0=found[:, q, t, :], scalar=0.0,
                                               in1=bank[:, 4 * q + t, COLS:2 * COLS], op0=ALU.is_gt,
                                               op1=ALU.mult, accum_out=dinv_src[:, j])
                    v.tensor_copy(block_base[:, cols(it, q)], bank[:, 4 * q:4 * q + 4, 2 * COLS]
                                  ).then_inc(matched, 1)

            each_iteration(eng, body0)
            eng.wait_ge(matched, GROUPS)
            link(v.tensor_tensor(norm[:, :], norm[:, :], dinv_src[:, :], ALU.mult))
            link(v.tensor_scalar(eq[:, :], place[:, :], 0.0, None, ALU.is_gt))
            link(v.tensor_tensor(tmp[:, :], block_base[:, :], place[:, :], ALU.add))
            link(v.scalar_tensor_tensor(out=tmp[:, :], in0=tmp[:, :], scalar=float(-1 - ROWS), in1=eq[:, :],
                                        op0=ALU.add, op1=ALU.mult))
            v.tensor_scalar(slot_i[:, :], tmp[:, :], float(ROWS), None, ALU.add).then_inc(weights_ok, 1)

            def scan(stage, it, par, q, tile):
                for t in range(GROUP):
                    at = GROUP * (2 * par + q) + t
                    j = 2 * GROUP * it + GROUP * q + t
                    eng.wait_ge(scanned, stage * COLS + j + 1)
                    v.scalar_tensor_tensor(out=state[:, at, :], in0=state[:, (at - 1) % (4 * GROUP), :],
                                           scalar=same[:, bass.ds(j, 1)], in1=tile(t),
                                           op0=ALU.mult, op1=ALU.add).then_inc(scanned, 1)

            def node_tail(items):
                for lane, q, n, xin, res, sums in items:
                    if sums:
                        eng.wait_ge(lane.product1, n + 1)
                        v.tensor_tensor(lane.sq[:, q], product_of(lane, q), sums[0], ALU.add
                                        ).then_inc(lane.added1, 1)
                for lane, q, n, xin, res, sums in items:
                    eng.wait_ge(lane.added1 if sums else lane.product1, n + 1)
                    got = lane.sq[:, q] if sums else product_of(lane, q)
                    v.scalar_tensor_tensor(out=lane.x1[0:lane.rows, q], in0=got, scalar=0.0, in1=xin,
                                           op0=ALU.max, op1=ALU.add).then_inc(lane.mid, 1)
                for i, (lane, q, n, xin, res, sums) in enumerate(items):
                    eng.wait_ge(lane.mid, MID_BASE[lane is edge] + n + 1)
                    ln_total(eng, lane, lane.norm2, q, n, lane.x1[0:lane.rows, q])
                for lane, q, n, xin, res, sums in items:
                    ln_centre(eng, lane, lane.norm2, q, n, lane.x1[0:lane.rows, q])
                for lane, q, n, xin, res, sums in items:
                    ln_spread(eng, lane, lane.norm2, q, n)
                for lane, q, n, xin, res, sums in items:
                    ln_scale(eng, lane, lane.norm2, q, n)
                for lane, q, n, xin, res, sums in items:
                    ln_hidden(eng, lane, lane.norm2, q, n, lane.h[0:lane.rows, q])
                for lane, q, n, xin, res, sums in items:
                    if sums:
                        eng.wait_ge(lane.product2, n + 1)
                        v.tensor_tensor(lane.sq[:, q], product_of(lane, q), sums[1], ALU.add
                                        ).then_inc(lane.added2, 1)
                for lane, q, n, xin, res, sums in items:
                    eng.wait_ge(lane.added2 if sums else lane.product2, n + 1)
                    got = lane.sq[:, q] if sums else product_of(lane, q)
                    v.scalar_tensor_tensor(out=res, in0=got, scalar=0.0, in1=lane.x1[0:lane.rows, q],
                                           op0=ALU.max, op1=ALU.add).then_inc(lane.out, 1)

            MID_BASE = {False: 0, True: GROUPS}

            def dense_items(base, it, par):
                n = base * 2 * ITERS + 2 * it
                xin = [tiles_of(dx[0:DP, 2 * par + q, :], dense) for q in range(2)]
                res = [tiles_of(dout[0:DP, 2 * par + q, :], dense) for q in range(2)]
                head = [(dense, dense.norm1, q, n + q, xin[q], dense.h[0:DP, q]) for q in range(2)]
                tail = [(dense, q, n + q, xin[q], res[q], None) for q in range(2)]
                return head, tail

            def await_dense(base, par, k):
                eng.wait_ge(dense_in[par], 16 * (base * turns(par) + k + 1))
                wait_past(eng, dense_out[par], 16 * (base * turns(par) + k))

            def body1(it, par, k):
                wait_past(eng, h_spilled[par], 16 * k)
                await_dense(0, par, k)
                for q in range(2):
                    eng.wait_ge(gathered[2 * par + q], 16 * GROUP * (turns(par) + k + 1))
                head, tail = dense_items(0, it, par)
                norms_v(eng, [(edge, edge.norm1, q, 2 * it + q, xr[:, slot(par, q), :],
                               hr[:, slot(par, q), :]) for q in range(2)] + head)
                for q in range(2):
                    eng.wait_ge(edge.norm1.hidden, 2 * it + q + 1)
                    v.tensor_tensor(msg[:, q], hr[:, slot(par, q), :], wide(norm[:, cols(it, q)], F), ALU.mult
                                    ).then_inc(weighed, 1)
                wait_past(eng, t_spilled[par], 16 * k)
                for q in range(2):
                    eng.wait_ge(weighed, 2 * it + q + 1)
                    scan(0, it, par, q, lambda t: msg[:, q, t, :])
                node_tail(tail)

            v.memset(state[:, 4 * GROUP - 1, :], 0.0).then_inc(scanned, 1)
            each_iteration(eng, body1)

            def patch(stage):
                eng.wait_ge(carried, stage + 1)
                eng.wait_ge(patch_in, 16 * (stage + 1))
                v.tensor_tensor(patched[:, :], bank[:, 3, 0:F], patch_row[:, :], ALU.add
                                ).then_inc(patch_made, 1)

            patch(0)

            def body2(it, par, k):
                await_dense(1, par, k)
                head, tail = dense_items(1, it, par)
                norms_v(eng, head)
                for q in range(2):
                    eng.wait_ge(arma_out, 2 * it + q + 1)
                    z = bank[:, edge.product_bank[q], GROUP * F:2 * GROUP * F].rearrange("p (t f) -> p t f", f=F)
                    v.tensor_tensor(msg[:, q], z, wide(norm[:, cols(it, q)], F), ALU.mult
                                    ).then_inc(weighed, 1)
                eng.wait_ge(t_spilled[par], 16 * (turns(par) + k))
                for q in range(2):
                    eng.wait_ge(weighed, GROUPS + 2 * it + q + 1)
                    scan(1, it, par, q, lambda t: msg[:, q, t, :])
                node_tail(tail)

            each_iteration(eng, body2)
            patch(1)

            def body3(it, par, k):
                eng.wait_ge(xu_in[par], 32 * (k + 1))
                for q in range(2):
                    eng.wait_ge(gathered[2 * par + q], 16 * GROUP * (3 * turns(par) + k + 1))
                    v.tensor_tensor(edge.sq[:, q], ar[:, slot(par, q), :], ur[:, slot(par, q), :], ALU.add
                                    ).then_inc(summed, 1)
                for q in range(2):
                    eng.wait_ge(summed, 2 * it + q + 1)
                    v.scalar_tensor_tensor(out=edge.x1[:, q], in0=edge.sq[:, q], scalar=0.0,
                                           in1=xr[:, slot(par, q), :], op0=ALU.max, op1=ALU.add
                                           ).then_inc(edge.mid, 1)
                eng.wait_ge(edge.mid, 2 * it + 2)
                norms_v(eng, [(edge, edge.norm1, q, GROUPS + 2 * it + q, edge.x1[:, q], edge.h[:, q])
                              for q in range(2)])
                for q in range(2):
                    eng.wait_ge(edge.norm1.hidden, GROUPS + 2 * it + q + 1)
                    for t in range(GROUP):
                        v.tensor_tensor(spread[:, q, t],
                                        edge.h[:, q, t, None, :].to_broadcast([128, R, F]),
                                        mask[:, bass.ds(2 * GROUP * it + GROUP * q + t, 1), :]
                                        .rearrange("p a r -> p (a r)").unsqueeze(2).to_broadcast([128, R, F]),
                                        ALU.mult).then_inc(spread_done, 1)
                eng.wait_ge(t_spilled[par], 16 * (2 * turns(par) + k))
                for q in range(2):
                    eng.wait_ge(rel_out, GROUP * (2 * it + q + 1))
                    scan(2, it, par, q,
                         lambda t: bank[:, edge.product_bank[q], F * t:F * t + F])

            each_iteration(eng, body3)
            patch(2)

            def body4(it, par, k):
                eng.wait_ge(xu_in[par], 32 * turns(par) + 48 * (k + 1))
                for q in range(2):
                    wait_past(eng, scattered[2 * par + q], 16 * GROUP * k)
                xin = [xr[:, slot(par, q), :] for q in range(2)]
                norms_v(eng, [(edge, edge.norm1, q, 2 * GROUPS + 2 * it + q, xin[q], edge.h[:, q])
                              for q in range(2)])
                node_tail([(edge, q, 2 * it + q, xin[q], eout[:, slot(par, q), :],
                            (ur[:, slot(par, q), :], tr[:, slot(par, q), :])) for q in range(2)])

            each_iteration(eng, body4)


PREP_DIAG = 15
PREP_TAIL = 15 + 2 + 2 + 5 + 5 + 24
PREP_DEG = PREP_TAIL + 4
PREP_BACK = PREP_DEG + 6 + 24


_INS = ['x', 'src', 'dst', 'edge_type_8', 'edge_weight', 'L0_gnn_init_weight', 'L0_gnn_weight',
        'L0_gnn_root_weight', 'L0_gnn_bias', 'L0_gnn_bn_gamma', 'L0_gnn_bn_beta', 'L0_gnn_bn_mean',
        'L0_gnn_bn_var', 'L1_gnn_weight', 'L1_gnn_self_loop_w']


def kernel(**inputs):
    import numpy as _np
    import concourse.bacc as _bacc
    from concourse import mybir as _mybir
    from concourse.bass_utils import run_bass_kernel_spmd as _run

    nc = _bacc.Bacc("TRN2", target_bir_lowering=False, num_devices=1)
    arrays, args = {}, []
    for name in _INS:
        a = _np.ascontiguousarray(inputs[name])
        arrays[f"in_{name}"] = a
        args.append(nc.dram_tensor(f"in_{name}", a.shape, _mybir.dt.from_np(a.dtype), kind="ExternalInput").ap())
    shape = tuple(inputs['x'].shape)
    out = nc.dram_tensor("out_x", shape, _mybir.dt.float32, kind="ExternalOutput").ap()
    gnn_kernel(nc, *args, out)
    r = _run(nc, [arrays], core_ids=[0])
    return r.results[0]["out_x"]
```

```python
import concourse.bass as bass
from concourse import mybir
from contextlib import ExitStack


class Norm:

    def __init__(self, sb, sem, name, fp32, rows, tiles, stats, at):
        self.rows, self.tiles = rows, tiles
        self.xc = sb(name + "_xc", [128, 2, tiles, 64], fp32)
        self.sq = sb(name + "_sq", [128, 2, tiles, 64], fp32)
        self.sum = sb(name + "_sum", [128, 2, tiles], fp32)
        self.h = sb(name + "_h", [128, 2, tiles, 64], fp32)
        self.hT = sb(name + "_hT", [128, 2, tiles // 2, 128], fp32)
        self.var, self.inv = [[t[:, at + q * tiles:at + (q + 1) * tiles] for q in range(2)] for t in stats]
        self.total = sem(name + "_total")
        self.centred = sem(name + "_centred")
        self.squared = sem(name + "_squared")
        self.spread = sem(name + "_spread")
        self.hidden = sem(name + "_hidden")
        self.turned = sem(name + "_turned")
        self.taken = sem(name + "_taken")
        self.product = sem(name + "_product")
        self.added = sem(name + "_added")
        self.done = sem(name + "_done")


class Lane:

    def __init__(self, sb, sem, name, fp32, rows, tiles, stats, at, turn_banks, banks1, banks2):
        self.rows, self.tiles = rows, tiles
        self.norm1 = Norm(sb, sem, name + "_n1", fp32, rows, tiles, stats, at)
        self.norm2 = Norm(sb, sem, name + "_n2", fp32, rows, tiles, stats, at + 2 * tiles)
        self.x1 = sb(name + "_x1", [128, 4, tiles, 64], fp32)
        self.turn_banks = turn_banks
        self.norm1.banks, self.norm2.banks = banks1, banks2


def gnn_kernel(nc, x, src, dst, edge_type, edge_weight, init_weight, weight, root_weight, bias,
               bn_gamma, bn_beta, bn_mean, bn_var, rel_weight, self_loop, out):
    fp32, bf16, i32 = mybir.dt.float32, mybir.dt.bfloat16, mybir.dt.int32
    ALU = mybir.AluOpType
    ACT = mybir.ActivationFunctionType
    AX = mybir.AxisListType

    N, F = x.shape
    E = src.shape[0]
    R = rel_weight.shape[0]
    EPS = 1e-5
    COLS = 200
    EP = E // COLS
    GROUP = 4
    GROUPS = COLS // GROUP
    ITERS = GROUPS // 2
    PAIRS = ITERS // 2
    ROWS = 128 * COLS
    DT = 8
    DP = N // (DT * 2 * GROUPS)
    CHUNK = DT * DP
    NOWHERE = 131071
    assert EP * COLS == E and DP * DT * 2 * GROUPS == N and F == 64 and ITERS % 2 == 1

    ctx = ExitStack()
    with ctx:
        def sb(name, shape, dt):
            return ctx.enter_context(nc.sbuf_tensor(name, shape, dt))

        def sem(name):
            return ctx.enter_context(nc.semaphore(name))

        def dram(name, shape, dt=fp32):
            return nc.dram_tensor(name, shape, dt).ap()

        table = [dram(f"sum_table{k}", [ROWS + 1, F]) for k in range(3)]
        xs_dram = dram("x_of_src", [ROWS, F])
        xd_dram = dram("x_of_dst", [ROWS, F])
        hs_dram = dram("h_of_src", [ROWS, F])
        us_dram = dram("root_term_of_src", [ROWS, F])
        src_by_column = dram("src_by_column", [COLS, 128])

        def by_col(t):
            return t[0:ROWS, :].rearrange("(p j) f -> p j f", j=COLS)

        src_i = sb("src_i", [128, COLS], i32)
        dst_i = sb("dst_i", [128, COLS], i32)
        typ_i = sb("typ_i", [128, COLS], i32)
        ew = sb("ew", [128, COLS], fp32)
        next_i = sb("next_i", [128, 1], i32)
        src1 = sb("src1", [128, COLS], fp32)
        srcf = sb("srcf", [128, COLS], fp32)
        dstf = sb("dstf", [128, COLS], fp32)
        typf = sb("typf", [128, COLS], fp32)
        nextf = sb("nextf", [128, 1], fp32)
        same = sb("same", [128, COLS], fp32)
        final = sb("final", [128, COLS], fp32)
        deg = sb("deg", [128, COLS], fp32)
        eq = sb("eq", [128, COLS], fp32)
        tmp = sb("tmp", [128, COLS], fp32)
        root = sb("root", [128, COLS], fp32)
        dinv = sb("dinv", [128, COLS], fp32)
        norm = sb("norm", [128, COLS], fp32)
        dinv_src = sb("dinv_src", [128, COLS], fp32)
        place = sb("place", [128, COLS], fp32)
        block_base = sb("block_base", [128, COLS], fp32)
        look = sb("look", [128, 2 * COLS + 1], fp32)
        slot_i = sb("slot_i", [128, COLS], i32)
        dstx_i = sb("dstx_i", [128, COLS], i32)
        dsto_i = sb("dsto_i", [128, COLS], i32)
        patch_i = sb("patch_i", [128, 1], i32)
        patchf = sb("patchf", [128, 1], fp32)
        pair_mask = sb("pair_mask", [128, COLS, R // 2], fp32)
        half_mask = sb("half_mask", [128, COLS, 2], fp32)
        carry_in = sb("carry_in", [128, 128], fp32)
        carry_back = sb("carry_back", [128, 128], fp32)
        diag = sb("diag", [128, 2, 128], fp32)
        srcT = sb("srcT", [COLS // 2, 2, 128], fp32)

        ident = sb("ident", [128, 128], fp32)
        ones = sb("ones", [128, 128], fp32)
        before = sb("before", [128, 128], fp32)
        after = sb("after", [128, 128], fp32)
        count_i = sb("count_i", [128, COLS], i32)
        count1 = sb("count1", [128, COLS], fp32)
        base_i = sb("base_i", [128, 1], i32)
        basef = sb("basef", [128, 1], fp32)
        rel_i = sb("rel_i", [128, R], i32)
        relf = sb("relf", [128, R], fp32)
        eps = sb("eps", [128, 1], fp32)
        zrow = sb("zrow", [1, F], fp32)
        w_arma = sb("w_arma", [128, 128], fp32)
        b_arma = sb("b_arma", [128, 1], fp32)
        w_next = sb("w_next", [128, F], fp32)
        w_root = sb("w_root", [128, 128], fp32)
        w_rootk = sb("w_rootk", [128, 2, F], fp32)
        w_loop = sb("w_loop", [128, 128], fp32)
        w_loopT = sb("w_loopT", [128, 128], fp32)
        w_rel = sb("w_rel", [128, R // 4, 2 * F], fp32)
        bnv = sb("bnv", [128, 4, F], fp32)
        bvec = sb("bvec", [128, 2, F], fp32)
        bns = sb("bns", [128, F], fp32)
        bn_t = sb("bn_t", [128, F], fp32)
        bias_part = sb("bias_part", [128, 3, F], bf16)
        bias_rest = sb("bias_rest", [128, 3, F], fp32)
        bias_row = sb("bias_row", [3, DT, F], bf16)
        ones3 = sb("ones3", [3, 128], bf16)

        xr = sb("xr", [128, 4 * GROUP, F], fp32)
        hr = sb("hr", [128, 4 * GROUP, F], fp32)
        cat = sb("cat", [128, 4 * GROUP, 2 * F], fp32)
        ar = sb("ar", [128, 4 * GROUP, F], fp32)
        ur = sb("ur", [128, 4 * GROUP, F], fp32)
        tr = sb("tr", [128, 4 * GROUP, F], fp32)
        state = sb("state", [128, 4 * GROUP, F], fp32)
        idx = sb("idx", [128, 4, GROUP], i32)
        msg = sb("msg", [128, 2, GROUP, F], fp32)
        sbc = sb("sbc", [128, 4, GROUP * 128], fp32)
        past_first = sb("past_first", [128, 2, GROUP * 128], fp32)
        pick = sb("pick", [128, 2, GROUP * 128], fp32)
        found = sb("found", [128, 2, GROUP, COLS], fp32)
        mask = found.rearrange("p q t j -> p (q t j)").rearrange("p (j r) -> p j r", r=R)
        dropped = sb("dropped", [128, 2, GROUP, COLS], fp32)
        catT, reluT = past_first, pick
        spread = sb("spread", [128, 2, GROUP, R // 2, F], fp32)
        spreadT = sb("spreadT", [128, 2, 2, 4 * 128], fp32)
        halves = sb("halves", [128, GROUP, 2, F], fp32)
        patch_row = sb("patch_row", [128, F], fp32)
        patched = sb("patched", [128, F], fp32)
        dx = sb("dx", [128, 4, DT * F], fp32)
        dout = sb("dout", [128, 4, DT * F], fp32)
        eout = sb("eout", [128, 4 * GROUP, F], fp32)

        bank = ctx.enter_context(nc.psum_tensor("bank", [128, 8, 512], fp32))
        EDGE_STATS, DENSE_STATS = 4 * GROUP, 4 * DT
        STATS = EDGE_STATS + DENSE_STATS
        var = sb("var", [128, STATS], fp32)
        std = sb("std", [128, STATS], fp32)
        inv = sb("inv", [128, STATS], fp32)
        edge = Lane(sb, sem, "edge", fp32, 128, GROUP, (var, inv), 0, (0, 3), (1, 2), (4, 5))
        dense = Lane(sb, sem, "dense", fp32, DP, DT, (var, inv), EDGE_STATS, (3, 3), (4, 5), (6, 7))

        edges_in = sem("edges_in")
        weights_in = sem("weights_in")
        filled = sem("filled")
        const = sem("const")
        pool_chain = sem("pool_chain")
        pool_passed = sem("pool_passed")
        prep = sem("prep")
        shown = sem("shown")
        rooted = sem("rooted")
        src_out = sem("src_out")
        zero_out = sem("zero_out")
        ready0 = sem("ready0")
        ready1 = sem("ready1")
        weights_ok = sem("weights_ok")
        idx_set = sem("idx_set")
        gathered = [sem(f"gathered{s}") for s in range(4)]
        bc_in = [sem(f"bc_in{p}") for p in range(2)]
        below = sem("below")
        picked = sem("picked")
        looked = sem("looked")
        placed = sem("placed")
        matched = sem("matched")
        x_spilled = [sem(f"x_spilled{p}") for p in range(2)]
        h_spilled = [sem(f"h_spilled{p}") for p in range(2)]
        u_spilled = [sem(f"u_spilled{p}") for p in range(2)]
        t_spilled = [sem(f"t_spilled{p}") for p in range(2)]
        h_in = [sem(f"h_in{p}") for p in range(2)]
        xu_in = [sem(f"xu_in{p}") for p in range(2)]
        dense_in = [sem(f"dense_in{p}") for p in range(2)]
        dense_out = [sem(f"dense_out{p}") for p in range(2)]
        weighed = sem("weighed")
        scanned = sem("scanned")
        cat_turned = sem("cat_turned")
        cat_taken = sem("cat_taken")
        arma_done = sem("arma_done")
        rooted_all = sem("rooted_all")
        scaled_all = sem("scaled_all")
        halved = sem("halved")
        t2_in = [sem(f"t2_in{p}") for p in range(2)]
        arma_relu = sem("arma_relu")
        arma_out = sem("arma_out")
        root_taken = sem("root_taken")
        summed = sem("summed")
        x1_made = sem("x1_made")
        spread_done = sem("spread_done")
        spread_turned = sem("spread_turned")
        spread_taken = sem("spread_taken")
        rel_out = sem("rel_out")
        carried = sem("carried")
        patch_in = sem("patch_in")
        patch_made = sem("patch_made")
        patch_out = sem("patch_out")
        scattered = [sem(f"scattered{s}") for s in range(4)]

        block = ctx.enter_context(nc.Block())

        S3_TURN = ((0, 3), (4, 5))
        S3_OUT = ((1, 2), (6, 7))

        def turns(par):
            return PAIRS + 1 if par == 0 else PAIRS

        def each_iteration(eng, body):
            body(0, 0, 0)
            body(1, 1, 0)
            with eng.Fori(1, PAIRS) as k:
                body(2 * k, 0, k)
                body(2 * k + 1, 1, k)
            body(2 * PAIRS, 0, PAIRS)

        def overlapped(eng, body, depth):
            def at(i, k=None):
                body(i, i % 2, i // 2, [0 <= i - d < ITERS for d in range(depth)])
            for i in range(4):
                at(i)
            with eng.Fori(2, PAIRS) as k:
                body(2 * k, 0, k, [True] * depth)
                body(2 * k + 1, 1, k, [True] * depth)
            for i in range(2 * PAIRS, ITERS + depth - 1):
                at(i)

        def earlier(it, par, k, by):
            if by == 2:
                return it - 2, par, k - 1
            return it - 1, 1 - par, (k if par == 1 else k - 1)

        def wait_past(eng, s, value):
            if not (isinstance(value, int) and value <= 0):
                eng.wait_ge(s, value)

        def cols(it, q):
            return bass.ds(2 * GROUP * it + GROUP * q, GROUP)

        def slots(par):
            return slice(2 * GROUP * par, 2 * GROUP * par + 2 * GROUP)

        def slot(par, q):
            s = 2 * par + q
            return slice(GROUP * s, GROUP * s + GROUP)

        def wide(ap, n):
            return ap.unsqueeze(2).to_broadcast([ap.shape[0], ap.shape[1], n])

        def dense_rows(t, it):
            return t[bass.ds(2 * CHUNK * it, 2 * CHUNK), :].rearrange(
                "(c p t) f -> p c (t f)", c=2, t=DT)

        @block.sync
        def _(eng):
            eng.wait_ge(filled, 1)
            for a, b in ((src_i, src), (dst_i, dst), (typ_i, edge_type), (ew, edge_weight)):
                eng.dma_start(a[0:EP, :], b.rearrange("(p j) -> p j", j=COLS)).then_inc(edges_in, 16)
            with nc.allow_non_contiguous_dma(reason="one element per partition"):
                eng.dma_start(next_i[0:EP - 1, :], dst.rearrange("(p j) -> p j", j=COLS)[1:EP, 0:1]
                              ).then_inc(edges_in, 16)
            for k in range(2):
                h = slice(k * F, (k + 1) * F)
                eng.dma_start(w_arma[0:F, h], init_weight[k]).then_inc(weights_in, 16)
                eng.dma_start(w_arma[F:128, h], root_weight[0, k]).then_inc(weights_in, 16)
                eng.dma_start(w_rootk[0:F, k, :], root_weight[1, k]).then_inc(weights_in, 16)
                eng.dma_start(w_rootk[F:128, k, :], root_weight[1, k]).then_inc(weights_in, 16)
                eng.dma_start(w_loop[h, h], self_loop).then_inc(weights_in, 16)
                eng.dma_start(bvec[:, k, :], bias[1, k].to_broadcast([128, F])).then_inc(weights_in, 16)
            eng.dma_start(w_next[:, :], weight[0].rearrange("k f o -> (k f) o")).then_inc(weights_in, 16)
            eng.dma_start(b_arma[:, :], bias[0].rearrange("k a o -> (k o) a")).then_inc(weights_in, 16)
            for b in range(2):
                for c in range(R // 4):
                    eng.dma_start(w_rel[b * F:(b + 1) * F, c, :].rearrange("f (r o) -> f r o", r=2),
                                  rel_weight[4 * c + 2 * b:4 * c + 2 * b + 2].rearrange("r f o -> f r o")
                                  ).then_inc(weights_in, 16)
            for k, v in enumerate((bn_gamma, bn_beta, bn_mean, bn_var)):
                eng.dma_start(bnv[:, k, :], v.unsqueeze(0).to_broadcast([128, F])).then_inc(weights_in, 16)
            eng.wait_ge(const, 1)
            for k in range(3):
                eng.dma_start(table[k][ROWS:ROWS + 1, :], zrow[:, :]).then_inc(zero_out, 16)
            eng.wait_ge(ready0, 2)
            eng.dma_start(src_by_column.rearrange("(c j) p -> j c p", c=2), srcT[:, :, :]
                          ).then_inc(src_out, 16)
            eng.wait_ge(src_out, 16)

            def store(stage_base, it, par, k, ring, where, done):
                eng.dma_start(by_col(where)[:, bass.ds(2 * GROUP * it, 2 * GROUP), :],
                              ring[:, slots(par), :]).then_inc(done[par], 16)

            def load(it, par, ring, where, s):
                eng.dma_start(ring[:, slots(par), :],
                              by_col(where)[:, bass.ds(2 * GROUP * it, 2 * GROUP), :]).then_inc(s[par], 16)

            def spilling(load_part, *store_parts):
                def body(it, par, k, on):
                    if on[0]:
                        load_part(it, par, k)
                    for d, part in enumerate(store_parts):
                        if on[d + 1]:
                            part(*earlier(it, par, k, d + 1))
                overlapped(eng, body, 1 + len(store_parts))

            def gather_done(stage, par, k):
                for q in range(2):
                    eng.wait_ge(gathered[2 * par + q], 16 * GROUP * (stage * turns(par) + k + 1))

            def load0(it, par, k):
                wait_past(eng, picked, 2 * it - 2)
                eng.dma_start(sbc[:, 2 * par:2 * par + 2, :],
                              src_by_column[bass.ds(2 * GROUP * it, 2 * GROUP), :]
                              .rearrange("(g t) p -> g (t p)", g=2).unsqueeze(0)
                              .to_broadcast([128, 2, GROUP * 128])).then_inc(bc_in[par], 16)

            def store0(it, par, k):
                gather_done(0, par, k)
                store(0, it, par, k, xr, xd_dram, x_spilled)

            spilling(load0, store0)

            def load_dense(base, it, par, k):
                wait_past(eng, dense.norm1.done, base * 2 * ITERS + 2 * it - 2)
                eng.dma_start(dx[0:DP, 2 * par:2 * par + 2, :], dense_rows(x, base * ITERS + it)
                              ).then_inc(dense_in[par], 16)

            def store_dense(base, it, par, k):
                eng.wait_ge(dense.norm2.done, base * 2 * ITERS + 2 * it + 2)
                eng.dma_start(dense_rows(out, base * ITERS + it), dout[0:DP, 2 * par:2 * par + 2, :]
                              ).then_inc(dense_out[par], 16)

            def store1(it, par, k):
                gather_done(1, par, k)
                store(1, it, par, k, xr, xs_dram, x_spilled)
                eng.wait_ge(edge.norm1.hidden, 2 * it + 2)
                store(1, it, par, k, hr, hs_dram, h_spilled)

            def store_sums(stage, it, par, k):
                eng.wait_ge(scanned, stage * COLS + 2 * GROUP * it + 2 * GROUP + 1)
                store(stage, it, par, k, state, table[stage], t_spilled)

            def store1_late(it, par, k):
                store_sums(0, it, par, k)
                store_dense(0, it, par, k)

            spilling(lambda it, par, k: load_dense(0, it, par, k), store1, store1_late)

            for p in range(2):
                eng.wait_ge(h_spilled[p], 16 * turns(p))

            def load2(it, par, k):
                wait_past(eng, cat_turned, 2 * it - 2)
                eng.dma_start(cat[:, slots(par), F:2 * F],
                              by_col(hs_dram)[:, bass.ds(2 * GROUP * it, 2 * GROUP), :]).then_inc(h_in[par], 16)
                load_dense(1, it, par, k)

            def store2(it, par, k):
                eng.wait_ge(root_taken, 2 * it + 2)
                store(2, it, par, k, ur, us_dram, u_spilled)

            def store2_late(it, par, k):
                store_sums(1, it, par, k)
                store_dense(1, it, par, k)

            spilling(load2, store2, store2_late)

            for p in range(2):
                eng.wait_ge(u_spilled[p], 16 * turns(p))
                eng.wait_ge(x_spilled[p], 16 * 2 * turns(p))

            def load3(it, par, k):
                wait_past(eng, x1_made, 2 * it - 2)
                load(it, par, xr, xs_dram, xu_in)
                load(it, par, ur, us_dram, xu_in)

            spilling(load3, lambda it, par, k: None, lambda it, par, k: store_sums(2, it, par, k))

            eng.wait_ge(x1_made, GROUPS)
            eng.wait_ge(patch_out, 16 * 3)

            def load4(it, par, k):
                wait_past(eng, edge.norm1.done, 2 * it - 2)
                load(it, par, xr, xd_dram, xu_in)
                load(it, par, ur, table[1], xu_in)

            def load4_late(it, par, k):
                wait_past(eng, edge.norm2.done, 2 * it - 2)
                load(it, par, tr, table[2], t2_in)

            spilling(load4, load4_late)
            for p in range(2):
                eng.wait_ge(dense_out[p], 16 * 2 * turns(p))
                eng.wait_ge(t_spilled[p], 16 * 3 * turns(p))
            eng.wait_ge(zero_out, 16 * 3)

        @block.gpsimd
        def _(eng):
            eng.memset(zrow[:, :], 0.0).then_inc(const, 1)
            eng.memset(ones[:, :], 1.0).then_inc(pool_chain, 1)
            eng.memset(eps[:, :], EPS).then_inc(pool_chain, 1)
            eng.iota(count_i[:, :], pattern=[[1, COLS]], base=1, channel_multiplier=0).then_inc(pool_chain, 1)
            eng.iota(base_i[:, :], pattern=[[0, 1]], base=0, channel_multiplier=COLS).then_inc(pool_chain, 1)
            eng.iota(rel_i[:, :], pattern=[[1, R]], base=0, channel_multiplier=0).then_inc(pool_chain, 1)
            eng.wait_ge(pool_chain, 5)
            eng.affine_select(out=ident[:, :], in_=ones[:, :], compare_op=ALU.is_equal, fill=0.0, base=0,
                              pattern=[[-1, 128]], channel_multiplier=1).then_inc(const, 1)
            eng.affine_select(out=before[:, :], in_=ones[:, :], compare_op=ALU.is_gt, fill=0.0, base=0,
                              pattern=[[1, 128]], channel_multiplier=-1).then_inc(const, 1)
            eng.affine_select(out=after[:, :], in_=ones[:, :], compare_op=ALU.is_gt, fill=0.0, base=0,
                              pattern=[[-1, 128]], channel_multiplier=1).then_inc(const, 1)

            def await_count(s, value):
                wait_past(eng, s, value)
                eng.sem_inc(pool_passed, 1)

            def place_idx(stage, it, par, q, indices):
                eng.tensor_copy(idx[:, 2 * par + q, :], indices[:, cols(it, q)]).then_inc(idx_set, 1)
                await_count(idx_set, stage * GROUPS + 2 * it + q + 1)

            def gather(stage, it, par, q, indices, rows, ring):
                place_idx(stage, it, par, q, indices)
                for t in range(GROUP):
                    s = 2 * par + q
                    eng.indirect_dma_start(
                        out=ring[:, GROUP * s + t, 0:F], out_offset=None, in_=rows,
                        in_offset=bass.IndirectOffsetOnAxis(ap=idx[:, s, t:t + 1], axis=0),
                    ).then_inc(gathered[s], 16)

            eng.wait_ge(ready0, 1)

            def gather0(it, par, k):
                await_count(x_spilled[par], 16 * k)
                for q in range(2):
                    gather(0, it, par, q, dstx_i, x, xr)

            each_iteration(eng, gather0)

            def gather1(it, par, k):
                await_count(x_spilled[par], 16 * (turns(par) + k))
                for q in range(2):
                    await_count(edge.norm1.centred, 2 * it + q - 3)
                    gather(1, it, par, q, src_i, x, xr)

            each_iteration(eng, gather1)

            def patch(stage):
                for p in range(2):
                    eng.wait_ge(t_spilled[p], 16 * (stage + 1) * turns(p))
                eng.indirect_dma_start(
                    out=patch_row[:, :], out_offset=None, in_=table[stage][:, :],
                    in_offset=bass.IndirectOffsetOnAxis(ap=patch_i[:, 0:1], axis=0)).then_inc(patch_in, 16)
                eng.wait_ge(patch_made, stage + 1)
                eng.indirect_dma_start(
                    out=table[stage][:, :], out_offset=bass.IndirectOffsetOnAxis(ap=patch_i[:, 0:1], axis=0),
                    in_=patched[:, :], in_offset=None).then_inc(patch_out, 16)
                eng.wait_ge(patch_out, 16 * (stage + 1))

            patch(0)
            eng.wait_ge(zero_out, 16 * 3)

            def gather2(it, par, k):
                for q in range(2):
                    await_count(cat_turned, 2 * it + q - 3)
                    gather(2, it, par, q, slot_i, table[0][:, :], cat)

            each_iteration(eng, gather2)
            patch(1)

            def gather3(it, par, k):
                for q in range(2):
                    await_count(summed, 2 * it + q - 3)
                    gather(3, it, par, q, slot_i, table[1][:, :], ar)

            each_iteration(eng, gather3)
            patch(2)

            for p in range(2):
                eng.wait_ge(dense_out[p], 16 * 2 * turns(p))

            def scatter(it, par, k):
                for q in range(2):
                    s = 2 * par + q
                    await_count(scattered[s], 16 * GROUP * k)
                    place_idx(4, it, par, q, dsto_i)
                    await_count(edge.norm2.done, 2 * it + q + 1)
                    for t in range(GROUP):
                        eng.indirect_dma_start(
                            out=out, out_offset=bass.IndirectOffsetOnAxis(ap=idx[:, s, t:t + 1], axis=0),
                            in_=eout[:, GROUP * s + t, :], in_offset=None,
                            bounds_check=N - 1, oob_is_err=False).then_inc(scattered[s], 16)

            each_iteration(eng, scatter)
            for s in range(4):
                eng.wait_ge(scattered[s], 16 * GROUP * turns(s // 2))

        def act_square(eng, norm, q, n):
            eng.wait_ge(norm.centred, n + 1)
            eng.activation(norm.sq[0:norm.rows, q], norm.xc[0:norm.rows, q], ACT.Square
                           ).then_inc(norm.squared, 1)

        def act_roots(eng, norms, lo, hi):
            for norm, n in norms:
                eng.wait_ge(norm.spread, n + 2)
            eng.activation(std[:, lo:hi], var[:, lo:hi], ACT.Sqrt, bias=eps[:, :], scale=1.0 / F
                           ).then_inc(rooted_all, 1)

        def act_take(eng, lane, norm, q, n):
            eng.wait_ge(norm.turned, n + 1)
            pairs = lane.tiles // 2
            eng.activation(norm.hT[:, q, :, 0:lane.rows],
                           bank[:, lane.turn_banks[q], 0:128 * pairs]
                           .rearrange("p (a b) -> p a b", a=pairs)[:, :, 0:lane.rows],
                           ACT.Copy).then_inc(norm.taken, 1)

        @block.scalar
        def _(eng):
            eng.wait_ge(prep, PREP_DEG)
            eng.activation(root[:, :], tmp[:, :], ACT.Sqrt).then_inc(rooted, 1)
            eng.wait_ge(weights_in, 16 * 22)
            eng.wait_ge(pool_chain, 2)
            eng.activation(bn_t[:, :], bnv[:, 3, :], ACT.Sqrt, bias=eps[:, :]).then_inc(rooted, 1)

            def node_network(lane, n, on, more, extra, lo, hi):
                if on[0]:
                    for norm, m in extra:
                        for q in range(2):
                            act_square(eng, norm, q, m + q)
                    for q in range(2):
                        act_square(eng, lane.norm1, q, n + q)
                        more()
                if on[1]:
                    for q in range(2):
                        act_square(eng, lane.norm2, q, n - 2 + q)
                        if on[0]:
                            more()
                if on[0] or on[1]:
                    act_roots(eng, (extra + [(lane.norm1, n)] if on[0] else [])
                              + ([(lane.norm2, n - 2)] if on[1] else []), lo, hi)
                for norm, m, yes in ((lane.norm1, n, on[0]), (lane.norm2, n - 2, on[1])):
                    for q in range(2):
                        if yes:
                            act_take(eng, lane, norm, q, m + q)

            def body1(it, par, k, on):
                node_network(dense, 2 * it, on, lambda: None, [(edge.norm1, 2 * it)], 0, STATS)

            overlapped(eng, body1, 3)

            def body2(it, par, k, on):
                def turn_cat(q):
                    eng.wait_ge(cat_turned, 2 * it + q + 1)
                    eng.activation(catT[:, q, :], bank[:, 0, :], ACT.Copy).then_inc(cat_taken, 1)

                def relu_arma(q):
                    eng.wait_ge(arma_done, 2 * it + q + 1)
                    eng.activation(reluT[:, q, :], bank[:, 0, :], ACT.Relu, bias=b_arma[:, :]
                                   ).then_inc(arma_relu, 1)

                def take_root(q):
                    if q == 0:
                        wait_past(eng, u_spilled[par], 16 * k)
                    eng.wait_ge(arma_out, 2 * it + 2)
                    eng.activation(ur[:, slot(par, q), :],
                                   bank[:, 1, GROUP * F * q:GROUP * F * (q + 1)]
                                   .rearrange("p (t f) -> p t f", f=F), ACT.Copy).then_inc(root_taken, 1)

                todo = [lambda: turn_cat(0), lambda: relu_arma(0), lambda: turn_cat(1), lambda: relu_arma(1)]

                def more():
                    if todo:
                        todo.pop(0)()

                if on[0]:
                    more()
                if on[0] and not on[1]:
                    more()
                    more()
                node_network(dense, 2 * ITERS + 2 * it, on, more, [], EDGE_STATS, STATS)
                if on[0]:
                    for q in range(2):
                        take_root(q)

            overlapped(eng, body2, 3)

            def body3(it, par, k, on):
                if on[0]:
                    for q in range(2):
                        act_square(eng, edge.norm1, q, GROUPS + 2 * it + q)
                    act_roots(eng, [(edge.norm1, GROUPS + 2 * it)], 0, 2 * GROUP)
                if on[1]:
                    for q in range(2):
                        for half in range(2):
                            eng.wait_ge(spread_turned, 4 * (it - 1) + 2 * q + half + 1)
                            eng.activation(spreadT[:, q, half, :], bank[:, S3_TURN[q][half], :], ACT.Copy
                                           ).then_inc(spread_taken, 1)

            overlapped(eng, body3, 3)

            def body4(it, par, k, on):
                if on[0]:
                    for q in range(2):
                        act_square(eng, edge.norm1, q, 2 * GROUPS + 2 * it + q)
                if on[1]:
                    for q in range(2):
                        act_square(eng, edge.norm2, q, 2 * it - 2 + q)
                if on[0] or on[1]:
                    act_roots(eng, ([(edge.norm1, 2 * GROUPS + 2 * it)] if on[0] else [])
                              + ([(edge.norm2, 2 * it - 2)] if on[1] else []), 0, EDGE_STATS)
                for norm, m, yes in ((edge.norm1, 2 * it, on[0]), (edge.norm2, 2 * it - 2, on[1])):
                    for q in range(2):
                        if yes:
                            act_take(eng, edge, norm, q, m + q)

            overlapped(eng, body4, 3)

        def pe_layer(eng, lane, norm, q, n, hidden_n, w, with_bias):
            P = lane.rows
            pairs = lane.tiles // 2
            eng.wait_ge(norm.hidden, hidden_n + 1)
            for a in range(pairs):
                last = nc.tensor.transpose(bank[:, lane.turn_banks[q], 128 * a:128 * a + P],
                                           norm.h[0:P, q, 2 * a:2 * a + 2, :].rearrange("p t f -> p (t f)"),
                                           ident[0:P, 0:P])
            last.then_inc(norm.turned, 1)
            b = norm.banks[q]
            wait_past(eng, norm.done, n - 1)
            if with_bias:
                nc.tensor.matmul(bank[0:P, b, 0:lane.tiles * F], ones3[:, 0:P],
                                 bias_row[:, 0:lane.tiles, :].rearrange("p t f -> p (t f)"),
                                 start=True, stop=False)
            eng.wait_ge(norm.taken, n + 1)
            for a in range(pairs):
                last = nc.tensor.matmul(bank[0:P, b, 128 * a:128 * a + 128], norm.hT[:, q, a, 0:P], w[:, :],
                                        start=not with_bias, stop=(a == pairs - 1 or not with_bias))
            last.then_inc(norm.product, 1)

        def pe_network(eng, lane, n, hidden_n, on):
            for q in range(2):
                if on[0]:
                    pe_layer(eng, lane, lane.norm1, q, n + q, hidden_n + q, w_root, True)
            for q in range(2):
                if on[1]:
                    pe_layer(eng, lane, lane.norm2, q, n - 2 + q, n - 2 + q, w_loopT, False)

        @block.tensor
        def _(eng):
            eng.wait_ge(const, 4)
            eng.wait_ge(prep, PREP_DIAG)
            nc.tensor.matmul(bank[:, 0, 0:256], ones[:, :], diag[:, :, :].rearrange("p a b -> p (a b)"),
                             start=True, stop=True).then_inc(shown, 1)
            for c in range(2):
                nc.tensor.transpose(bank[0:COLS // 2, 4 + c, 0:128],
                                    srcf[:, c * (COLS // 2):(c + 1) * (COLS // 2)], ident[:, :]
                                    ).then_inc(shown, 1)
            eng.wait_ge(prep, PREP_TAIL)
            nc.tensor.matmul(bank[:, 1, 0:1], carry_in[:, :], deg[:, COLS - 1:COLS],
                             start=True, stop=True).then_inc(shown, 1)
            eng.wait_ge(prep, PREP_BACK)
            nc.tensor.matmul(bank[:, 2, 0:1], carry_back[:, :], dinv[:, 0:1],
                             start=True, stop=True).then_inc(shown, 1)
            eng.wait_ge(weights_in, 16 * 22)
            nc.tensor.transpose(bank[:, 3, 0:128], w_loop[:, :], ident[:, :]).then_inc(shown, 1)

            eng.wait_ge(ready0, 3)

            def body0(it, par, k):
                for q in range(2):
                    eng.wait_ge(picked, 2 * it + q + 1)
                    wait_past(eng, matched, 2 * it + q - 1)
                    for t in range(GROUP):
                        last = nc.tensor.matmul(bank[:, 4 * q + t, 0:2 * COLS + 1],
                                                pick[:, q, 128 * t:128 * t + 128], look[:, :],
                                                start=True, stop=True)
                    last.then_inc(looked, 1)

            each_iteration(eng, body0)
            eng.wait_ge(matched, GROUPS)
            eng.wait_ge(weights_ok, 2)

            def body1(it, par, k, on):
                pe_network(eng, dense, 2 * it, 2 * it, on)

            overlapped(eng, body1, 3)

            def carry(stage):
                eng.wait_ge(scanned, (stage + 1) * COLS + 1)
                last_slot = GROUP * 2 - 1
                nc.tensor.matmul(bank[:, 0, 0:F], carry_in[:, :], state[:, last_slot, :],
                                 start=True, stop=True).then_inc(carried, 1)

            carry(0)
            eng.wait_ge(patch_made, 1)

            def body2(it, par, k, on):
                for q in range(2):
                    if not on[0]:
                        continue
                    s = 2 * par + q
                    eng.wait_ge(h_in[par], 16 * (k + 1))
                    eng.wait_ge(gathered[s], 16 * GROUP * (2 * turns(par) + k + 1))
                    wait_past(eng, arma_relu, 2 * it + q)
                    for t in range(GROUP):
                        last = nc.tensor.transpose(bank[:, 0, 128 * t:128 * t + 128],
                                                   cat[:, GROUP * s + t, :], ident[:, :])
                    last.then_inc(cat_turned, 1)
                    wait_past(eng, root_taken, 2 * it)
                    nc.tensor.matmul(bank[:, 1, GROUP * F * q:GROUP * F * (q + 1)], ones3[:, :],
                                     bias_row[:, 0:GROUP, :].rearrange("p t f -> p (t f)"),
                                     start=True, stop=False)
                    eng.wait_ge(cat_taken, 2 * it + q + 1)
                    nc.tensor.matmul(bank[:, 0, :], w_arma[:, :], catT[:, q, :],
                                     start=True, stop=True).then_inc(arma_done, 1)
                    for t in range(GROUP):
                        at = F * (GROUP * q + t)
                        nc.tensor.matmul(bank[:, 1, at:at + F], catT[:, q, 128 * t:128 * t + 128],
                                         w_root[:, F:128], start=False, stop=(t == GROUP - 1))
                for q in range(2):
                    if not on[0]:
                        continue
                    eng.wait_ge(weighed, GROUPS + 2 * it)
                    eng.wait_ge(arma_relu, 2 * it + q + 1)
                    for t in range(GROUP):
                        at = F * (GROUP * q + t)
                        last = nc.tensor.matmul(bank[:, 2, at:at + F],
                                                reluT[:, q, 128 * t:128 * t + 128], w_next[:, :],
                                                start=True, stop=True)
                    last.then_inc(arma_out, 1)
                pe_network(eng, dense, 2 * ITERS + 2 * it, 2 * ITERS + 2 * it, on)

            overlapped(eng, body2, 3)
            carry(1)
            eng.wait_ge(patch_made, 2)

            def body3(it, par, k, on):
                if not on[1]:
                    return
                it, par, k = earlier(it, par, k, 1)
                for q in range(2):
                    eng.wait_ge(spread_done, 2 * it + q + 1)
                    for half in range(2):
                        b = S3_TURN[q][half]
                        wait_past(eng, spread_taken, 4 * it + 2 * q + half - 3)
                        for i in range(4):
                            t, c = 2 * half + i // 2, i % 2
                            last = nc.tensor.transpose(
                                bank[:, b, 128 * i:128 * i + 128],
                                spread[:, q, t, 2 * c:2 * c + 2, :].rearrange("p r f -> p (r f)"), ident[:, :])
                        last.then_inc(spread_turned, 1)
                for q in range(2):
                    wait_past(eng, halved, 2 * it + q - 3)
                    for half in range(2):
                        eng.wait_ge(spread_taken, 4 * it + 2 * q + half + 1)
                        for i in range(4):
                            t, c = 2 * half + i // 2, i % 2
                            last = nc.tensor.matmul(bank[:, S3_OUT[par][q], 128 * t:128 * t + 128],
                                                    spreadT[:, q, half, 128 * i:128 * i + 128], w_rel[:, c, :],
                                                    start=(c == 0), stop=(c == 1))
                    last.then_inc(rel_out, 1)

            overlapped(eng, body3, 3)
            carry(2)
            eng.wait_ge(patch_made, 3)

            def body4(it, par, k, on):
                pe_network(eng, edge, 2 * it, 2 * GROUPS + 2 * it, on)

            overlapped(eng, body4, 3)

        def tiles_of(ap):
            return ap.rearrange("p (t f) -> p t f", f=F)

        def product_of(norm, q):
            return tiles_of(bank[0:norm.rows, norm.banks[q], 0:norm.tiles * F])

        def ln_centre(eng, items, between):
            for norm, q, n, xin in items:
                nc.vector.tensor_reduce(norm.sum[0:norm.rows, q], xin, AX.X, ALU.add).then_inc(norm.total, 1)
                between()
            for norm, q, n, xin in items:
                eng.wait_ge(norm.total, n + 1)
                nc.vector.scalar_tensor_tensor(out=norm.xc[0:norm.rows, q],
                                               in0=wide(norm.sum[0:norm.rows, q], F), scalar=-1.0 / F,
                                               in1=xin, op0=ALU.mult, op1=ALU.add).then_inc(norm.centred, 1)
                between()

        def ln_spread(eng, items, between):
            for norm, q, n, xin in items:
                eng.wait_ge(norm.squared, n + 1)
                nc.vector.tensor_reduce(norm.var[q][0:norm.rows], norm.sq[0:norm.rows, q], AX.X, ALU.add
                                        ).then_inc(norm.spread, 1)
                between()

        def ln_scale(eng, count, lo, hi):
            eng.wait_ge(rooted_all, count + 1)
            nc.vector.reciprocal(inv[:, lo:hi], std[:, lo:hi]).then_inc(scaled_all, 1)

        def ln_hidden(eng, items, count, out_of, between):
            eng.wait_ge(scaled_all, count + 1)
            for norm, q, n, xin in items:
                nc.vector.scalar_tensor_tensor(out=out_of(norm, q), in0=norm.xc[0:norm.rows, q], scalar=0.0,
                                               in1=wide(norm.inv[q][0:norm.rows], F), op0=ALU.max,
                                               op1=ALU.mult).then_inc(norm.hidden, 1)
                between()

        def own_h(norm, q):
            return norm.h[0:norm.rows, q]

        def add_relu(eng, norm, q, n, xin, res, sums):
            got = product_of(norm, q)
            eng.wait_ge(norm.product, n + 1)
            if sums is not None:
                with_sums = cat[:, GROUP * q:GROUP * q + GROUP, 0:F] if norm is edge.norm1 else \
                    cat[:, GROUP * q:GROUP * q + GROUP, F:2 * F]
                nc.vector.tensor_tensor(with_sums, got, sums, ALU.add).then_inc(norm.added, 1)
                got = with_sums
                eng.wait_ge(norm.added, n + 1)
            nc.vector.scalar_tensor_tensor(out=res, in0=got, scalar=0.0, in1=xin,
                                           op0=ALU.max, op1=ALU.add).then_inc(norm.done, 1)

        @block.vector
        def _(eng):
            v = nc.vector
            steps = [0]

            def link(ins):
                steps[0] += 1
                ins.then_inc(prep, 1)
                eng.wait_ge(prep, steps[0])

            link(v.memset(src_i[:, :], 0))
            link(v.memset(typ_i[:, :], 0))
            link(v.memset(ew[:, :], 0.0))
            link(v.memset(next_i[:, :], NOWHERE))
            link(v.memset(w_loop[:, :], 0.0))
            v.memset(dst_i[:, :], NOWHERE).then_inc(filled, 1)
            link(v.memset(w_root[:, :], 0.0))
            eng.wait_ge(edges_in, 16 * 5)
            eng.wait_ge(const, 4)
            for a, b in ((srcf, src_i), (dstf, dst_i), (typf, typ_i), (nextf, next_i), (count1, count_i),
                         (basef, base_i), (relf, rel_i)):
                link(v.tensor_copy(a[:, :], b[:, :]))
            first, last = dstf[:, 0:1], dstf[:, COLS - 1:COLS]
            link(v.tensor_scalar(diag[:, 0, :], ident[:, :], first, None, ALU.mult))
            link(v.tensor_scalar(diag[:, 1, :], ident[:, :], last, None, ALU.mult))
            assert steps[0] == PREP_DIAG
            link(v.tensor_scalar(tmp[:, :], dstf[:, :], float(N - 1), None, ALU.min))
            link(v.tensor_copy(dstx_i[:, :], tmp[:, :]))
            v.tensor_scalar(src1[:, :], srcf[:, :], 1.0, None, ALU.add).then_inc(ready0, 1)
            eng.wait_ge(shown, 3)
            for c in range(2):
                link(v.tensor_copy(srcT[:, c, :], bank[0:COLS // 2, 4 + c, 0:128]))
            v.tensor_scalar(tmp[:, :], dstf[:, :], first, None, ALU.is_equal).then_inc(ready0, 1)
            eng.wait_ge(ready0, 2)
            link(v.tensor_reduce(patchf[:, :], tmp[:, :], AX.X, ALU.add))
            link(v.scalar_tensor_tensor(out=patchf[:, :], in0=patchf[:, :], scalar=-1.0, in1=basef[:, :],
                                        op0=ALU.add, op1=ALU.add))
            link(v.tensor_copy(patch_i[:, :], patchf[:, :]))
            link(v.scalar_tensor_tensor(out=carry_in[:, :], in0=bank[:, 0, 0:128], scalar=last,
                                        in1=before[:, :], op0=ALU.is_equal, op1=ALU.mult))
            link(v.scalar_tensor_tensor(out=carry_back[:, :], in0=bank[:, 0, 128:256], scalar=first,
                                        in1=after[:, :], op0=ALU.is_equal, op1=ALU.mult))
            link(v.memset(same[:, 0:1], 0.0))
            link(v.tensor_tensor(same[:, 1:COLS], dstf[:, 1:COLS], dstf[:, 0:COLS - 1], ALU.is_equal))
            link(v.tensor_tensor(final[:, 0:COLS - 1], dstf[:, 0:COLS - 1], dstf[:, 1:COLS], ALU.not_equal))
            link(v.tensor_tensor(final[:, COLS - 1:COLS], last, nextf[:, :], ALU.not_equal))
            link(v.tensor_copy(deg[:, :], ew[:, :]))
            k = 1
            while k < COLS:
                link(v.tensor_tensor(eq[:, k:COLS], dstf[:, k:COLS], dstf[:, 0:COLS - k], ALU.is_equal))
                link(v.tensor_tensor(tmp[:, k:COLS], eq[:, k:COLS], deg[:, 0:COLS - k], ALU.mult))
                link(v.tensor_tensor(deg[:, k:COLS], deg[:, k:COLS], tmp[:, k:COLS], ALU.add))
                k *= 2
            assert steps[0] == PREP_TAIL, steps
            link(v.tensor_scalar(eq[:, :], dstf[:, :], first, None, ALU.is_equal))
            eng.wait_ge(shown, 4)
            link(v.tensor_copy(patchf[:, :], bank[:, 1, 0:1]))
            link(v.scalar_tensor_tensor(out=deg[:, :], in0=eq[:, :], scalar=patchf[:, :], in1=deg[:, :],
                                        op0=ALU.mult, op1=ALU.add))
            link(v.tensor_scalar(tmp[:, :], deg[:, :], 1e-12, None, ALU.max))
            assert steps[0] == PREP_DEG, steps
            link(v.tensor_scalar(eq[:, :], deg[:, :], 0.0, None, ALU.is_gt))
            eng.wait_ge(rooted, 1)
            link(v.reciprocal(dinv[:, :], root[:, :]))
            link(v.tensor_tensor(dinv[:, :], dinv[:, :], eq[:, :], ALU.mult))
            link(v.tensor_tensor(dinv[:, :], dinv[:, :], final[:, :], ALU.mult))
            link(v.scalar_tensor_tensor(out=look[:, 0:COLS], in0=dstf[:, :], scalar=1.0, in1=final[:, :],
                                        op0=ALU.add, op1=ALU.mult))
            link(v.tensor_copy(look[:, COLS:2 * COLS], dinv[:, :]))
            v.tensor_copy(look[:, 2 * COLS:2 * COLS + 1], basef[:, :]).then_inc(ready0, 1)
            k = 1
            while k < COLS:
                link(v.tensor_tensor(eq[:, 0:COLS - k], dstf[:, k:COLS], dstf[:, 0:COLS - k], ALU.is_equal))
                link(v.tensor_tensor(tmp[:, 0:COLS - k], eq[:, 0:COLS - k], dinv[:, k:COLS], ALU.mult))
                link(v.tensor_tensor(dinv[:, 0:COLS - k], dinv[:, 0:COLS - k], tmp[:, 0:COLS - k], ALU.add))
                k *= 2
            assert steps[0] == PREP_BACK, steps
            link(v.tensor_scalar(eq[:, :], dstf[:, :], last, None, ALU.is_equal))
            eng.wait_ge(shown, 5)
            link(v.tensor_copy(patchf[:, :], bank[:, 2, 0:1]))
            link(v.scalar_tensor_tensor(out=dinv[:, :], in0=eq[:, :], scalar=patchf[:, :], in1=dinv[:, :],
                                        op0=ALU.mult, op1=ALU.add))
            link(v.tensor_tensor(norm[:, :], dinv[:, :], ew[:, :], ALU.mult))
            link(v.scalar_tensor_tensor(out=tmp[:, :], in0=dstf[:, :], scalar=float(-NOWHERE), in1=final[:, :],
                                        op0=ALU.add, op1=ALU.mult))
            link(v.tensor_scalar(dsto_i[:, :], tmp[:, :], float(NOWHERE), None, ALU.add))
            link(v.tensor_tensor(mask[:, :, :], wide(typf[:, :], R),
                                 relf[:, None, :].to_broadcast([128, COLS, R]), ALU.is_equal))
            link(v.tensor_reduce(pair_mask[:, :, :], mask[:, :, :].rearrange("p j (b r) -> p j b r", r=2),
                                 AX.X, ALU.add))
            link(v.tensor_reduce(half_mask[:, :, :], mask[:, :, :].rearrange("p j (b r) -> p j r b", r=2),
                                 AX.X, ALU.add))
            link(v.memset(state[:, :, :], 0.0))
            link(v.memset(var[:, :], 1.0))

            eng.wait_ge(weights_in, 16 * 22)
            eng.wait_ge(rooted, 2)
            link(v.reciprocal(bns[:, :], bn_t[:, :]))
            link(v.tensor_tensor(bns[:, :], bns[:, :], bnv[:, 0, :], ALU.mult))
            link(v.scalar_tensor_tensor(out=w_next[:, :], in0=w_next[:, :], scalar=0.5, in1=bns[:, :],
                                        op0=ALU.mult, op1=ALU.mult))
            link(v.tensor_tensor(w_rootk[:, 0, :], w_rootk[:, 0, :], w_rootk[:, 1, :], ALU.add))
            for c in range(2):
                h = slice(c * F, (c + 1) * F)
                link(v.scalar_tensor_tensor(out=w_root[h, h], in0=w_rootk[h, 0, :], scalar=0.5, in1=bns[h, :],
                                            op0=ALU.mult, op1=ALU.mult))
            link(v.tensor_tensor(bn_t[:, :], bvec[:, 0, :], bvec[:, 1, :], ALU.add))
            link(v.scalar_tensor_tensor(out=bn_t[:, :], in0=bn_t[:, :], scalar=0.5, in1=bnv[:, 2, :],
                                        op0=ALU.mult, op1=ALU.subtract))
            link(v.tensor_tensor(bn_t[:, :], bn_t[:, :], bns[:, :], ALU.mult))
            link(v.tensor_tensor(bias_rest[:, 0, :], bn_t[:, :], bnv[:, 1, :], ALU.add))
            for c in range(3):
                link(v.tensor_copy(bias_part[:, c, :], bias_rest[:, c, :]))
                if c < 2:
                    link(v.tensor_tensor(bias_rest[:, c + 1, :], bias_rest[:, c, :], bias_part[:, c, :],
                                         ALU.subtract))
            link(v.tensor_scalar(bn_t[:, :], bias_part[:, 0, :], ident[:, 0:1], None, ALU.mult))
            for c in range(1, 3):
                link(v.scalar_tensor_tensor(out=bn_t[:, :], in0=bias_part[:, c, :], scalar=ident[:, c:c + 1],
                                            in1=bn_t[:, :], op0=ALU.mult, op1=ALU.add))
            link(v.tensor_copy(bias_row[:, :, :], bn_t[0:3, None, :].to_broadcast([3, DT, F])))
            link(v.tensor_copy(ones3[:, :], ones[0:3, :]))
            eng.wait_ge(shown, 6)
            v.tensor_copy(w_loopT[:, :], bank[:, 3, 0:128]).then_inc(weights_ok, 1)

            def body0(it, par, k, on):
                if on[0]:
                    eng.wait_ge(bc_in[par], 16 * (k + 1))
                    for q in range(2):
                        wait_past(eng, looked, 2 * it + q - 1)
                        v.tensor_scalar(past_first[:, q, :], sbc[:, 2 * par + q, :], first, None, ALU.is_ge
                                        ).then_inc(below, 1)
                    for q in range(2):
                        eng.wait_ge(below, 2 * it + q + 1)
                        v.scalar_tensor_tensor(out=pick[:, q, :], in0=sbc[:, 2 * par + q, :],
                                               scalar=nextf[:, :], in1=past_first[:, q, :],
                                               op0=ALU.is_lt, op1=ALU.mult).then_inc(picked, 1)
                if not on[1]:
                    return
                it, par, k = earlier(it, par, k, 1)
                for q in range(2):
                    eng.wait_ge(looked, 2 * it + q + 1)
                    wait_past(eng, matched, 2 * it + q - 1)
                    for t in range(GROUP):
                        j = bass.ds(2 * GROUP * it + GROUP * q + t, 1)
                        v.scalar_tensor_tensor(out=found[:, q, t, :], in0=bank[:, 4 * q + t, 0:COLS],
                                               scalar=src1[:, j], in1=count1[:, :], op0=ALU.is_equal,
                                               op1=ALU.mult, accum_out=place[:, j]).then_inc(placed, 1)
                    for t in range(GROUP):
                        j = bass.ds(2 * GROUP * it + GROUP * q + t, 1)
                        eng.wait_ge(placed, 2 * GROUP * it + GROUP * q + t + 1)
                        v.scalar_tensor_tensor(out=dropped[:, q, t, :], in0=found[:, q, t, :], scalar=0.0,
                                               in1=bank[:, 4 * q + t, COLS:2 * COLS], op0=ALU.is_gt,
                                               op1=ALU.mult, accum_out=dinv_src[:, j])
                    v.tensor_copy(block_base[:, cols(it, q)], bank[:, 4 * q:4 * q + 4, 2 * COLS]
                                  ).then_inc(matched, 1)

            overlapped(eng, body0, 2)
            eng.wait_ge(matched, GROUPS)
            link(v.tensor_tensor(norm[:, :], norm[:, :], dinv_src[:, :], ALU.mult))
            link(v.tensor_scalar(eq[:, :], place[:, :], 0.0, None, ALU.is_gt))
            link(v.tensor_tensor(tmp[:, :], block_base[:, :], place[:, :], ALU.add))
            link(v.scalar_tensor_tensor(out=tmp[:, :], in0=tmp[:, :], scalar=float(-1 - ROWS), in1=eq[:, :],
                                        op0=ALU.add, op1=ALU.mult))
            v.tensor_scalar(slot_i[:, :], tmp[:, :], float(ROWS), None, ALU.add).then_inc(weights_ok, 1)

            def scan_steps(stage, it, par, k):
                count = [0]

                def step():
                    i = count[0]
                    if i == 2 * GROUP:
                        return
                    count[0] += 1
                    at = 2 * GROUP * par + i
                    j = 2 * GROUP * it + i
                    if i == 0:
                        wait_past(eng, t_spilled[par], 16 * (stage * turns(par) + k))
                    eng.wait_ge(scanned, stage * COLS + j + 1)
                    v.scalar_tensor_tensor(out=state[:, at, :], in0=state[:, (at - 1) % (4 * GROUP), :],
                                           scalar=same[:, bass.ds(j, 1)], in1=msg[:, i // GROUP, i % GROUP, :],
                                           op0=ALU.mult, op1=ALU.add).then_inc(scanned, 1)
                return step

            def finish(step):
                for _ in range(2 * GROUP):
                    step()

            def nothing():
                pass

            def dense_x(par, q):
                return tiles_of(dx[0:DP, 2 * par + q, :])

            def dense_stage(base, it, par, k, on, extra, count, lo, out_of, between):
                n = base * 2 * ITERS + 2 * it
                items1, items2 = [], []
                if on[0]:
                    eng.wait_ge(dense_in[par], 16 * (base * turns(par) + k + 1))
                    items1 = extra + [(dense.norm1, q, n + q, dense_x(par, q)) for q in range(2)]
                    ln_centre(eng, items1, between)
                if on[1]:
                    for q in range(2):
                        add_relu(eng, dense.norm1, q, n - 2 + q, dense_x(1 - par, q),
                                 dense.x1[0:DP, 2 * (1 - par) + q], None)
                        between()
                    eng.wait_ge(dense.norm1.done, n)
                    items2 = [(dense.norm2, q, n - 2 + q, dense.x1[0:DP, 2 * (1 - par) + q]) for q in range(2)]
                    ln_centre(eng, items2, between)
                if on[2]:
                    wait_past(eng, dense_out[par], 16 * (base * turns(par) + k - 1))
                    for q in range(2):
                        add_relu(eng, dense.norm2, q, n - 4 + q, dense.x1[0:DP, 2 * par + q],
                                 tiles_of(dout[0:DP, 2 * par + q, :]), None)
                        between()
                ln_spread(eng, items1 + items2, between)
                if on[0] or on[1]:
                    ln_scale(eng, count, lo, STATS)
                    between()
                    ln_hidden(eng, [i for i in items1 + items2 if i[0].rows == DP]
                              + [i for i in items1 if i[0].rows != DP], count, out_of, between)

            def body1(it, par, k, on):
                step = scan_steps(0, *earlier(it, par, k, 1)) if on[1] else nothing
                extra = []
                if on[0]:
                    wait_past(eng, h_spilled[par], 16 * k)
                    for q in range(2):
                        eng.wait_ge(gathered[2 * par + q], 16 * GROUP * (turns(par) + k + 1))
                    extra = [(edge.norm1, q, 2 * it + q, xr[:, slot(par, q), :]) for q in range(2)]
                if on[1]:
                    eng.wait_ge(weighed, 2 * it)
                dense_stage(0, it, par, k, on, extra, it, 0,
                            lambda norm, q: hr[:, slot(par, q), :] if norm is edge.norm1 else own_h(norm, q),
                            step)
                if on[1]:
                    finish(step)
                if on[0]:
                    wait_past(eng, scanned, 2 * GROUP * it + 1)
                    for q in range(2):
                        eng.wait_ge(edge.norm1.hidden, 2 * it + q + 1)
                        v.tensor_tensor(msg[:, q], hr[:, slot(par, q), :], wide(norm[:, cols(it, q)], F),
                                        ALU.mult).then_inc(weighed, 1)

            v.memset(state[:, 4 * GROUP - 1, :], 0.0).then_inc(scanned, 1)
            overlapped(eng, body1, 3)
            BODIES = ITERS + 1

            def patch(stage):
                eng.wait_ge(carried, stage + 1)
                eng.wait_ge(patch_in, 16 * (stage + 1))
                v.tensor_tensor(patched[:, :], bank[:, 0, 0:F], patch_row[:, :], ALU.add
                                ).then_inc(patch_made, 1)

            patch(0)

            def body2(it, par, k, on):
                step = nothing
                if on[1]:
                    step = scan_steps(1, *earlier(it, par, k, 1))
                    eng.wait_ge(scanned, COLS + 2 * GROUP * it - 2 * GROUP + 1)
                    for q in range(2):
                        eng.wait_ge(arma_out, 2 * it)
                        z = tiles_of(bank[:, 2, GROUP * F * q:GROUP * F * (q + 1)])
                        v.tensor_tensor(msg[:, q], z, wide(norm[:, cols(it - 1, q)], F), ALU.mult
                                        ).then_inc(weighed, 1)
                    eng.wait_ge(weighed, GROUPS + 2 * it)
                dense_stage(1, it, par, k, on, [], BODIES + it, EDGE_STATS, own_h, step)
                if on[1]:
                    finish(step)

            overlapped(eng, body2, 3)
            patch(1)

            def body3(it, par, k, on):
                step = scan_steps(2, *earlier(it, par, k, 2)) if on[2] else nothing
                if on[2]:
                    eng.wait_ge(scanned, 2 * COLS + 2 * GROUP * it - 4 * GROUP + 1)
                    for q in range(2):
                        n = 2 * it - 4 + q
                        eng.wait_ge(rel_out, n + 1)
                        v.tensor_tensor(halves[:, :, :, :],
                                        bank[:, S3_OUT[par][q], :].rearrange("p (t r f) -> p t r f", t=GROUP, r=2),
                                        half_mask[:, cols(it - 2, q), :].unsqueeze(3)
                                        .to_broadcast([128, GROUP, 2, F]), ALU.mult).then_inc(halved, 1)
                        eng.wait_ge(halved, n + 1)
                        v.tensor_tensor(msg[:, q], halves[:, :, 0, :], halves[:, :, 1, :], ALU.add
                                        ).then_inc(weighed, 1)
                        eng.wait_ge(weighed, 2 * GROUPS + n + 1)
                items = []
                if on[0]:
                    eng.wait_ge(xu_in[par], 32 * (k + 1))
                    for q in range(2):
                        eng.wait_ge(gathered[2 * par + q], 16 * GROUP * (3 * turns(par) + k + 1))
                        v.tensor_tensor(edge.norm2.sq[:, q], ar[:, slot(par, q), :], ur[:, slot(par, q), :],
                                        ALU.add).then_inc(summed, 1)
                        step()
                    for q in range(2):
                        eng.wait_ge(summed, 2 * it + q + 1)
                        v.scalar_tensor_tensor(out=edge.x1[:, q], in0=edge.norm2.sq[:, q], scalar=0.0,
                                               in1=xr[:, slot(par, q), :], op0=ALU.max, op1=ALU.add
                                               ).then_inc(x1_made, 1)
                        step()
                    eng.wait_ge(x1_made, 2 * it + 2)
                    items = [(edge.norm1, q, GROUPS + 2 * it + q, edge.x1[:, q]) for q in range(2)]
                    ln_centre(eng, items, step)

                def typed(q):
                    v.tensor_tensor(spread[:, q],
                                    edge.norm1.h[:, q, :, None, :].to_broadcast([128, GROUP, R // 2, F]),
                                    pair_mask[:, cols(it - 1, q), :].unsqueeze(3)
                                    .to_broadcast([128, GROUP, R // 2, F]), ALU.mult).then_inc(spread_done, 1)

                if on[1]:
                    wait_past(eng, spread_turned, 4 * it - 4)
                    typed(0)
                    step()
                ln_spread(eng, items, step)
                if on[1]:
                    typed(1)
                    step()
                if on[0]:
                    if on[1]:
                        eng.wait_ge(spread_done, 2 * it)
                    ln_scale(eng, 2 * BODIES + it, 0, 2 * GROUP)
                    ln_hidden(eng, items, 2 * BODIES + it, own_h, step)
                    eng.wait_ge(edge.norm1.hidden, GROUPS + 2 * it + 2)
                if on[2]:
                    finish(step)

            overlapped(eng, body3, 3)
            patch(2)

            def body4(it, par, k, on):
                n = 2 * it
                items1, items2 = [], []
                if on[0]:
                    eng.wait_ge(xu_in[par], 32 * turns(par) + 32 * (k + 1))
                    items1 = [(edge.norm1, q, 2 * GROUPS + n + q, xr[:, slot(par, q), :]) for q in range(2)]
                    ln_centre(eng, items1, nothing)
                if on[1]:
                    for q in range(2):
                        add_relu(eng, edge.norm1, q, n - 2 + q, xr[:, slot(1 - par, q), :],
                                 edge.x1[:, 2 * (1 - par) + q],
                                 ur[:, slot(1 - par, q), :])
                    eng.wait_ge(edge.norm1.done, n)
                    items2 = [(edge.norm2, q, n - 2 + q, edge.x1[:, 2 * (1 - par) + q]) for q in range(2)]
                    ln_centre(eng, items2, nothing)
                if on[2]:
                    eng.wait_ge(t2_in[par], 16 * k)
                    for q in range(2):
                        s = 2 * par + q
                        wait_past(eng, scattered[s], 16 * GROUP * (k - 1))
                        add_relu(eng, edge.norm2, q, n - 4 + q, edge.x1[:, 2 * par + q], eout[:, slot(par, q), :],
                                 tr[:, slot(par, q), :])
                ln_spread(eng, items1 + items2, nothing)
                if on[0] or on[1]:
                    count = 2 * BODIES + ITERS + it
                    ln_scale(eng, count, 0, EDGE_STATS)
                    ln_hidden(eng, items1 + items2, count, own_h, nothing)

            overlapped(eng, body4, 3)


PREP_DIAG = 15
PREP_TAIL = 15 + 2 + 2 + 5 + 5 + 24
PREP_DEG = PREP_TAIL + 4
PREP_BACK = PREP_DEG + 6 + 24


_INS = ['x', 'src', 'dst', 'edge_type_8', 'edge_weight', 'L0_gnn_init_weight', 'L0_gnn_weight',
        'L0_gnn_root_weight', 'L0_gnn_bias', 'L0_gnn_bn_gamma', 'L0_gnn_bn_beta', 'L0_gnn_bn_mean',
        'L0_gnn_bn_var', 'L1_gnn_weight', 'L1_gnn_self_loop_w']


def kernel(**inputs):
    import numpy as _np
    import concourse.bacc as _bacc
    from concourse import mybir as _mybir
    from concourse.bass_utils import run_bass_kernel_spmd as _run

    nc = _bacc.Bacc("TRN2", target_bir_lowering=False, num_devices=1)
    arrays, args = {}, []
    for name in _INS:
        a = _np.ascontiguousarray(inputs[name])
        arrays[f"in_{name}"] = a
        args.append(nc.dram_tensor(f"in_{name}", a.shape, _mybir.dt.from_np(a.dtype), kind="ExternalInput").ap())
    shape = tuple(inputs['x'].shape)
    out = nc.dram_tensor("out_x", shape, _mybir.dt.float32, kind="ExternalOutput").ap()
    gnn_kernel(nc, *args, out)
    r = _run(nc, [arrays], core_ids=[0])
    return r.results[0]["out_x"]
```

```python
import concourse.bass as bass
from concourse import mybir
from contextlib import ExitStack


class Norm:

    def __init__(self, sb, sem, name, fp32, rows, tiles, stats, at):
        self.rows, self.tiles = rows, tiles
        self.xc = sb(name + "_xc", [128, 2, tiles, 64], fp32)
        self.sq = sb(name + "_sq", [128, 2, tiles, 64], fp32)
        self.sum = sb(name + "_sum", [128, 2, tiles], fp32)
        self.h = sb(name + "_h", [128, 2, tiles, 64], fp32)
        self.hT = sb(name + "_hT", [128, 2, tiles // 2, 128], fp32)
        self.var, self.inv = [[t[:, at + q * tiles:at + (q + 1) * tiles] for q in range(2)] for t in stats]
        self.total = sem(name + "_total")
        self.centred = sem(name + "_centred")
        self.squared = sem(name + "_squared")
        self.spread = sem(name + "_spread")
        self.hidden = sem(name + "_hidden")
        self.turned = sem(name + "_turned")
        self.taken = sem(name + "_taken")
        self.product = sem(name + "_product")
        self.added = sem(name + "_added")
        self.done = sem(name + "_done")


class Lane:

    def __init__(self, sb, sem, name, fp32, rows, tiles, stats, at, banks1, banks2):
        self.rows, self.tiles = rows, tiles
        self.norm1 = Norm(sb, sem, name + "_n1", fp32, rows, tiles, stats, at)
        self.norm2 = Norm(sb, sem, name + "_n2", fp32, rows, tiles, stats, at + 2 * tiles)
        self.x1 = sb(name + "_x1", [128, 4, tiles, 64], fp32)
        self.norm1.banks, self.norm2.banks = banks1, banks2


def gnn_kernel(nc, x, src, dst, edge_type, edge_weight, init_weight, weight, root_weight, bias,
               bn_gamma, bn_beta, bn_mean, bn_var, rel_weight, self_loop, out):
    fp32, bf16, i32 = mybir.dt.float32, mybir.dt.bfloat16, mybir.dt.int32
    ALU = mybir.AluOpType
    ACT = mybir.ActivationFunctionType
    AX = mybir.AxisListType

    N, F = x.shape
    E = src.shape[0]
    R = rel_weight.shape[0]
    EPS = 1e-5
    COLS = 200
    EP = E // COLS
    GROUP = 4
    GROUPS = COLS // GROUP
    ITERS = GROUPS // 2
    PAIRS = ITERS // 2
    ROWS = 128 * COLS
    DT = 8
    DP = N // (DT * 2 * GROUPS)
    CHUNK = DT * DP
    NOWHERE = 131071
    assert EP * COLS == E and DP * DT * 2 * GROUPS == N and F == 64 and ITERS % 2 == 1

    ctx = ExitStack()
    with ctx:
        def sb(name, shape, dt):
            return ctx.enter_context(nc.sbuf_tensor(name, shape, dt))

        def sem(name):
            return ctx.enter_context(nc.semaphore(name))

        def dram(name, shape, dt=fp32):
            return nc.dram_tensor(name, shape, dt).ap()

        table = [dram(f"sum_table{k}", [ROWS + 1, F]) for k in range(3)]
        xs_dram = dram("x_of_src", [ROWS, F])
        xd_dram = dram("x_of_dst", [ROWS, F])
        hs_dram = dram("h_of_src", [ROWS, F])
        us_dram = dram("root_term_of_src", [ROWS, F])
        src_by_column = dram("src_by_column", [COLS, 128])
        sorted_edges = dram("sorted_edges", [E, 4])

        def by_col(t):
            return t[0:ROWS, :].rearrange("(p j) f -> p j f", j=COLS)

        src_i = sb("src_i", [128, COLS], i32)
        dst_i = sb("dst_i", [128, COLS], i32)
        typ_i = sb("typ_i", [128, COLS], i32)
        ew = sb("ew", [128, COLS], fp32)
        next_i = sb("next_i", [128, 1], i32)
        src1 = sb("src1", [128, COLS], fp32)
        srcf = sb("srcf", [128, COLS], fp32)
        dstf = sb("dstf", [128, COLS], fp32)
        typf = sb("typf", [128, COLS], fp32)
        nextf = sb("nextf", [128, 1], fp32)
        same = sb("same", [128, COLS], fp32)
        final = sb("final", [128, COLS], fp32)
        deg = sb("deg", [128, COLS], fp32)
        eq = sb("eq", [128, COLS], fp32)
        tmp = sb("tmp", [128, COLS], fp32)
        root = sb("root", [128, COLS], fp32)
        dinv = sb("dinv", [128, COLS], fp32)
        norm = sb("norm", [128, COLS], fp32)
        dinv_src = sb("dinv_src", [128, COLS], fp32)
        place = sb("place", [128, COLS], fp32)
        block_base = sb("block_base", [128, COLS], fp32)
        look = sb("look", [128, 2 * COLS + 1], fp32)
        look_part = sb("look_part", [128, 2, 2 * COLS + 1], bf16)
        look_last = sb("look_last", [128, COLS], bf16)
        slot_i = sb("slot_i", [128, COLS], i32)
        dstx_i = sb("dstx_i", [128, COLS], i32)
        dsto_i = sb("dsto_i", [128, COLS], i32)
        patch_i = sb("patch_i", [128, 1], i32)
        patchf = sb("patchf", [128, 1], fp32)
        pair_mask = sb("pair_mask", [128, COLS, R // 2], fp32)
        half_mask = sb("half_mask", [128, COLS, 2], fp32)
        carry_in = sb("carry_in", [128, 128], fp32)
        carry_back = sb("carry_back", [128, 128], fp32)
        diag = sb("diag", [128, 2, 128], fp32)
        srcT = sb("srcT", [COLS // 2, 2, 128], fp32)

        ident = sb("ident", [128, 128], fp32)
        ones = sb("ones", [128, 128], fp32)
        before = sb("before", [128, 128], fp32)
        after = sb("after", [128, 128], fp32)
        count_i = sb("count_i", [128, COLS], i32)
        count1 = sb("count1", [128, COLS], fp32)
        base_i = sb("base_i", [128, 1], i32)
        basef = sb("basef", [128, 1], fp32)
        rel_i = sb("rel_i", [128, R], i32)
        relf = sb("relf", [128, R], fp32)
        eps = sb("eps", [128, 1], fp32)
        zrow = sb("zrow", [1, F], fp32)
        w_arma = sb("w_arma", [128, 128], fp32)
        b_arma = sb("b_arma", [128, 1], fp32)
        w_next = sb("w_next", [128, F], fp32)
        w_root = sb("w_root", [128, 128], fp32)
        w_rootk = sb("w_rootk", [128, 2, F], fp32)
        w_loop = sb("w_loop", [128, 128], fp32)
        w_loopT = sb("w_loopT", [128, 128], fp32)
        w_rel = sb("w_rel", [128, R // 4, 2 * F], fp32)
        bnv = sb("bnv", [128, 4, F], fp32)
        bvec = sb("bvec", [128, 2, F], fp32)
        bns = sb("bns", [128, F], fp32)
        bn_t = sb("bn_t", [128, F], fp32)
        bias_part = sb("bias_part", [128, 3, F], bf16)
        bias_rest = sb("bias_rest", [128, 3, F], fp32)
        bias_row = sb("bias_row", [3, DT, F], bf16)
        ones3 = sb("ones3", [3, 128], bf16)

        xr = sb("xr", [128, 4 * GROUP, F], fp32)
        hr = sb("hr", [128, 4 * GROUP, F], fp32)
        cat = sb("cat", [128, 4 * GROUP, 2 * F], fp32)
        ar = sb("ar", [128, 4 * GROUP, F], fp32)
        ur = sb("ur", [128, 4 * GROUP, F], fp32)
        tr = sb("tr", [128, 4 * GROUP, F], fp32)
        state = sb("state", [128, 4 * GROUP, F], fp32)
        idx = sb("idx", [128, 4, GROUP], i32)
        msg = sb("msg", [128, 2, GROUP, F], fp32)
        sbc = sb("sbc", [128, 4, GROUP * 128], fp32)
        past_first = sb("past_first", [128, 2, GROUP * 128], fp32)
        pick = sb("pick", [128, 2, GROUP * 128], fp32)
        pick_bf = pick.bitcast(bf16)[:, :, 0:GROUP * 128]
        found = sb("found", [128, 2, GROUP, COLS], fp32)
        mask = found.rearrange("p q t j -> p (q t j)").rearrange("p (j r) -> p j r", r=R)
        dropped = sb("dropped", [128, 2, GROUP, COLS], fp32)
        catT, reluT = past_first, pick
        spread = sb("spread", [128, 2, GROUP, R // 2, F], fp32)
        spreadT = sb("spreadT", [128, 2, 2, 4 * 128], fp32)
        halves = sb("halves", [128, GROUP, 2, F], fp32)
        patch_row = sb("patch_row", [128, F], fp32)
        patched = sb("patched", [128, F], fp32)
        dx = sb("dx", [128, 4, DT * F], fp32)
        dout = sb("dout", [128, 4, DT * F], fp32)
        eout = sb("eout", [128, 4 * GROUP, F], fp32)

        SORT_KEYS = 5 * COLS
        SORT_CHUNKS = E // SORT_KEYS
        SORT_SPAN = 32768
        assert SORT_CHUNKS * SORT_KEYS == E and SORT_KEYS <= GROUP * 2 * 128 and ROWS < SORT_SPAN
        out_of_order = sb("out_of_order", [128, 1], fp32)
        unsorted_i = sb("unsorted_i", [128, 1], i32)
        packed = dout.rearrange("p s f -> p (s f)")[:, 0:4 * COLS].rearrange("p (j c) -> p j c", c=4)
        keys_raw = sbc.bitcast(i32).rearrange("p s e -> p (s e)")[:, 0:SORT_KEYS]
        number_i = past_first.bitcast(i32).rearrange("p s e -> p (s e)")[:, 0:SORT_KEYS]
        minus_number = pick.rearrange("p s e -> p (s e)")[:, 0:SORT_KEYS]
        keys = found.rearrange("p q t j -> p (q t j)")[:, 0:SORT_KEYS]
        key_gap = dropped.rearrange("p q t j -> p (q t j)")[:, 0:SORT_KEYS]
        is_before = dx.rearrange("p s f -> p (s f)")[:, 0:SORT_KEYS]

        bank = ctx.enter_context(nc.psum_tensor("bank", [128, 8, 512], fp32))
        EDGE_STATS, DENSE_STATS = 4 * GROUP, 4 * DT
        STATS = EDGE_STATS + DENSE_STATS
        var = sb("var", [128, STATS], fp32)
        std = sb("std", [128, STATS], fp32)
        inv = sb("inv", [128, STATS], fp32)
        edge = Lane(sb, sem, "edge", fp32, 128, GROUP, (var, inv), 0, (1, 2), (4, 5))
        dense = Lane(sb, sem, "dense", fp32, DP, DT, (var, inv), EDGE_STATS, (4, 5), (6, 7))

        SUMMED1 = [(edge.norm1, 0), (edge.norm1, 1), (dense.norm1, 0), (dense.norm1, 1)]
        SUMMED2 = []

        edges_in = sem("edges_in")
        weights_in = sem("weights_in")
        filled = sem("filled")
        const = sem("const")
        pool_chain = sem("pool_chain")
        pool_passed = sem("pool_passed")
        prep = sem("prep")
        shown = sem("shown")
        rooted = sem("rooted")
        src_out = sem("src_out")
        order_step = sem("order_step")
        order_shown = sem("order_shown")
        order_known = sem("order_known")
        sort_step = sem("sort_step")
        numbered = sem("numbered")
        keys_in = sem("keys_in")
        keys_taken = sem("keys_taken")
        sort_passed = sem("sort_passed")
        ranked = sem("ranked")
        sort_set = sem("sort_set")
        sort_out = sem("sort_out")
        sorted_in = sem("sorted_in")
        zero_out = sem("zero_out")
        ready0 = sem("ready0")
        ready1 = sem("ready1")
        weights_ok = sem("weights_ok")
        idx_set = sem("idx_set")
        gathered = [sem(f"gathered{s}") for s in range(4)]
        bc_in = [sem(f"bc_in{p}") for p in range(2)]
        below = sem("below")
        picked = sem("picked")
        looked = sem("looked")
        placed = sem("placed")
        matched = sem("matched")
        based = sem("based")
        x_spilled = [sem(f"x_spilled{p}") for p in range(2)]
        h_spilled = [sem(f"h_spilled{p}") for p in range(2)]
        u_spilled = [sem(f"u_spilled{p}") for p in range(2)]
        t_spilled = [sem(f"t_spilled{p}") for p in range(2)]
        h_in = [sem(f"h_in{p}") for p in range(2)]
        xu_in = [sem(f"xu_in{p}") for p in range(2)]
        dense_in = [sem(f"dense_in{p}") for p in range(2)]
        dense_out = [sem(f"dense_out{p}") for p in range(2)]
        weighed = sem("weighed")
        scanned = sem("scanned")
        cat_turned = sem("cat_turned")
        cat_taken = sem("cat_taken")
        arma_done = sem("arma_done")
        rooted_all = sem("rooted_all")
        scaled_all = sem("scaled_all")
        halved = sem("halved")
        t2_in = [sem(f"t2_in{p}") for p in range(2)]
        arma_relu = sem("arma_relu")
        arma_out = sem("arma_out")
        root_taken = sem("root_taken")
        summed = sem("summed")
        x1_made = sem("x1_made")
        spread_done = sem("spread_done")
        spread_turned = sem("spread_turned")
        spread_taken = sem("spread_taken")
        rel_out = sem("rel_out")
        carried = sem("carried")
        patch_in = sem("patch_in")
        patch_made = sem("patch_made")
        patch_out = sem("patch_out")
        scattered = [sem(f"scattered{s}") for s in range(4)]

        block = ctx.enter_context(nc.Block())

        S1_TURN, S2_TURN, S4_TURN = (3, 0), 3, (0, 3)
        S3_TURN = ((0, 3), (4, 5))
        S3_OUT = ((1, 2), (6, 7))

        def turns(par):
            return PAIRS + 1 if par == 0 else PAIRS

        def each_iteration(eng, body):
            body(0, 0, 0)
            body(1, 1, 0)
            with eng.Fori(1, PAIRS) as k:
                body(2 * k, 0, k)
                body(2 * k + 1, 1, k)
            body(2 * PAIRS, 0, PAIRS)

        def overlapped(eng, body, depth):
            def at(i, k=None):
                body(i, i % 2, i // 2, [0 <= i - d < ITERS for d in range(depth)])
            for i in range(4):
                at(i)
            with eng.Fori(2, PAIRS) as k:
                body(2 * k, 0, k, [True] * depth)
                body(2 * k + 1, 1, k, [True] * depth)
            for i in range(2 * PAIRS, ITERS + depth - 1):
                at(i)

        def earlier(it, par, k, by):
            return it - by, (par + by) % 2, k - (by + 1 - par) // 2

        def wait_past(eng, s, value):
            if not (isinstance(value, int) and value <= 0):
                eng.wait_ge(s, value)

        def cols(it, q):
            return bass.ds(2 * GROUP * it + GROUP * q, GROUP)

        def slots(par):
            return slice(2 * GROUP * par, 2 * GROUP * par + 2 * GROUP)

        def slot(par, q):
            s = 2 * par + q
            return slice(GROUP * s, GROUP * s + GROUP)

        def wide(ap, n):
            return ap.unsqueeze(2).to_broadcast([ap.shape[0], ap.shape[1], n])

        def dense_rows(t, it):
            return t[bass.ds(2 * CHUNK * it, 2 * CHUNK), :].rearrange(
                "(c p t) f -> p c (t f)", c=2, t=DT)

        @block.sync
        def _(eng):
            eng.wait_ge(filled, 1)
            for a, b in ((src_i, src), (dst_i, dst), (typ_i, edge_type), (ew, edge_weight)):
                eng.dma_start(a[0:EP, :], b.rearrange("(p j) -> p j", j=COLS)).then_inc(edges_in, 16)
            with nc.allow_non_contiguous_dma(reason="one element per partition"):
                eng.dma_start(next_i[0:EP - 1, :], dst.rearrange("(p j) -> p j", j=COLS)[1:EP, 0:1]
                              ).then_inc(edges_in, 16)
            for k in range(2):
                h = slice(k * F, (k + 1) * F)
                eng.dma_start(w_arma[0:F, h], init_weight[k]).then_inc(weights_in, 16)
                eng.dma_start(w_arma[F:128, h], root_weight[0, k]).then_inc(weights_in, 16)
                eng.dma_start(w_rootk[0:F, k, :], root_weight[1, k]).then_inc(weights_in, 16)
                eng.dma_start(w_rootk[F:128, k, :], root_weight[1, k]).then_inc(weights_in, 16)
                eng.dma_start(w_loop[h, h], self_loop).then_inc(weights_in, 16)
                eng.dma_start(bvec[:, k, :], bias[1, k].to_broadcast([128, F])).then_inc(weights_in, 16)
            eng.dma_start(w_next[:, :], weight[0].rearrange("k f o -> (k f) o")).then_inc(weights_in, 16)
            eng.dma_start(b_arma[:, :], bias[0].rearrange("k a o -> (k o) a")).then_inc(weights_in, 16)
            for b in range(2):
                for c in range(R // 4):
                    eng.dma_start(w_rel[b * F:(b + 1) * F, c, :].rearrange("f (r o) -> f r o", r=2),
                                  rel_weight[4 * c + 2 * b:4 * c + 2 * b + 2].rearrange("r f o -> f r o")
                                  ).then_inc(weights_in, 16)
            for k, v in enumerate((bn_gamma, bn_beta, bn_mean, bn_var)):
                eng.dma_start(bnv[:, k, :], v.unsqueeze(0).to_broadcast([128, F])).then_inc(weights_in, 16)
            eng.wait_ge(const, 1)
            for k in range(3):
                eng.dma_start(table[k][ROWS:ROWS + 1, :], zrow[:, :]).then_inc(zero_out, 16)
            eng.wait_ge(ready0, 2)
            eng.dma_start(src_by_column.rearrange("(c j) p -> j c p", c=2), srcT[:, :, :]
                          ).then_inc(src_out, 16)
            eng.wait_ge(src_out, 16)

            def store(stage_base, it, par, k, ring, where, done):
                eng.dma_start(by_col(where)[:, bass.ds(2 * GROUP * it, 2 * GROUP), :],
                              ring[:, slots(par), :]).then_inc(done[par], 16)

            def load(it, par, ring, where, s):
                eng.dma_start(ring[:, slots(par), :],
                              by_col(where)[:, bass.ds(2 * GROUP * it, 2 * GROUP), :]).then_inc(s[par], 16)

            def spilling(load_part, *store_parts):
                def body(it, par, k, on):
                    if on[0]:
                        load_part(it, par, k)
                    for d, part in enumerate(store_parts):
                        if on[d + 1]:
                            part(*earlier(it, par, k, d + 1))
                overlapped(eng, body, 1 + len(store_parts))

            def gather_done(stage, par, k):
                for q in range(2):
                    eng.wait_ge(gathered[2 * par + q], 16 * GROUP * (stage * turns(par) + k + 1))

            def store0(it, par, k):
                gather_done(0, par, k)
                store(0, it, par, k, xr, xd_dram, x_spilled)

            each_iteration(eng, store0)

            def load_dense(base, it, par, k):
                wait_past(eng, dense.norm1.done, base * 2 * ITERS + 2 * it - 2)
                eng.dma_start(dx[0:DP, 2 * par:2 * par + 2, :], dense_rows(x, base * ITERS + it)
                              ).then_inc(dense_in[par], 16)

            def store_dense(base, it, par, k):
                eng.wait_ge(dense.norm2.done, base * 2 * ITERS + 2 * it + 2)
                eng.dma_start(dense_rows(out, base * ITERS + it), dout[0:DP, 2 * par:2 * par + 2, :]
                              ).then_inc(dense_out[par], 16)

            def store1(it, par, k):
                gather_done(1, par, k)
                store(1, it, par, k, xr, xs_dram, x_spilled)
                eng.wait_ge(edge.norm1.hidden, 2 * it + 2)
                store(1, it, par, k, hr, hs_dram, h_spilled)

            def store_sums(stage, it, par, k):
                eng.wait_ge(scanned, stage * COLS + 2 * GROUP * it + 2 * GROUP + 1)
                store(stage, it, par, k, state, table[stage], t_spilled)

            spilling(lambda it, par, k: load_dense(0, it, par, k), store1,
                     lambda it, par, k: store_sums(0, it, par, k),
                     lambda it, par, k: store_dense(0, it, par, k))

            for p in range(2):
                eng.wait_ge(h_spilled[p], 16 * turns(p))

            def load2(it, par, k):
                wait_past(eng, cat_turned, 2 * it - 2)
                eng.dma_start(cat[:, slots(par), F:2 * F],
                              by_col(hs_dram)[:, bass.ds(2 * GROUP * it, 2 * GROUP), :]).then_inc(h_in[par], 16)
                load_dense(1, it, par, k)

            def store2(it, par, k):
                eng.wait_ge(root_taken, 2 * it + 2)
                store(2, it, par, k, ur, us_dram, u_spilled)

            spilling(load2, store2, lambda it, par, k: store_sums(1, it, par, k),
                     lambda it, par, k: store_dense(1, it, par, k))

            for p in range(2):
                eng.wait_ge(u_spilled[p], 16 * turns(p))
                eng.wait_ge(x_spilled[p], 16 * 2 * turns(p))

            def load3(it, par, k):
                wait_past(eng, x1_made, 2 * it - 2)
                load(it, par, xr, xs_dram, xu_in)
                load(it, par, ur, us_dram, xu_in)

            def nothing(it, par, k):
                pass

            spilling(load3, nothing, nothing, lambda it, par, k: store_sums(2, it, par, k))

            eng.wait_ge(x1_made, GROUPS)
            eng.wait_ge(patch_out, 16 * 3)

            def load4(it, par, k):
                wait_past(eng, edge.norm1.done, 2 * it - 2)
                load(it, par, xr, xd_dram, xu_in)
                load(it, par, ur, table[1], xu_in)

            def load4_late(it, par, k):
                wait_past(eng, edge.norm2.done, 2 * it - 2)
                load(it, par, tr, table[2], t2_in)

            spilling(load4, load4_late)
            for p in range(2):
                eng.wait_ge(dense_out[p], 16 * 2 * turns(p))
                eng.wait_ge(t_spilled[p], 16 * 3 * turns(p))
            eng.wait_ge(zero_out, 16 * 3)

        @block.gpsimd
        def _(eng):
            eng.memset(zrow[:, :], 0.0).then_inc(const, 1)
            eng.memset(ones[:, :], 1.0).then_inc(pool_chain, 1)
            eng.memset(eps[:, :], EPS).then_inc(pool_chain, 1)
            eng.iota(count_i[:, :], pattern=[[1, COLS]], base=1, channel_multiplier=0).then_inc(pool_chain, 1)
            eng.iota(base_i[:, :], pattern=[[0, 1]], base=0, channel_multiplier=COLS).then_inc(pool_chain, 1)
            eng.iota(rel_i[:, :], pattern=[[1, R]], base=0, channel_multiplier=0).then_inc(pool_chain, 1)
            eng.wait_ge(pool_chain, 5)
            eng.affine_select(out=ident[:, :], in_=ones[:, :], compare_op=ALU.is_equal, fill=0.0, base=0,
                              pattern=[[-1, 128]], channel_multiplier=1).then_inc(const, 1)
            eng.affine_select(out=before[:, :], in_=ones[:, :], compare_op=ALU.is_gt, fill=0.0, base=0,
                              pattern=[[1, 128]], channel_multiplier=-1).then_inc(const, 1)
            eng.affine_select(out=after[:, :], in_=ones[:, :], compare_op=ALU.is_gt, fill=0.0, base=0,
                              pattern=[[-1, 128]], channel_multiplier=1).then_inc(const, 1)

            def await_count(s, value):
                wait_past(eng, s, value)
                eng.sem_inc(pool_passed, 1)

            def place_idx(stage, it, par, q, indices):
                eng.tensor_copy(idx[:, 2 * par + q, :], indices[:, cols(it, q)]).then_inc(idx_set, 1)
                await_count(idx_set, stage * GROUPS + 2 * it + q + 1)

            def gather(stage, it, par, q, indices, rows, ring):
                place_idx(stage, it, par, q, indices)
                for t in range(GROUP):
                    s = 2 * par + q
                    eng.indirect_dma_start(
                        out=ring[:, GROUP * s + t, 0:F], out_offset=None, in_=rows,
                        in_offset=bass.IndirectOffsetOnAxis(ap=idx[:, s, t:t + 1], axis=0),
                    ).then_inc(gathered[s], 16)

            eng.wait_ge(order_known, 1)
            unsorted = eng.value_load(unsorted_i[0:1, 0:1], min_val=0, max_val=E)
            with eng.If(unsorted > 0):
                eng.iota(number_i, pattern=[[1, SORT_KEYS]], base=1, channel_multiplier=0).then_inc(numbered, 1)

                def load_keys(c):
                    eng.dma_start(keys_raw, dst[bass.ds(SORT_KEYS * c, SORT_KEYS)].unsqueeze(0)
                                  .to_broadcast([128, SORT_KEYS])).then_inc(keys_in, 16)

                load_keys(0)
                with eng.Fori(1, SORT_CHUNKS) as c:
                    await_count(keys_taken, c)
                    load_keys(c)
                eng.wait_ge(ranked, 1)
                with eng.Fori(0, COLS) as j:
                    eng.tensor_copy(idx[:, 0, 0:1], slot_i[:, bass.ds(j, 1)]).then_inc(sort_set, 1)
                    eng.tensor_copy(eout[:, 0, 0:4], packed[:, bass.ds(j, 1), :].rearrange("p j c -> p (j c)")
                                    ).then_inc(sort_set, 1)
                    await_count(sort_set, 2 * j + 2)
                    eng.indirect_dma_start(
                        out=sorted_edges, out_offset=bass.IndirectOffsetOnAxis(ap=idx[:, 0, 0:1], axis=0),
                        in_=eout[:, 0, 0:4], in_offset=None,
                        bounds_check=E - 1, oob_is_err=False).then_inc(sort_out, 16)
                    await_count(sort_out, 16 * j + 16)
                by_partition = sorted_edges.rearrange("(p j) c -> p j c", j=COLS)
                eng.dma_start(packed[0:EP], by_partition).then_inc(sorted_in, 16)
                with nc.allow_non_contiguous_dma(reason="one element per partition"):
                    eng.dma_start(nextf[0:EP - 1, :], by_partition[1:EP, 0, 1:2]).then_inc(sorted_in, 16)

            eng.wait_ge(ready0, 1)

            def gather0(it, par, k):
                await_count(x_spilled[par], 16 * k)
                for q in range(2):
                    gather(0, it, par, q, dstx_i, x, xr)

            each_iteration(eng, gather0)

            def gather1(it, par, k):
                await_count(x_spilled[par], 16 * (turns(par) + k))
                for q in range(2):
                    await_count(edge.norm1.centred, 2 * it + q - 3)
                    gather(1, it, par, q, src_i, x, xr)

            each_iteration(eng, gather1)

            def patch(stage):
                for p in range(2):
                    eng.wait_ge(t_spilled[p], 16 * (stage + 1) * turns(p))
                eng.indirect_dma_start(
                    out=patch_row[:, :], out_offset=None, in_=table[stage][:, :],
                    in_offset=bass.IndirectOffsetOnAxis(ap=patch_i[:, 0:1], axis=0)).then_inc(patch_in, 16)
                eng.wait_ge(patch_made, stage + 1)
                eng.indirect_dma_start(
                    out=table[stage][:, :], out_offset=bass.IndirectOffsetOnAxis(ap=patch_i[:, 0:1], axis=0),
                    in_=patched[:, :], in_offset=None).then_inc(patch_out, 16)
                eng.wait_ge(patch_out, 16 * (stage + 1))

            patch(0)
            eng.wait_ge(zero_out, 16 * 3)

            def gather2(it, par, k):
                for q in range(2):
                    await_count(cat_turned, 2 * it + q - 3)
                    gather(2, it, par, q, slot_i, table[0][:, :], cat)

            each_iteration(eng, gather2)
            patch(1)

            def gather3(it, par, k):
                for q in range(2):
                    await_count(summed, 2 * it + q - 3)
                    gather(3, it, par, q, slot_i, table[1][:, :], ar)

            each_iteration(eng, gather3)
            patch(2)

            for p in range(2):
                eng.wait_ge(dense_out[p], 16 * 2 * turns(p))

            def scatter(it, par, k):
                for q in range(2):
                    s = 2 * par + q
                    await_count(scattered[s], 16 * GROUP * k)
                    place_idx(4, it, par, q, dsto_i)
                    await_count(edge.norm2.done, 2 * it + q + 1)
                    for t in range(GROUP):
                        eng.indirect_dma_start(
                            out=out, out_offset=bass.IndirectOffsetOnAxis(ap=idx[:, s, t:t + 1], axis=0),
                            in_=eout[:, GROUP * s + t, :], in_offset=None,
                            bounds_check=N - 1, oob_is_err=False).then_inc(scattered[s], 16)

            each_iteration(eng, scatter)
            for s in range(4):
                eng.wait_ge(scattered[s], 16 * GROUP * turns(s // 2))

        def act_square(eng, norm, q, n, on_scalar=()):
            eng.wait_ge(norm.centred, n + 1)
            if (norm, q) in on_scalar:
                for t in range(norm.tiles):
                    last = eng.activation(norm.sq[0:norm.rows, q, t], norm.xc[0:norm.rows, q, t], ACT.Square,
                                          accum_out=norm.var[q][0:norm.rows, t:t + 1])
                    if t == norm.tiles - 2:
                        last.then_inc(norm.squared, 1)
                last.then_inc(norm.spread, 1)
                return
            eng.activation(norm.sq[0:norm.rows, q], norm.xc[0:norm.rows, q], ACT.Square
                           ).then_inc(norm.squared, 1)

        def act_roots(eng, norms, lo, hi):
            for norm, n in norms:
                eng.wait_ge(norm.spread, n + 2)
            eng.activation(std[:, lo:hi], var[:, lo:hi], ACT.Sqrt, bias=eps[:, :], scale=1.0 / F
                           ).then_inc(rooted_all, 1)

        def act_take(eng, lane, norm, q, n, turn_bank):
            eng.wait_ge(norm.turned, n + 1)
            pairs = lane.tiles // 2
            eng.activation(norm.hT[:, q, :, 0:lane.rows],
                           bank[:, turn_bank, 0:128 * pairs]
                           .rearrange("p (a b) -> p a b", a=pairs)[:, :, 0:lane.rows],
                           ACT.Copy).then_inc(norm.taken, 1)

        @block.scalar
        def _(eng):
            eng.wait_ge(prep, PREP_DEG)
            eng.activation(root[:, :], tmp[:, :], ACT.Sqrt).then_inc(rooted, 1)
            eng.wait_ge(weights_in, 16 * 22)
            eng.wait_ge(pool_chain, 2)
            eng.activation(bn_t[:, :], bnv[:, 3, :], ACT.Sqrt, bias=eps[:, :]).then_inc(rooted, 1)

            eng.wait_ge(src_out, 16)

            def body0(it, par, k, on):
                if on[0]:
                    wait_past(eng, picked, 2 * it - 2)
                    eng.dma_start(sbc[:, 2 * par:2 * par + 2, :],
                                  src_by_column[bass.ds(2 * GROUP * it, 2 * GROUP), :]
                                  .rearrange("(g t) p -> g (t p)", g=2).unsqueeze(0)
                                  .to_broadcast([128, 2, GROUP * 128])).then_inc(bc_in[par], 16)
                if not on[2]:
                    return
                for q in range(2):
                    for t in range(GROUP):
                        tile = 2 * GROUP * (it - 2) + GROUP * q + t
                        eng.wait_ge(matched, tile + 1)
                        eng.activation(block_base[:, bass.ds(tile, 1)], bank[:, 4 * q + t, 2 * COLS:2 * COLS + 1],
                                       ACT.Copy).then_inc(based, 1)

            overlapped(eng, body0, 3)

            def body1(it, par, k, on):
                n = 2 * it
                if on[0]:
                    for norm in (edge.norm1, dense.norm1):
                        for q in range(2):
                            act_square(eng, norm, q, n + q, SUMMED1)
                if on[1]:
                    for q in range(2):
                        act_square(eng, dense.norm2, q, n - 2 + q, SUMMED1)
                if on[0] or on[1]:
                    act_roots(eng, ([(edge.norm1, n), (dense.norm1, n)] if on[0] else [])
                              + ([(dense.norm2, n - 2)] if on[1] else []), 0, STATS)
                for norm, m, yes in ((dense.norm1, n, on[0]), (dense.norm2, n - 2, on[1])):
                    for q in range(2):
                        if yes:
                            act_take(eng, dense, norm, q, m + q, S1_TURN[q])

            overlapped(eng, body1, 3)

            def body2(it, par, k, on):
                n = 2 * ITERS + 2 * it

                def turn_cat(q):
                    if on[0]:
                        eng.wait_ge(cat_turned, 2 * it + q + 1)
                        eng.activation(catT[:, q, :], bank[:, 0, :], ACT.Copy).then_inc(cat_taken, 1)

                def relu_arma(q):
                    if on[0]:
                        eng.wait_ge(arma_done, 2 * it + q + 1)
                        eng.activation(reluT[:, q, :], bank[:, 0, :], ACT.Relu, bias=b_arma[:, :]
                                       ).then_inc(arma_relu, 1)

                def take(layer, q):
                    if on[layer]:
                        act_take(eng, dense, (dense.norm1, dense.norm2)[layer - 1], q, n - 2 * layer + q, S2_TURN)

                def square(layer, q):
                    if on[layer - 1]:
                        act_square(eng, (dense.norm1, dense.norm2)[layer - 1], q, n - 2 * layer + 2 + q,
                                   SUMMED2)

                if on[1]:
                    before_it, before_par, before_k = earlier(it, par, k, 1)
                    wait_past(eng, u_spilled[before_par], 16 * before_k)
                    eng.wait_ge(arma_out, 2 * it)
                    for q in range(2):
                        eng.activation(ur[:, slot(before_par, q), :],
                                       bank[:, 1, GROUP * F * q:GROUP * F * (q + 1)]
                                       .rearrange("p (t f) -> p t f", f=F), ACT.Copy).then_inc(root_taken, 1)
                take(1, 0)
                turn_cat(0)
                take(1, 1)
                relu_arma(0)
                square(1, 0)
                square(1, 1)
                take(2, 0)
                turn_cat(1)
                take(2, 1)
                relu_arma(1)
                square(2, 0)
                square(2, 1)
                if on[0] or on[1]:
                    act_roots(eng, ([(dense.norm1, n)] if on[0] else [])
                              + ([(dense.norm2, n - 2)] if on[1] else []), EDGE_STATS, STATS)

            overlapped(eng, body2, 3)

            def body3(it, par, k, on):
                for q in range(2):
                    for half in range(2):
                        if on[1]:
                            eng.wait_ge(spread_turned, 4 * (it - 1) + 2 * q + half + 1)
                            eng.activation(spreadT[:, q, half, :], bank[:, S3_TURN[q][half], :], ACT.Copy
                                           ).then_inc(spread_taken, 1)
                    if on[0] and q == 0:
                        for item in range(2):
                            act_square(eng, edge.norm1, item, GROUPS + 2 * it + item)
                if on[0]:
                    act_roots(eng, [(edge.norm1, GROUPS + 2 * it)], 0, 2 * GROUP)

            overlapped(eng, body3, 3)

            def body4(it, par, k, on):
                if on[0]:
                    for q in range(2):
                        act_square(eng, edge.norm1, q, 2 * GROUPS + 2 * it + q)
                if on[1]:
                    for q in range(2):
                        act_square(eng, edge.norm2, q, 2 * it - 2 + q)
                if on[0] or on[1]:
                    act_roots(eng, ([(edge.norm1, 2 * GROUPS + 2 * it)] if on[0] else [])
                              + ([(edge.norm2, 2 * it - 2)] if on[1] else []), 0, EDGE_STATS)
                for norm, m, yes in ((edge.norm1, 2 * it, on[0]), (edge.norm2, 2 * it - 2, on[1])):
                    for q in range(2):
                        if yes:
                            act_take(eng, edge, norm, q, m + q, S4_TURN[q])

            overlapped(eng, body4, 3)

        def pe_turn(eng, lane, norm, q, n, hidden_n, turn_bank):
            P = lane.rows
            eng.wait_ge(norm.hidden, hidden_n + 1)
            for a in range(lane.tiles // 2):
                last = nc.tensor.transpose(bank[:, turn_bank, 128 * a:128 * a + P],
                                           norm.h[0:P, q, 2 * a:2 * a + 2, :].rearrange("p t f -> p (t f)"),
                                           ident[0:P, 0:P])
            last.then_inc(norm.turned, 1)

        def pe_product(eng, lane, norm, q, n, w, with_bias):
            P = lane.rows
            pairs = lane.tiles // 2
            b = norm.banks[q]
            wait_past(eng, norm.done, n - 1)
            if with_bias:
                nc.tensor.matmul(bank[0:P, b, 0:lane.tiles * F], ones3[:, 0:P],
                                 bias_row[:, 0:lane.tiles, :].rearrange("p t f -> p (t f)"),
                                 start=True, stop=False)
            eng.wait_ge(norm.taken, n + 1)
            for a in range(pairs):
                last = nc.tensor.matmul(bank[0:P, b, 128 * a:128 * a + 128], norm.hT[:, q, a, 0:P], w[:, :],
                                        start=not with_bias, stop=(a == pairs - 1 or not with_bias))
            last.then_inc(norm.product, 1)

        def pe_network(eng, lane, n, hidden_n, on, turn_banks):
            if on[0]:
                for q in range(2):
                    pe_turn(eng, lane, lane.norm1, q, n + q, hidden_n + q, turn_banks[q])
                for q in range(2):
                    pe_product(eng, lane, lane.norm1, q, n + q, w_root, True)
            if on[1]:
                for q in range(2):
                    pe_turn(eng, lane, lane.norm2, q, n - 2 + q, n - 2 + q, turn_banks[q])
                for q in range(2):
                    pe_product(eng, lane, lane.norm2, q, n - 2 + q, w_loopT, False)

        @block.tensor
        def _(eng):
            eng.wait_ge(const, 4)
            eng.wait_ge(order_step, 3)
            nc.tensor.matmul(bank[:, 7, 0:1], ones[:, :], out_of_order[:, :], start=True, stop=True
                             ).then_inc(order_shown, 1)
            eng.wait_ge(prep, PREP_DIAG)
            nc.tensor.matmul(bank[:, 0, 0:256], ones[:, :], diag[:, :, :].rearrange("p a b -> p (a b)"),
                             start=True, stop=True).then_inc(shown, 1)
            for c in range(2):
                nc.tensor.transpose(bank[0:COLS // 2, 4 + c, 0:128],
                                    srcf[:, c * (COLS // 2):(c + 1) * (COLS // 2)], ident[:, :]
                                    ).then_inc(shown, 1)
            eng.wait_ge(prep, PREP_TAIL)
            nc.tensor.matmul(bank[:, 1, 0:1], carry_in[:, :], deg[:, COLS - 1:COLS],
                             start=True, stop=True).then_inc(shown, 1)
            eng.wait_ge(prep, PREP_BACK)
            nc.tensor.matmul(bank[:, 2, 0:1], carry_back[:, :], dinv[:, 0:1],
                             start=True, stop=True).then_inc(shown, 1)
            eng.wait_ge(weights_in, 16 * 22)
            nc.tensor.transpose(bank[:, 3, 0:128], w_loop[:, :], ident[:, :]).then_inc(shown, 1)

            eng.wait_ge(ready0, 3)

            def body0(it, par, k):
                for q in range(2):
                    eng.wait_ge(picked, 2 * it + q + 1)
                    for t in range(GROUP):
                        tile = 2 * GROUP * it + GROUP * q + t
                        wait_past(eng, based, tile + 1 - 2 * GROUP)
                        one_hot = pick_bf[:, q, 128 * t:128 * t + 128]
                        nc.tensor.matmul(bank[:, 4 * q + t, 0:2 * COLS + 1], one_hot, look_part[:, 0, :],
                                         start=True, stop=False)
                        nc.tensor.matmul(bank[:, 4 * q + t, 0:2 * COLS + 1], one_hot, look_part[:, 1, :],
                                         start=False, stop=False)
                        nc.tensor.matmul(bank[:, 4 * q + t, COLS:2 * COLS], one_hot, look_last[:, :],
                                         start=False, stop=True).then_inc(looked, 1)

            each_iteration(eng, body0)
            eng.wait_ge(based, COLS)
            eng.wait_ge(weights_ok, 2)

            def body1(it, par, k, on):
                pe_network(eng, dense, 2 * it, 2 * it, on, S1_TURN)

            overlapped(eng, body1, 3)

            def carry(stage):
                eng.wait_ge(scanned, (stage + 1) * COLS + 1)
                last_slot = GROUP * 2 - 1
                nc.tensor.matmul(bank[:, 0, 0:F], carry_in[:, :], state[:, last_slot, :],
                                 start=True, stop=True).then_inc(carried, 1)

            carry(0)
            eng.wait_ge(patch_made, 1)

            def body2(it, par, k, on):
                n = 2 * ITERS + 2 * it

                def turn_cat(q):
                    if on[0]:
                        s = 2 * par + q
                        eng.wait_ge(h_in[par], 16 * (k + 1))
                        eng.wait_ge(gathered[s], 16 * GROUP * (2 * turns(par) + k + 1))
                        wait_past(eng, arma_relu, 2 * it + q)
                        for t in range(GROUP):
                            last = nc.tensor.transpose(bank[:, 0, 128 * t:128 * t + 128],
                                                       cat[:, GROUP * s + t, :], ident[:, :])
                        last.then_inc(cat_turned, 1)

                def arma(q):
                    if on[0]:
                        eng.wait_ge(cat_taken, 2 * it + q + 1)
                        nc.tensor.matmul(bank[:, 0, :], w_arma[:, :], catT[:, q, :],
                                         start=True, stop=True).then_inc(arma_done, 1)

                def root_term(q):
                    if on[0]:
                        wait_past(eng, root_taken, 2 * it)
                        nc.tensor.matmul(bank[:, 1, GROUP * F * q:GROUP * F * (q + 1)], ones3[:, :],
                                         bias_row[:, 0:GROUP, :].rearrange("p t f -> p (t f)"),
                                         start=True, stop=False)
                        for t in range(GROUP):
                            at = F * (GROUP * q + t)
                            nc.tensor.matmul(bank[:, 1, at:at + F], catT[:, q, 128 * t:128 * t + 128],
                                             w_root[:, F:128], start=False, stop=(t == GROUP - 1))

                def arma_step(q):
                    if on[0]:
                        eng.wait_ge(weighed, GROUPS + 2 * it)
                        eng.wait_ge(arma_relu, 2 * it + q + 1)
                        for t in range(GROUP):
                            at = F * (GROUP * q + t)
                            last = nc.tensor.matmul(bank[:, 2, at:at + F],
                                                    reluT[:, q, 128 * t:128 * t + 128], w_next[:, :],
                                                    start=True, stop=True)
                        last.then_inc(arma_out, 1)

                def turn(layer, q):
                    if on[layer]:
                        m = n - 2 * layer + q
                        pe_turn(eng, dense, (dense.norm1, dense.norm2)[layer - 1], q, m, m, S2_TURN)

                def product(layer, q):
                    if on[layer]:
                        pe_product(eng, dense, (dense.norm1, dense.norm2)[layer - 1], q, n - 2 * layer + q,
                                   (w_root, w_loopT)[layer - 1], layer == 1)

                turn(1, 0)
                turn_cat(0)
                product(1, 0)
                turn(1, 1)
                arma(0)
                product(1, 1)
                turn(2, 0)
                root_term(0)
                turn_cat(1)
                product(2, 0)
                turn(2, 1)
                arma(1)
                product(2, 1)
                root_term(1)
                arma_step(0)
                arma_step(1)

            overlapped(eng, body2, 3)
            carry(1)
            eng.wait_ge(patch_made, 2)

            def body3(it, par, k, on):
                if not on[1]:
                    return
                it, par, k = earlier(it, par, k, 1)
                for q in range(2):
                    eng.wait_ge(spread_done, 2 * it + q + 1)
                    for half in range(2):
                        b = S3_TURN[q][half]
                        wait_past(eng, spread_taken, 4 * it + 2 * q + half - 3)
                        for i in range(4):
                            t, c = 2 * half + i // 2, i % 2
                            last = nc.tensor.transpose(
                                bank[:, b, 128 * i:128 * i + 128],
                                spread[:, q, t, 2 * c:2 * c + 2, :].rearrange("p r f -> p (r f)"), ident[:, :])
                        last.then_inc(spread_turned, 1)
                    wait_past(eng, halved, 2 * it + q - 3)
                    for half in range(2):
                        eng.wait_ge(spread_taken, 4 * it + 2 * q + half + 1)
                        for i in range(4):
                            t, c = 2 * half + i // 2, i % 2
                            last = nc.tensor.matmul(bank[:, S3_OUT[par][q], 128 * t:128 * t + 128],
                                                    spreadT[:, q, half, 128 * i:128 * i + 128], w_rel[:, c, :],
                                                    start=(c == 0), stop=(c == 1))
                    last.then_inc(rel_out, 1)

            overlapped(eng, body3, 3)
            carry(2)
            eng.wait_ge(patch_made, 3)

            def body4(it, par, k, on):
                pe_network(eng, edge, 2 * it, 2 * GROUPS + 2 * it, on, S4_TURN)

            overlapped(eng, body4, 3)

        def tiles_of(ap):
            return ap.rearrange("p (t f) -> p t f", f=F)

        def product_of(norm, q):
            return tiles_of(bank[0:norm.rows, norm.banks[q], 0:norm.tiles * F])

        def ln_centre(eng, items, between):
            for norm, q, n, xin in items:
                nc.vector.tensor_reduce(norm.sum[0:norm.rows, q], xin, AX.X, ALU.add).then_inc(norm.total, 1)
                between()
            for norm, q, n, xin in items:
                eng.wait_ge(norm.total, n + 1)
                nc.vector.scalar_tensor_tensor(out=norm.xc[0:norm.rows, q],
                                               in0=wide(norm.sum[0:norm.rows, q], F), scalar=-1.0 / F,
                                               in1=xin, op0=ALU.mult, op1=ALU.add).then_inc(norm.centred, 1)
                between()

        def ln_spread(eng, items, between, on_scalar=()):
            for norm, q, n, xin in items:
                if (norm, q) in on_scalar:
                    continue
                eng.wait_ge(norm.squared, n + 1)
                nc.vector.tensor_reduce(norm.var[q][0:norm.rows], norm.sq[0:norm.rows, q], AX.X, ALU.add
                                        ).then_inc(norm.spread, 1)
                between()

        def ln_scale(eng, count, lo, hi):
            eng.wait_ge(rooted_all, count + 1)
            nc.vector.reciprocal(inv[:, lo:hi], std[:, lo:hi]).then_inc(scaled_all, 1)

        def ln_hidden(eng, items, count, out_of, between):
            eng.wait_ge(scaled_all, count + 1)
            for norm, q, n, xin in items:
                nc.vector.scalar_tensor_tensor(out=out_of(norm, q), in0=norm.xc[0:norm.rows, q], scalar=0.0,
                                               in1=wide(norm.inv[q][0:norm.rows], F), op0=ALU.max,
                                               op1=ALU.mult).then_inc(norm.hidden, 1)
                between()

        def own_h(norm, q):
            return norm.h[0:norm.rows, q]

        def add_relu(eng, norm, q, n, xin, res):
            eng.wait_ge(norm.product, n + 1)
            nc.vector.scalar_tensor_tensor(out=res, in0=product_of(norm, q), scalar=0.0, in1=xin,
                                           op0=ALU.max, op1=ALU.add).then_inc(norm.done, 1)

        def with_sums(norm, q):
            f = slice(0, F) if norm is edge.norm1 else slice(F, 2 * F)
            return cat[:, GROUP * q:GROUP * q + GROUP, f]

        def add_sums(eng, norm, q, n, sums):
            eng.wait_ge(norm.product, n + 1)
            nc.vector.tensor_tensor(with_sums(norm, q), product_of(norm, q), sums, ALU.add
                                    ).then_inc(norm.added, 1)

        def relu_of_sums(eng, norm, q, n, xin, res):
            eng.wait_ge(norm.added, n + 1)
            nc.vector.scalar_tensor_tensor(out=res, in0=with_sums(norm, q), scalar=0.0, in1=xin,
                                           op0=ALU.max, op1=ALU.add).then_inc(norm.done, 1)

        @block.vector
        def _(eng):
            v = nc.vector
            steps = [0]

            def link(ins):
                steps[0] += 1
                ins.then_inc(prep, 1)
                eng.wait_ge(prep, steps[0])

            link(v.memset(src_i[:, :], 0))
            link(v.memset(typ_i[:, :], 0))
            link(v.memset(ew[:, :], 0.0))
            link(v.memset(next_i[:, :], NOWHERE))
            link(v.memset(w_loop[:, :], 0.0))
            v.memset(dst_i[:, :], NOWHERE).then_inc(filled, 1)
            link(v.memset(w_root[:, :], 0.0))
            eng.wait_ge(edges_in, 16 * 5)
            eng.wait_ge(const, 4)
            for a, b in ((srcf, src_i), (dstf, dst_i), (typf, typ_i), (nextf, next_i), (count1, count_i),
                         (basef, base_i), (relf, rel_i)):
                link(v.tensor_copy(a[:, :], b[:, :]))
            first, last = dstf[:, 0:1], dstf[:, COLS - 1:COLS]

            v.tensor_tensor(eq[:, 0:COLS - 1], dstf[:, 0:COLS - 1], dstf[:, 1:COLS], ALU.is_gt
                            ).then_inc(order_step, 1)
            v.tensor_tensor(eq[:, COLS - 1:COLS], last, nextf[:, :], ALU.is_gt).then_inc(order_step, 1)
            eng.wait_ge(order_step, 2)
            v.tensor_reduce(out_of_order[:, :], eq[:, :], AX.X, ALU.add).then_inc(order_step, 1)
            eng.wait_ge(order_shown, 1)
            v.tensor_copy(unsorted_i[:, :], bank[:, 7, 0:1]).then_inc(order_known, 1)
            eng.wait_ge(order_known, 1)
            unsorted = eng.value_load(unsorted_i[0:1, 0:1], min_val=0, max_val=E)
            with eng.If(unsorted > 0):
                own_key, own_number, rank, below_chunk = tmp, root, deg, norm

                def sort(ins, count):
                    ins.then_inc(sort_step, 1)
                    eng.wait_ge(sort_step, count)

                sort(v.tensor_scalar(own_key[:, :], dstf[:, :], float(SORT_SPAN), None, ALU.mult), 1)
                sort(v.tensor_scalar(own_number[:, :], count1[:, :], basef[:, :], None, ALU.add), 2)
                sort(v.memset(rank[:, :], 0.0), 3)
                fields = (srcf, dstf, typf, ew)
                for f, a in enumerate(fields):
                    sort(v.tensor_copy(packed[:, :, f], a[:, :]), 4 + f)
                eng.wait_ge(numbered, 1)
                sort(v.tensor_scalar(minus_number, number_i, -1.0, None, ALU.mult), 8)
                SETUP, CHUNK_STEPS = 8, 3 * COLS + 2
                with eng.Fori(0, SORT_CHUNKS) as c:
                    done = SETUP + CHUNK_STEPS * c
                    eng.wait_ge(keys_in, 16 * c + 16)
                    v.tensor_scalar(keys, keys_raw, float(SORT_SPAN), None, ALU.mult).then_inc(keys_taken, 1)
                    eng.wait_ge(keys_taken, c + 1)
                    eng.sem_inc(sort_passed, 1)
                    with eng.Fori(0, COLS) as j:
                        col = bass.ds(j, 1)
                        sort(v.tensor_scalar(key_gap, keys, own_key[:, col], None, ALU.subtract),
                             done + 3 * j + 1)
                        sort(v.scalar_tensor_tensor(out=is_before, in0=minus_number, scalar=own_number[:, col],
                                                    in1=key_gap, op0=ALU.add, op1=ALU.is_gt), done + 3 * j + 2)
                        sort(v.tensor_reduce(below_chunk[:, col], is_before, AX.X, ALU.add), done + 3 * j + 3)
                    sort(v.tensor_tensor(rank[:, :], rank[:, :], below_chunk[:, :], ALU.add),
                         done + 3 * COLS + 1)
                    sort(v.tensor_scalar(own_number[:, :], own_number[:, :], -float(SORT_KEYS), None, ALU.add),
                         done + 3 * COLS + 2)
                v.tensor_copy(slot_i[:, :], rank[:, :]).then_inc(ranked, 1)
                eng.wait_ge(sorted_in, 16 * 2)
                done = SETUP + CHUNK_STEPS * SORT_CHUNKS
                for f, a in enumerate(fields):
                    sort(v.tensor_copy(a[0:EP, :], packed[0:EP, :, f]), done + f + 1)
                sort(v.tensor_copy(src_i[0:EP, :], packed[0:EP, :, 0]), done + 5)
            link(v.tensor_scalar(diag[:, 0, :], ident[:, :], first, None, ALU.mult))
            link(v.tensor_scalar(diag[:, 1, :], ident[:, :], last, None, ALU.mult))
            assert steps[0] == PREP_DIAG
            link(v.tensor_scalar(tmp[:, :], dstf[:, :], float(N - 1), None, ALU.min))
            link(v.tensor_copy(dstx_i[:, :], tmp[:, :]))
            v.tensor_scalar(src1[:, :], srcf[:, :], 1.0, None, ALU.add).then_inc(ready0, 1)
            eng.wait_ge(shown, 3)
            for c in range(2):
                link(v.tensor_copy(srcT[:, c, :], bank[0:COLS // 2, 4 + c, 0:128]))
            v.tensor_scalar(tmp[:, :], dstf[:, :], first, None, ALU.is_equal).then_inc(ready0, 1)
            eng.wait_ge(ready0, 2)
            link(v.tensor_reduce(patchf[:, :], tmp[:, :], AX.X, ALU.add))
            link(v.scalar_tensor_tensor(out=patchf[:, :], in0=patchf[:, :], scalar=-1.0, in1=basef[:, :],
                                        op0=ALU.add, op1=ALU.add))
            link(v.tensor_copy(patch_i[:, :], patchf[:, :]))
            link(v.scalar_tensor_tensor(out=carry_in[:, :], in0=bank[:, 0, 0:128], scalar=last,
                                        in1=before[:, :], op0=ALU.is_equal, op1=ALU.mult))
            link(v.scalar_tensor_tensor(out=carry_back[:, :], in0=bank[:, 0, 128:256], scalar=first,
                                        in1=after[:, :], op0=ALU.is_equal, op1=ALU.mult))
            link(v.memset(same[:, 0:1], 0.0))
            link(v.tensor_tensor(same[:, 1:COLS], dstf[:, 1:COLS], dstf[:, 0:COLS - 1], ALU.is_equal))
            link(v.tensor_tensor(final[:, 0:COLS - 1], dstf[:, 0:COLS - 1], dstf[:, 1:COLS], ALU.not_equal))
            link(v.tensor_tensor(final[:, COLS - 1:COLS], last, nextf[:, :], ALU.not_equal))
            link(v.tensor_copy(deg[:, :], ew[:, :]))
            k = 1
            while k < COLS:
                link(v.tensor_tensor(eq[:, k:COLS], dstf[:, k:COLS], dstf[:, 0:COLS - k], ALU.is_equal))
                link(v.tensor_tensor(tmp[:, k:COLS], eq[:, k:COLS], deg[:, 0:COLS - k], ALU.mult))
                link(v.tensor_tensor(deg[:, k:COLS], deg[:, k:COLS], tmp[:, k:COLS], ALU.add))
                k *= 2
            assert steps[0] == PREP_TAIL, steps
            link(v.tensor_scalar(eq[:, :], dstf[:, :], first, None, ALU.is_equal))
            eng.wait_ge(shown, 4)
            link(v.tensor_copy(patchf[:, :], bank[:, 1, 0:1]))
            link(v.scalar_tensor_tensor(out=deg[:, :], in0=eq[:, :], scalar=patchf[:, :], in1=deg[:, :],
                                        op0=ALU.mult, op1=ALU.add))
            link(v.tensor_scalar(tmp[:, :], deg[:, :], 1e-12, None, ALU.max))
            assert steps[0] == PREP_DEG, steps
            link(v.tensor_scalar(eq[:, :], deg[:, :], 0.0, None, ALU.is_gt))
            eng.wait_ge(rooted, 1)
            link(v.reciprocal(dinv[:, :], root[:, :]))
            link(v.tensor_tensor(dinv[:, :], dinv[:, :], eq[:, :], ALU.mult))
            link(v.tensor_tensor(dinv[:, :], dinv[:, :], final[:, :], ALU.mult))
            link(v.scalar_tensor_tensor(out=look[:, 0:COLS], in0=dstf[:, :], scalar=1.0, in1=final[:, :],
                                        op0=ALU.add, op1=ALU.mult))
            link(v.tensor_copy(look[:, COLS:2 * COLS], dinv[:, :]))
            link(v.tensor_copy(look[:, 2 * COLS:2 * COLS + 1], basef[:, :]))
            link(v.tensor_copy(look_part[:, 0, :], look[:, :]))
            link(v.tensor_tensor(look[:, :], look[:, :], look_part[:, 0, :], ALU.subtract))
            link(v.tensor_copy(look_part[:, 1, :], look[:, :]))
            link(v.tensor_tensor(look[:, COLS:2 * COLS], look[:, COLS:2 * COLS], look_part[:, 1, COLS:2 * COLS],
                                 ALU.subtract))
            v.tensor_copy(look_last[:, :], look[:, COLS:2 * COLS]).then_inc(ready0, 1)
            k = 1
            while k < COLS:
                link(v.tensor_tensor(eq[:, 0:COLS - k], dstf[:, k:COLS], dstf[:, 0:COLS - k], ALU.is_equal))
                link(v.tensor_tensor(tmp[:, 0:COLS - k], eq[:, 0:COLS - k], dinv[:, k:COLS], ALU.mult))
                link(v.tensor_tensor(dinv[:, 0:COLS - k], dinv[:, 0:COLS - k], tmp[:, 0:COLS - k], ALU.add))
                k *= 2
            assert steps[0] == PREP_BACK, steps
            link(v.tensor_scalar(eq[:, :], dstf[:, :], last, None, ALU.is_equal))
            eng.wait_ge(shown, 5)
            link(v.tensor_copy(patchf[:, :], bank[:, 2, 0:1]))
            link(v.scalar_tensor_tensor(out=dinv[:, :], in0=eq[:, :], scalar=patchf[:, :], in1=dinv[:, :],
                                        op0=ALU.mult, op1=ALU.add))
            link(v.tensor_tensor(norm[:, :], dinv[:, :], ew[:, :], ALU.mult))
            link(v.scalar_tensor_tensor(out=tmp[:, :], in0=dstf[:, :], scalar=float(-NOWHERE), in1=final[:, :],
                                        op0=ALU.add, op1=ALU.mult))
            link(v.tensor_scalar(dsto_i[:, :], tmp[:, :], float(NOWHERE), None, ALU.add))
            link(v.tensor_tensor(mask[:, :, :], wide(typf[:, :], R),
                                 relf[:, None, :].to_broadcast([128, COLS, R]), ALU.is_equal))
            link(v.tensor_reduce(pair_mask[:, :, :], mask[:, :, :].rearrange("p j (b r) -> p j b r", r=2),
                                 AX.X, ALU.add))
            link(v.tensor_reduce(half_mask[:, :, :], mask[:, :, :].rearrange("p j (b r) -> p j r b", r=2),
                                 AX.X, ALU.add))
            link(v.memset(state[:, :, :], 0.0))
            link(v.memset(var[:, :], 1.0))

            eng.wait_ge(weights_in, 16 * 22)
            eng.wait_ge(rooted, 2)
            link(v.reciprocal(bns[:, :], bn_t[:, :]))
            link(v.tensor_tensor(bns[:, :], bns[:, :], bnv[:, 0, :], ALU.mult))
            link(v.scalar_tensor_tensor(out=w_next[:, :], in0=w_next[:, :], scalar=0.5, in1=bns[:, :],
                                        op0=ALU.mult, op1=ALU.mult))
            link(v.tensor_tensor(w_rootk[:, 0, :], w_rootk[:, 0, :], w_rootk[:, 1, :], ALU.add))
            for c in range(2):
                h = slice(c * F, (c + 1) * F)
                link(v.scalar_tensor_tensor(out=w_root[h, h], in0=w_rootk[h, 0, :], scalar=0.5, in1=bns[h, :],
                                            op0=ALU.mult, op1=ALU.mult))
            link(v.tensor_tensor(bn_t[:, :], bvec[:, 0, :], bvec[:, 1, :], ALU.add))
            link(v.scalar_tensor_tensor(out=bn_t[:, :], in0=bn_t[:, :], scalar=0.5, in1=bnv[:, 2, :],
                                        op0=ALU.mult, op1=ALU.subtract))
            link(v.tensor_tensor(bn_t[:, :], bn_t[:, :], bns[:, :], ALU.mult))
            link(v.tensor_tensor(bias_rest[:, 0, :], bn_t[:, :], bnv[:, 1, :], ALU.add))
            for c in range(3):
                link(v.tensor_copy(bias_part[:, c, :], bias_rest[:, c, :]))
                if c < 2:
                    link(v.tensor_tensor(bias_rest[:, c + 1, :], bias_rest[:, c, :], bias_part[:, c, :],
                                         ALU.subtract))
            link(v.tensor_scalar(bn_t[:, :], bias_part[:, 0, :], ident[:, 0:1], None, ALU.mult))
            for c in range(1, 3):
                link(v.scalar_tensor_tensor(out=bn_t[:, :], in0=bias_part[:, c, :], scalar=ident[:, c:c + 1],
                                            in1=bn_t[:, :], op0=ALU.mult, op1=ALU.add))
            link(v.tensor_copy(bias_row[:, :, :], bn_t[0:3, None, :].to_broadcast([3, DT, F])))
            link(v.tensor_copy(ones3[:, :], ones[0:3, :]))
            eng.wait_ge(shown, 6)
            v.tensor_copy(w_loopT[:, :], bank[:, 3, 0:128]).then_inc(weights_ok, 1)

            def body0(it, par, k, on):
                def choose(q):
                    v.tensor_scalar(past_first[:, q, :], sbc[:, 2 * par + q, :], first, None, ALU.is_ge
                                    ).then_inc(below, 1)
                    eng.wait_ge(below, 2 * it + q + 1)
                    wait_past(eng, looked, 2 * GROUP * it + GROUP * q - GROUP)
                    v.scalar_tensor_tensor(out=pick_bf[:, q, :], in0=sbc[:, 2 * par + q, :],
                                           scalar=nextf[:, :], in1=past_first[:, q, :],
                                           op0=ALU.is_lt, op1=ALU.mult).then_inc(picked, 1)

                def match(q):
                    tile = 2 * GROUP * (it - 1) + GROUP * q
                    wait_past(eng, matched, tile - GROUP)
                    for t in range(GROUP):
                        j = bass.ds(tile + t, 1)
                        eng.wait_ge(looked, tile + t + 1)
                        v.scalar_tensor_tensor(out=found[:, q, t, :], in0=bank[:, 4 * q + t, 0:COLS],
                                               scalar=src1[:, j], in1=count1[:, :], op0=ALU.is_equal,
                                               op1=ALU.mult, accum_out=place[:, j]).then_inc(placed, 1)
                        if t > 0:
                            take_dinv(q, tile, t - 1)
                    take_dinv(q, tile, GROUP - 1)

                def take_dinv(q, tile, t):
                    eng.wait_ge(placed, tile + t + 1)
                    v.scalar_tensor_tensor(out=dropped[:, q, t, :], in0=found[:, q, t, :], scalar=0.0,
                                           in1=bank[:, 4 * q + t, COLS:2 * COLS], op0=ALU.is_gt,
                                           op1=ALU.mult, accum_out=dinv_src[:, bass.ds(tile + t, 1)]
                                           ).then_inc(matched, 1)

                if on[0]:
                    eng.wait_ge(bc_in[par], 16 * (k + 1))
                for q in range(2):
                    if on[0]:
                        choose(q)
                    if on[1]:
                        match(q)

            overlapped(eng, body0, 2)
            eng.wait_ge(matched, COLS)
            eng.wait_ge(based, COLS)
            link(v.tensor_tensor(norm[:, :], norm[:, :], dinv_src[:, :], ALU.mult))
            link(v.tensor_scalar(eq[:, :], place[:, :], 0.0, None, ALU.is_gt))
            link(v.tensor_tensor(tmp[:, :], block_base[:, :], place[:, :], ALU.add))
            link(v.scalar_tensor_tensor(out=tmp[:, :], in0=tmp[:, :], scalar=float(-1 - ROWS), in1=eq[:, :],
                                        op0=ALU.add, op1=ALU.mult))
            v.tensor_scalar(slot_i[:, :], tmp[:, :], float(ROWS), None, ALU.add).then_inc(weights_ok, 1)

            def scan_steps(stage, it, par, k):
                count = [0]

                def step():
                    i = count[0]
                    if i == 2 * GROUP:
                        return
                    count[0] += 1
                    at = 2 * GROUP * par + i
                    j = 2 * GROUP * it + i
                    if i == 0:
                        wait_past(eng, t_spilled[par], 16 * (stage * turns(par) + k))
                    eng.wait_ge(scanned, stage * COLS + j + 1)
                    v.scalar_tensor_tensor(out=state[:, at, :], in0=state[:, (at - 1) % (4 * GROUP), :],
                                           scalar=same[:, bass.ds(j, 1)], in1=msg[:, i // GROUP, i % GROUP, :],
                                           op0=ALU.mult, op1=ALU.add).then_inc(scanned, 1)
                return step

            def finish(step):
                for _ in range(2 * GROUP):
                    step()

            def nothing():
                pass

            def dense_x(par, q):
                return tiles_of(dx[0:DP, 2 * par + q, :])

            def dense_stage(base, it, par, k, on, extra, count, lo, out_of, between):
                n = base * 2 * ITERS + 2 * it
                items1, items2 = [], []
                if on[0]:
                    eng.wait_ge(dense_in[par], 16 * (base * turns(par) + k + 1))
                    items1 = extra + [(dense.norm1, q, n + q, dense_x(par, q)) for q in range(2)]
                    ln_centre(eng, items1, between)
                if on[1]:
                    for q in range(2):
                        add_relu(eng, dense.norm1, q, n - 2 + q, dense_x(1 - par, q),
                                 dense.x1[0:DP, 2 * (1 - par) + q])
                        between()
                    eng.wait_ge(dense.norm1.done, n)
                    items2 = [(dense.norm2, q, n - 2 + q, dense.x1[0:DP, 2 * (1 - par) + q]) for q in range(2)]
                    ln_centre(eng, items2, between)

                def end_items():
                    if on[2]:
                        wait_past(eng, dense_out[par], 16 * (base * turns(par) + k - 1))
                        for q in range(2):
                            add_relu(eng, dense.norm2, q, n - 4 + q, dense.x1[0:DP, 2 * par + q],
                                     tiles_of(dout[0:DP, 2 * par + q, :]))
                            between()

                if base == 0:
                    end_items()
                ln_spread(eng, items1 + items2, between, (SUMMED1, SUMMED2)[base])
                if on[0] or on[1]:
                    ln_scale(eng, count, lo, STATS)
                    between()
                    ln_hidden(eng, [i for i in items1 if i[0].rows == DP], count, out_of, between)
                    ln_hidden(eng, items2 + [i for i in items1 if i[0].rows != DP], count, out_of, between)
                if base == 1:
                    end_items()

            def body1(it, par, k, on):
                step = scan_steps(0, *earlier(it, par, k, 1)) if on[1] else nothing
                extra = []
                if on[0]:
                    wait_past(eng, h_spilled[par], 16 * k)
                    for q in range(2):
                        eng.wait_ge(gathered[2 * par + q], 16 * GROUP * (turns(par) + k + 1))
                    extra = [(edge.norm1, q, 2 * it + q, xr[:, slot(par, q), :]) for q in range(2)]
                if on[1]:
                    eng.wait_ge(weighed, 2 * it)
                dense_stage(0, it, par, k, on, extra, it, 0,
                            lambda norm, q: hr[:, slot(par, q), :] if norm is edge.norm1 else own_h(norm, q),
                            step)
                if on[1]:
                    finish(step)
                if on[0]:
                    wait_past(eng, scanned, 2 * GROUP * it + 1)
                    for q in range(2):
                        eng.wait_ge(edge.norm1.hidden, 2 * it + q + 1)
                        v.tensor_tensor(msg[:, q], hr[:, slot(par, q), :], wide(norm[:, cols(it, q)], F),
                                        ALU.mult).then_inc(weighed, 1)

            v.memset(state[:, 4 * GROUP - 1, :], 0.0).then_inc(scanned, 1)
            overlapped(eng, body1, 3)
            BODIES = ITERS + 1

            def patch(stage):
                eng.wait_ge(carried, stage + 1)
                eng.wait_ge(patch_in, 16 * (stage + 1))
                v.tensor_tensor(patched[:, :], bank[:, 0, 0:F], patch_row[:, :], ALU.add
                                ).then_inc(patch_made, 1)

            patch(0)

            def body2(it, par, k, on):
                step = nothing
                if on[1]:
                    step = scan_steps(1, *earlier(it, par, k, 1))
                    eng.wait_ge(scanned, COLS + 2 * GROUP * it - 2 * GROUP + 1)
                    for q in range(2):
                        eng.wait_ge(arma_out, 2 * it)
                        z = tiles_of(bank[:, 2, GROUP * F * q:GROUP * F * (q + 1)])
                        v.tensor_tensor(msg[:, q], z, wide(norm[:, cols(it - 1, q)], F), ALU.mult
                                        ).then_inc(weighed, 1)
                    eng.wait_ge(weighed, GROUPS + 2 * it)
                dense_stage(1, it, par, k, on, [], BODIES + it, EDGE_STATS, own_h, step)
                if on[1]:
                    finish(step)

            overlapped(eng, body2, 3)
            patch(1)

            def body3(it, par, k, on):
                def typed(q):
                    if q == 0:
                        wait_past(eng, spread_turned, 4 * it - 4)
                    v.tensor_tensor(spread[:, q],
                                    edge.norm1.h[:, q, :, None, :].to_broadcast([128, GROUP, R // 2, F]),
                                    pair_mask[:, cols(it - 1, q), :].unsqueeze(3)
                                    .to_broadcast([128, GROUP, R // 2, F]), ALU.mult).then_inc(spread_done, 1)

                def keep(q):
                    n = 2 * it - 4 + q
                    if q == 1:
                        eng.wait_ge(weighed, 2 * GROUPS + n)
                    eng.wait_ge(rel_out, n + 1)
                    v.tensor_tensor(halves[:, :, :, :],
                                    bank[:, S3_OUT[par][q], :].rearrange("p (t r f) -> p t r f", t=GROUP, r=2),
                                    half_mask[:, cols(it - 2, q), :].unsqueeze(3)
                                    .to_broadcast([128, GROUP, 2, F]), ALU.mult).then_inc(halved, 1)

                def messages(q):
                    eng.wait_ge(halved, 2 * it - 4 + q + 1)
                    v.tensor_tensor(msg[:, q], halves[:, :, 0, :], halves[:, :, 1, :], ALU.add
                                    ).then_inc(weighed, 1)

                items = []
                if on[1]:
                    eng.wait_ge(edge.norm1.hidden, GROUPS + 2 * it)
                    typed(0)
                if on[0]:
                    eng.wait_ge(xu_in[par], 32 * (k + 1))
                    for q in range(2):
                        eng.wait_ge(gathered[2 * par + q], 16 * GROUP * (3 * turns(par) + k + 1))
                        v.tensor_tensor(edge.norm2.sq[:, q], ar[:, slot(par, q), :], ur[:, slot(par, q), :],
                                        ALU.add).then_inc(summed, 1)
                    for q in range(2):
                        eng.wait_ge(summed, 2 * it + q + 1)
                        v.scalar_tensor_tensor(out=edge.x1[:, q], in0=edge.norm2.sq[:, q], scalar=0.0,
                                               in1=xr[:, slot(par, q), :], op0=ALU.max, op1=ALU.add
                                               ).then_inc(x1_made, 1)
                if on[1]:
                    typed(1)
                step = nothing
                behind = []
                if on[2]:
                    eng.wait_ge(scanned, 2 * COLS + 2 * GROUP * it - 4 * GROUP + 1)
                    keep(0)
                    step = scan_steps(2, *earlier(it, par, k, 2))

                    def scan_first():
                        messages(1)
                        eng.wait_ge(weighed, 2 * GROUPS + 2 * it - 3)
                        step()

                    def scan_second():
                        eng.wait_ge(weighed, 2 * GROUPS + 2 * it - 2)
                        step()

                    behind = [lambda: messages(0), lambda: keep(1), scan_first, scan_second]

                def between():
                    if behind:
                        behind.pop(0)()
                    else:
                        step()

                if on[0]:
                    eng.wait_ge(x1_made, 2 * it + 2)
                    items = [(edge.norm1, q, GROUPS + 2 * it + q, edge.x1[:, q]) for q in range(2)]
                    ln_centre(eng, items, between)
                    ln_spread(eng, items, between)
                    if on[1]:
                        eng.wait_ge(spread_done, 2 * it)
                    ln_scale(eng, 2 * BODIES + it, 0, 2 * GROUP)
                    between()
                    ln_hidden(eng, items, 2 * BODIES + it, own_h, between)
                if on[2]:
                    while behind:
                        between()
                    finish(step)

            overlapped(eng, body3, 3)
            patch(2)

            def body4(it, par, k, on):
                n = 2 * it
                items1, items2 = [], []
                if on[0]:
                    eng.wait_ge(xu_in[par], 32 * turns(par) + 32 * (k + 1))
                    items1 = [(edge.norm1, q, 2 * GROUPS + n + q, xr[:, slot(par, q), :]) for q in range(2)]
                    ln_centre(eng, items1, nothing)
                if on[1]:
                    for q in range(2):
                        add_sums(eng, edge.norm1, q, n - 2 + q, ur[:, slot(1 - par, q), :])
                    for q in range(2):
                        relu_of_sums(eng, edge.norm1, q, n - 2 + q, xr[:, slot(1 - par, q), :],
                                     edge.x1[:, 2 * (1 - par) + q])
                    eng.wait_ge(edge.norm1.done, n)
                    items2 = [(edge.norm2, q, n - 2 + q, edge.x1[:, 2 * (1 - par) + q]) for q in range(2)]
                    ln_centre(eng, items2, nothing)
                ln_spread(eng, items1, nothing)
                if on[2]:
                    eng.wait_ge(t2_in[par], 16 * k)
                    for q in range(2):
                        add_sums(eng, edge.norm2, q, n - 4 + q, tr[:, slot(par, q), :])
                ln_spread(eng, items2, nothing)
                if on[2]:
                    for q in range(2):
                        s = 2 * par + q
                        wait_past(eng, scattered[s], 16 * GROUP * (k - 1))
                        relu_of_sums(eng, edge.norm2, q, n - 4 + q, edge.x1[:, 2 * par + q],
                                     eout[:, slot(par, q), :])
                if on[0] or on[1]:
                    count = 2 * BODIES + ITERS + it
                    ln_scale(eng, count, 0, EDGE_STATS)
                    ln_hidden(eng, items1 + items2, count, own_h, nothing)

            overlapped(eng, body4, 3)


PREP_DIAG = 15
PREP_TAIL = 15 + 2 + 2 + 5 + 5 + 24
PREP_DEG = PREP_TAIL + 4
PREP_BACK = PREP_DEG + 11 + 24


_INS = ['x', 'src', 'dst', 'edge_type_8', 'edge_weight', 'L0_gnn_init_weight', 'L0_gnn_weight',
        'L0_gnn_root_weight', 'L0_gnn_bias', 'L0_gnn_bn_gamma', 'L0_gnn_bn_beta', 'L0_gnn_bn_mean',
        'L0_gnn_bn_var', 'L1_gnn_weight', 'L1_gnn_self_loop_w']


def kernel(**inputs):
    import numpy as _np
    import concourse.bacc as _bacc
    from concourse import mybir as _mybir
    from concourse.bass_utils import run_bass_kernel_spmd as _run

    nc = _bacc.Bacc("TRN2", target_bir_lowering=False, num_devices=1)
    arrays, args = {}, []
    for name in _INS:
        a = _np.ascontiguousarray(inputs[name])
        arrays[f"in_{name}"] = a
        args.append(nc.dram_tensor(f"in_{name}", a.shape, _mybir.dt.from_np(a.dtype), kind="ExternalInput").ap())
    shape = tuple(inputs['x'].shape)
    out = nc.dram_tensor("out_x", shape, _mybir.dt.float32, kind="ExternalOutput").ap()
    gnn_kernel(nc, *args, out)
    r = _run(nc, [arrays], core_ids=[0])
    return r.results[0]["out_x"]
```
